# Optimizing a Trainium2 kernel written in Bass

```python
import numpy as np
import jax
import jax.numpy as jnp

def _softmax(x, axis=-1):
    return jax.nn.softmax(x, axis=axis)

def _gelu(x):
    return jax.nn.gelu(x, approximate=True)

def _silu(x):
    return jax.nn.silu(x)

def _sigmoid(x):
    return jax.nn.sigmoid(x)

def _layernorm(x, axis=-1, eps=1e-05):
    m = jnp.mean(x, axis=axis, keepdims=True)
    v = jnp.var(x, axis=axis, keepdims=True)
    return (x - m) / jnp.sqrt(v + eps)

def _scatter_add(tgt, idx, src, axis=0):
    return tgt.at[idx].add(src)

def _segment_sum(src, seg, n):
    return jax.ops.segment_sum(src, seg, n)
kernel_name = 'mk_perceiver_d2_seqx_r8_452152'

def setup_inputs(seed: int=0):
    np.random.seed(seed)
    _w = jnp.asarray

    def _rec_inputs():
        import jax
        import jax.numpy as jnp
        _rk = jax.random.key(seed)
        x = 7.22e-05 + 1 * jax.random.normal(jax.random.fold_in(_rk, 1), (32, 32, 128), jnp.float32)
        _lenS = 32 - jax.random.randint(jax.random.fold_in(_rk, 7), (32,), 0, max(1, 32 // 4) + 1, jnp.int32)
        _lenS2 = 257 - jax.random.randint(jax.random.fold_in(_rk, 8), (32,), 0, max(1, 257 // 4) + 1, jnp.int32)
        _ctx_1024P = jax.random.normal(jax.random.fold_in(_rk, 11), (32, 16, 128), jnp.float32)
        _ctx_1024c = jax.random.dirichlet(jax.random.fold_in(_rk, 511), 0.3 * jnp.ones((16,), jnp.float32), (32, 257))
        _ctx_1024t = jnp.einsum('bsk,bkd->bsd', _ctx_1024c, _ctx_1024P)
        _ctx_1024t = _ctx_1024t * jax.lax.rsqrt(jnp.mean(jnp.square(_ctx_1024t)) + 1e-12) * 0.953939
        ctx_1024 = 4.13588e-05 + 0.999923 * (_ctx_1024t + 0.3 * jax.random.normal(jax.random.fold_in(_rk, 611), (32, 257, 128), jnp.float32))
        _validS = jnp.arange(32)[None, :] < _lenS[:, None]
        _validS2 = jnp.arange(257)[None, :] < _lenS2[:, None]
        _causal = jnp.tril(jnp.ones((32, 32), dtype=bool))
        mask_BxSxS2_ik0 = jnp.where(jnp.broadcast_to(_validS2[:, None, :], (32, 32, 257)), 0, 1).astype(jnp.int32)
        mask_Bx1x1xS2_ik0 = jnp.where(jnp.broadcast_to(_validS2[:, None, None, :], (32, 1, 1, 257)), 0, 1).astype(jnp.int32)
        return (x, ctx_1024, mask_BxSxS2_ik0, mask_Bx1x1xS2_ik0)
    x, ctx_1024, mask_BxSxS2_ik0, mask_Bx1x1xS2_ik0 = _rec_inputs()

    def _L0_xattn_setup():
        import jax, jax.numpy as jnp
        import numpy as np
        import math
        B, S, E = (4, 256, 128)
        key = jax.random.key(seed)
        ks = jax.random.split(key, 12)
        scale = 1.0 / math.sqrt(E)
        inp = {'query': jax.random.normal(ks[0], (B, S, E), jnp.float32), 'key_': jax.random.normal(ks[1], (B, S, E), jnp.float32), 'value': jax.random.normal(ks[2], (B, S, E), jnp.float32), 'mask': jnp.broadcast_to(jnp.tril(jnp.ones((S, S), jnp.int32)), (B, S, S)), 'Wq': jax.random.uniform(ks[3], (E, E), jnp.float32, -scale, scale), 'bq': jax.random.uniform(ks[4], (E,), jnp.float32, -scale, scale), 'Wk': jax.random.uniform(ks[5], (E, E), jnp.float32, -scale, scale), 'bk': jax.random.uniform(ks[6], (E,), jnp.float32, -scale, scale), 'Wv': jax.random.uniform(ks[7], (E, E), jnp.float32, -scale, scale), 'bv': jax.random.uniform(ks[8], (E,), jnp.float32, -scale, scale), 'Wo': jax.random.uniform(ks[9], (E, E), jnp.float32, -scale, scale), 'bo': jax.random.uniform(ks[10], (E,), jnp.float32, -scale, scale)}
        return inp
    _L0_xattn_all = _L0_xattn_setup()
    _L0_xattn_in = {k: v for k, v in _L0_xattn_all.items() if k in ('Wq', 'bq', 'Wk', 'bk', 'Wv', 'bv', 'Wo', 'bo')}
    del _L0_xattn_all

    def _L0_attn_setup():
        import jax, jax.numpy as jnp
        import numpy as np
        DIM = 128
        NUM_HEADS = 16
        HEAD_DIM = DIM // NUM_HEADS
        SCALE = HEAD_DIM ** (-0.5)
        key = jax.random.key(seed)
        ks = jax.random.split(key, 5)
        x = jax.random.normal(ks[0], (4, 256, DIM), dtype=jnp.float32)
        w_qkv = jax.random.normal(ks[1], (DIM, 3 * DIM), dtype=jnp.float32) * DIM ** (-0.5)
        b_qkv = jax.random.normal(ks[2], (3 * DIM,), dtype=jnp.float32) * 0.02
        w_proj = jax.random.normal(ks[3], (DIM, DIM), dtype=jnp.float32) * DIM ** (-0.5)
        b_proj = jax.random.normal(ks[4], (DIM,), dtype=jnp.float32) * 0.02
        return {'x': x, 'w_qkv': w_qkv, 'b_qkv': b_qkv, 'w_proj': w_proj, 'b_proj': b_proj}
    _L0_attn_all = _L0_attn_setup()
    _L0_attn_in = {k: v for k, v in _L0_attn_all.items() if k in ('w_qkv', 'b_qkv', 'w_proj', 'b_proj')}
    del _L0_attn_all

    def _L0_ffn_setup():
        import jax, jax.numpy as jnp
        import numpy as np
        from jax.scipy.linalg import expm
        B, S, D, E, K, NROT = (2, 256, 128, 8, 2, 3)
        DF = 4 * D
        EPS = 1e-05
        key = jax.random.key(seed)
        ks = jax.random.split(key, 8)
        s = lambda d: 1.0 / np.sqrt(d)
        return {'x': jax.random.normal(ks[0], (B, S, D), jnp.float32), 'ln_g': jnp.ones((D,), jnp.float32), 'ln_b': jnp.zeros((D,), jnp.float32), 'abel_w': jax.random.normal(ks[1], (D, D), jnp.float32) * s(D), 'abel_b': jnp.zeros((D,), jnp.float32), 'gate_w_moe': jax.random.normal(ks[2], (D, E), jnp.float32) * s(D), 'gate_b_moe': jnp.zeros((E,), jnp.float32), 'w1': jax.random.normal(ks[3], (E, D, DF), jnp.float32) * s(D), 'b1': jnp.zeros((E, DF), jnp.float32), 'w2': jax.random.normal(ks[4], (E, DF, D), jnp.float32) * s(DF), 'b2': jnp.zeros((E, D), jnp.float32), 'gens': jax.random.normal(ks[5], (NROT, D, D), jnp.float32) * 0.02, 'mix_w': jax.random.normal(ks[6], (2 * D, 1), jnp.float32) * s(2 * D), 'mix_b': jnp.zeros((1,), jnp.float32)}
    _L0_ffn_all = _L0_ffn_setup()
    _L0_ffn_in = {k: v for k, v in _L0_ffn_all.items() if k in ('ln_g', 'ln_b', 'abel_w', 'abel_b', 'gate_w_moe', 'gate_b_moe', 'w1', 'b1', 'w2', 'b2', 'gens', 'mix_w', 'mix_b')}
    del _L0_ffn_all

    def _L1_xattn_setup():
        import jax, jax.numpy as jnp
        import numpy as np
        B, S, D, H = (2, 256, 128, 16)
        HD = D // H
        key = jax.random.key(seed)
        ks = jax.random.split(key, 12)
        inp = {'query': jax.random.normal(ks[0], (B, S, D), jnp.float32), 'key': jax.random.normal(ks[1], (B, S, D), jnp.float32), 'value': jax.random.normal(ks[2], (B, S, D), jnp.float32), 'mask': jax.random.randint(ks[3], (B, 1, 1, S), 0, 2, jnp.int32), 'Wq': jax.random.normal(ks[4], (D, D), jnp.float32) / np.sqrt(D), 'bq': jnp.zeros((D,), jnp.float32), 'Wk': jax.random.normal(ks[5], (D, D), jnp.float32) / np.sqrt(D), 'bk': jnp.zeros((D,), jnp.float32), 'Wv': jax.random.normal(ks[6], (D, D), jnp.float32) / np.sqrt(D), 'bv': jnp.zeros((D,), jnp.float32), 'Wo': jax.random.normal(ks[7], (D, D), jnp.float32) / np.sqrt(D), 'bo': jnp.zeros((D,), jnp.float32)}
        return inp
    _L1_xattn_all = _L1_xattn_setup()
    _L1_xattn_in = {k: v for k, v in _L1_xattn_all.items() if k in ('Wq', 'bq', 'Wk', 'bk', 'Wv', 'bv', 'Wo', 'bo')}
    del _L1_xattn_all

    def _L1_attn_setup():
        import jax, jax.numpy as jnp
        import numpy as np
        EMB = 128
        HEADS = 16
        EPS = 1e-05

        def layer_norm(x):
            mu = jnp.mean(x, axis=-1, keepdims=True)
            var = jnp.var(x, axis=-1, keepdims=True)
            return (x - mu) / jnp.sqrt(var + EPS)

        def pattention(x, K, V):
            scale = EMB ** (-0.5)
            a = jax.nn.softmax(scale * jnp.einsum('btc,nc->btn', x, K), axis=-1)
            return jnp.einsum('btn,nc->btc', a, V)

        def causal_sdpa(q, k, v):
            T = q.shape[2]
            d = q.shape[-1]
            scores = jnp.einsum('bhqd,bhkd->bhqk', q, k) / jnp.sqrt(jnp.asarray(d, q.dtype))
            mask = jnp.tril(jnp.ones((T, T), dtype=bool))
            scores = jnp.where(mask, scores, jnp.asarray(-jnp.inf, q.dtype))
            attn = jax.nn.softmax(scores, axis=-1)
            return jnp.einsum('bhqk,bhkd->bhqd', attn, v)
        key = jax.random.key(seed)
        ks = jax.random.split(key, 11)
        B, T, C = (2, 256, EMB)
        N = 256 // 2
        inp = {'x': jax.random.normal(ks[0], (B, T, C), dtype=jnp.float32)}
        names = ['qK', 'qV', 'kK', 'kV', 'vK', 'vV', 'pK', 'pV']
        for i, nm in enumerate(names):
            inp[nm] = jax.random.normal(ks[1 + i], (N, C), dtype=jnp.float32)
        inp['fK'] = jax.random.normal(ks[9], (4 * N, C), dtype=jnp.float32)
        inp['fV'] = jax.random.normal(ks[10], (4 * N, C), dtype=jnp.float32)
        return inp
    _L1_attn_all = _L1_attn_setup()
    _L1_attn_in = {k: v for k, v in _L1_attn_all.items() if k in ('qK', 'qV', 'kK', 'kV', 'vK', 'vV', 'pK', 'pV', 'fK', 'fV')}
    del _L1_attn_all

    def _L1_ffn_setup():
        import jax, jax.numpy as jnp
        import numpy as np
        B, T = (2, 256)
        D_MODEL, D_HIDDEN = (128, 256)
        N_EXPERTS, TOP_K = (8, 2)
        N_TOKENS = B * T
        CAPACITY = 2 * N_TOKENS * TOP_K // N_EXPERTS
        key = jax.random.key(seed)
        k_x, k_rw, k_w, k_v, k_o = jax.random.split(key, 5)
        x = jax.random.normal(k_x, (B, T, D_MODEL), jnp.float32)
        router_w = jax.random.normal(k_rw, (N_EXPERTS, D_MODEL), jnp.float32) * D_MODEL ** (-0.5)
        router_b = jnp.zeros((N_EXPERTS,), jnp.float32)
        W = jax.random.normal(k_w, (N_EXPERTS, D_MODEL, D_HIDDEN), jnp.float32) * D_MODEL ** (-0.5)
        V = jax.random.normal(k_v, (N_EXPERTS, D_MODEL, D_HIDDEN), jnp.float32) * D_MODEL ** (-0.5)
        W_out = jax.random.normal(k_o, (N_EXPERTS, D_HIDDEN, D_MODEL), jnp.float32) * D_HIDDEN ** (-0.5)
        return {'x': x, 'router_w': router_w, 'router_b': router_b, 'W': W, 'V': V, 'W_out': W_out}
    _L1_ffn_all = _L1_ffn_setup()
    _L1_ffn_in = {k: v for k, v in _L1_ffn_all.items() if k in ('router_w', 'router_b', 'W', 'V', 'W_out')}
    del _L1_ffn_all
    return {'x': x, 'ctx_1024': ctx_1024, 'mask_BxSxS2_ik0': mask_BxSxS2_ik0, 'mask_Bx1x1xS2_ik0': mask_Bx1x1xS2_ik0, 'L0_xattn_Wq': _L0_xattn_in['Wq'], 'L0_xattn_bq': _L0_xattn_in['bq'], 'L0_xattn_Wk': _L0_xattn_in['Wk'], 'L0_xattn_bk': _L0_xattn_in['bk'], 'L0_xattn_Wv': _L0_xattn_in['Wv'], 'L0_xattn_bv': _L0_xattn_in['bv'], 'L0_xattn_Wo': _L0_xattn_in['Wo'], 'L0_xattn_bo': _L0_xattn_in['bo'], 'L0_attn_w_qkv': _L0_attn_in['w_qkv'], 'L0_attn_b_qkv': _L0_attn_in['b_qkv'], 'L0_attn_w_proj': _L0_attn_in['w_proj'], 'L0_attn_b_proj': _L0_attn_in['b_proj'], 'L0_ffn_ln_g': _L0_ffn_in['ln_g'], 'L0_ffn_ln_b': _L0_ffn_in['ln_b'], 'L0_ffn_abel_w': _L0_ffn_in['abel_w'], 'L0_ffn_abel_b': _L0_ffn_in['abel_b'], 'L0_ffn_gate_w_moe': _L0_ffn_in['gate_w_moe'], 'L0_ffn_gate_b_moe': _L0_ffn_in['gate_b_moe'], 'L0_ffn_w1': _L0_ffn_in['w1'], 'L0_ffn_b1': _L0_ffn_in['b1'], 'L0_ffn_w2': _L0_ffn_in['w2'], 'L0_ffn_b2': _L0_ffn_in['b2'], 'L0_ffn_gens': _L0_ffn_in['gens'], 'L0_ffn_mix_w': _L0_ffn_in['mix_w'], 'L0_ffn_mix_b': _L0_ffn_in['mix_b'], 'L1_xattn_Wq': _L1_xattn_in['Wq'], 'L1_xattn_bq': _L1_xattn_in['bq'], 'L1_xattn_Wk': _L1_xattn_in['Wk'], 'L1_xattn_bk': _L1_xattn_in['bk'], 'L1_xattn_Wv': _L1_xattn_in['Wv'], 'L1_xattn_bv': _L1_xattn_in['bv'], 'L1_xattn_Wo': _L1_xattn_in['Wo'], 'L1_xattn_bo': _L1_xattn_in['bo'], 'L1_attn_qK': _L1_attn_in['qK'], 'L1_attn_qV': _L1_attn_in['qV'], 'L1_attn_kK': _L1_attn_in['kK'], 'L1_attn_kV': _L1_attn_in['kV'], 'L1_attn_vK': _L1_attn_in['vK'], 'L1_attn_vV': _L1_attn_in['vV'], 'L1_attn_pK': _L1_attn_in['pK'], 'L1_attn_pV': _L1_attn_in['pV'], 'L1_attn_fK': _L1_attn_in['fK'], 'L1_attn_fV': _L1_attn_in['fV'], 'L1_ffn_router_w': _L1_ffn_in['router_w'], 'L1_ffn_router_b': _L1_ffn_in['router_b'], 'L1_ffn_W': _L1_ffn_in['W'], 'L1_ffn_V': _L1_ffn_in['V'], 'L1_ffn_W_out': _L1_ffn_in['W_out']}

def reference(x, ctx_1024, mask_BxSxS2_ik0, mask_Bx1x1xS2_ik0, L0_xattn_Wq, L0_xattn_bq, L0_xattn_Wk, L0_xattn_bk, L0_xattn_Wv, L0_xattn_bv, L0_xattn_Wo, L0_xattn_bo, L0_attn_w_qkv, L0_attn_b_qkv, L0_attn_w_proj, L0_attn_b_proj, L0_ffn_ln_g, L0_ffn_ln_b, L0_ffn_abel_w, L0_ffn_abel_b, L0_ffn_gate_w_moe, L0_ffn_gate_b_moe, L0_ffn_w1, L0_ffn_b1, L0_ffn_w2, L0_ffn_b2, L0_ffn_gens, L0_ffn_mix_w, L0_ffn_mix_b, L1_xattn_Wq, L1_xattn_bq, L1_xattn_Wk, L1_xattn_bk, L1_xattn_Wv, L1_xattn_bv, L1_xattn_Wo, L1_xattn_bo, L1_attn_qK, L1_attn_qV, L1_attn_kK, L1_attn_kV, L1_attn_vK, L1_attn_vV, L1_attn_pK, L1_attn_pV, L1_attn_fK, L1_attn_fV, L1_ffn_router_w, L1_ffn_router_b, L1_ffn_W, L1_ffn_V, L1_ffn_W_out):
    import jax
    import jax.numpy as jnp

    def _L0_xattn_ref(query, key_, value, mask, Wq, bq, Wk, bk, Wv, bv, Wo, bo):
        import jax, jax.numpy as jnp
        import numpy as np
        import math
        B, S, E = (4, 256, 128)
        Q = jnp.einsum('bse,fe->bsf', query, Wq) + bq
        K = jnp.einsum('bse,fe->bsf', key_, Wk) + bk
        V = jnp.einsum('bse,fe->bsf', value, Wv) + bv
        scores = jnp.einsum('bqe,bke->bqk', Q, K) / jnp.sqrt(jnp.asarray(E, Q.dtype))
        scores = jnp.where(mask == 0, -jnp.inf, scores)
        attn = jax.nn.softmax(scores, axis=-1)
        attn_out = jnp.einsum('bqk,bke->bqe', attn, V)
        return jnp.einsum('bse,fe->bsf', attn_out, Wo) + bo

    def _L0_attn_ref(x, w_qkv, b_qkv, w_proj, b_proj):
        import jax, jax.numpy as jnp
        import numpy as np
        DIM = 128
        NUM_HEADS = 16
        HEAD_DIM = DIM // NUM_HEADS
        SCALE = HEAD_DIM ** (-0.5)
        b, n, c = x.shape
        qkv = x @ w_qkv + b_qkv
        qkv = qkv.reshape(b, n, 3, NUM_HEADS, HEAD_DIM)
        qkv = jnp.transpose(qkv, (2, 0, 3, 1, 4))
        q, k, v = (qkv[0], qkv[1], qkv[2])
        attn = jnp.einsum('bhnd,bhmd->bhnm', q, k) * SCALE
        attn = jax.nn.softmax(attn, axis=-1)
        out = jnp.einsum('bhnm,bhmd->bhnd', attn, v)
        out = jnp.transpose(out, (0, 2, 1, 3)).reshape(b, n, c)
        out = out @ w_proj + b_proj
        return out

    def _L0_ffn_ref(x, ln_g, ln_b, abel_w, abel_b, gate_w_moe, gate_b_moe, w1, b1, w2, b2, gens, mix_w, mix_b):
        import jax, jax.numpy as jnp
        import numpy as np
        from jax.scipy.linalg import expm
        B, S, D, E, K, NROT = (2, 256, 128, 8, 2, 3)
        DF = 4 * D
        EPS = 1e-05
        residual = x
        mu = jnp.mean(x, axis=-1, keepdims=True)
        var = jnp.mean((x - mu) ** 2, axis=-1, keepdims=True)
        xn = (x - mu) * jax.lax.rsqrt(var + EPS) * ln_g + ln_b
        abel = jax.nn.gelu(xn @ abel_w + abel_b, approximate=False)
        logits = xn @ gate_w_moe + gate_b_moe
        tw, ti = jax.lax.top_k(logits, K)
        tw = jax.nn.softmax(tw, axis=-1)
        onehot = (ti[..., None] == jnp.arange(E)).astype(tw.dtype)
        wdense = jnp.sum(tw[..., None] * onehot, axis=2)
        h = jax.nn.gelu(jnp.einsum('bsd,edf->besf', xn, w1) + b1[None, :, None, :], approximate=False)
        eo = jnp.einsum('besf,efd->besd', h, w2) + b2[None, :, None, :]
        moe = jnp.einsum('besd,bse->bsd', eo, wdense)
        rot = expm(gens[0])
        for i in range(1, NROT):
            rot = rot @ expm(gens[i])
        nonabel = moe @ rot
        combined = jnp.concatenate([abel, nonabel], axis=-1)
        g = jax.nn.sigmoid(combined @ mix_w + mix_b)
        return residual + abel * (1.0 - g) + nonabel * g

    def _L1_xattn_ref(query, key, value, mask, Wq, bq, Wk, bk, Wv, bv, Wo, bo):
        import jax, jax.numpy as jnp
        import numpy as np
        B, S, D, H = (2, 256, 128, 16)
        HD = D // H
        b = query.shape[0]

        def split_heads(x):
            return x.reshape(b, -1, H, HD).transpose(0, 2, 1, 3)
        q = split_heads(query @ Wq + bq)
        k = split_heads(key @ Wk + bk)
        v = split_heads(value @ Wv + bv)
        scores = jnp.einsum('bhqd,bhkd->bhqk', q, k) / np.sqrt(HD).astype(jnp.float32)
        scores = jnp.where(mask == 0, jnp.float32(-10000.0), scores)
        p = jax.nn.softmax(scores, axis=-1)
        x = jnp.einsum('bhqk,bhkd->bhqd', p, v)
        x = x.transpose(0, 2, 1, 3).reshape(b, -1, D)
        return x @ Wo + bo

    def _L1_attn_ref(x, qK, qV, kK, kV, vK, vV, pK, pV, fK, fV):
        import jax, jax.numpy as jnp
        import numpy as np
        EMB = 128
        HEADS = 16
        EPS = 1e-05

        def layer_norm(x):
            mu = jnp.mean(x, axis=-1, keepdims=True)
            var = jnp.var(x, axis=-1, keepdims=True)
            return (x - mu) / jnp.sqrt(var + EPS)

        def pattention(x, K, V):
            scale = EMB ** (-0.5)
            a = jax.nn.softmax(scale * jnp.einsum('btc,nc->btn', x, K), axis=-1)
            return jnp.einsum('btn,nc->btc', a, V)

        def causal_sdpa(q, k, v):
            T = q.shape[2]
            d = q.shape[-1]
            scores = jnp.einsum('bhqd,bhkd->bhqk', q, k) / jnp.sqrt(jnp.asarray(d, q.dtype))
            mask = jnp.tril(jnp.ones((T, T), dtype=bool))
            scores = jnp.where(mask, scores, jnp.asarray(-jnp.inf, q.dtype))
            attn = jax.nn.softmax(scores, axis=-1)
            return jnp.einsum('bhqk,bhkd->bhqd', attn, v)
        B, T, C = x.shape
        H = HEADS
        D = C // H
        x_in = x
        h = layer_norm(x)
        k = pattention(h, kK, kV)
        q = pattention(h, qK, qV)
        v = pattention(h, vK, vV)
        to_heads = lambda t: t.reshape(B, T, H, D).transpose(0, 2, 1, 3)
        o = causal_sdpa(to_heads(q), to_heads(k), to_heads(v))
        o = o.transpose(0, 2, 1, 3).reshape(B, T, C)
        o = pattention(o, pK, pV)
        x = o + x_in
        x_inter = x
        x = pattention(layer_norm(x), fK, fV)
        return x + x_inter

    def _L1_ffn_ref(x, router_w, router_b, W, V, W_out):
        import jax, jax.numpy as jnp
        import numpy as np
        B, T = (2, 256)
        D_MODEL, D_HIDDEN = (128, 256)
        N_EXPERTS, TOP_K = (8, 2)
        N_TOKENS = B * T
        CAPACITY = 2 * N_TOKENS * TOP_K // N_EXPERTS
        Bq, Tq, D = x.shape
        N = Bq * Tq
        x_flat = x.reshape(N, D)
        router_logits = x_flat @ router_w.T + router_b
        top_vals, top_ids = jax.lax.top_k(router_logits, TOP_K)
        top_probs = jax.nn.softmax(top_vals, axis=-1)
        x_pad = jnp.concatenate([x_flat, jnp.zeros((1, D), x_flat.dtype)], axis=0)
        probs_pad = jnp.concatenate([top_probs, jnp.zeros((1, TOP_K), top_probs.dtype)], axis=0)
        out = jnp.zeros((N + 1, D), x_flat.dtype)
        for e in range(N_EXPERTS):
            tok, slot = jnp.nonzero(top_ids == e, size=CAPACITY, fill_value=(N, 0))
            w = probs_pad[tok, slot][:, None]
            xin = x_pad[tok]
            a = xin @ W[e]
            b = xin @ V[e]
            y = a * (b * jax.nn.sigmoid(b)) @ W_out[e]
            out = out.at[tok].add(y * w)
        return out[:N].reshape(Bq, Tq, D)
    x = x + _L0_xattn_ref(_layernorm(x, axis=-1), ctx_1024, ctx_1024, mask_BxSxS2_ik0, L0_xattn_Wq, L0_xattn_bq, L0_xattn_Wk, L0_xattn_bk, L0_xattn_Wv, L0_xattn_bv, L0_xattn_Wo, L0_xattn_bo)
    x = x + _L0_attn_ref(_layernorm(x, axis=-1), L0_attn_w_qkv, L0_attn_b_qkv, L0_attn_w_proj, L0_attn_b_proj)
    x = x + _L0_ffn_ref(_layernorm(x, axis=-1), L0_ffn_ln_g, L0_ffn_ln_b, L0_ffn_abel_w, L0_ffn_abel_b, L0_ffn_gate_w_moe, L0_ffn_gate_b_moe, L0_ffn_w1, L0_ffn_b1, L0_ffn_w2, L0_ffn_b2, L0_ffn_gens, L0_ffn_mix_w, L0_ffn_mix_b)
    x = x + _L1_xattn_ref(_layernorm(x, axis=-1), ctx_1024, ctx_1024, mask_Bx1x1xS2_ik0, L1_xattn_Wq, L1_xattn_bq, L1_xattn_Wk, L1_xattn_bk, L1_xattn_Wv, L1_xattn_bv, L1_xattn_Wo, L1_xattn_bo)
    x = x + _L1_attn_ref(_layernorm(x, axis=-1), L1_attn_qK, L1_attn_qV, L1_attn_kK, L1_attn_kV, L1_attn_vK, L1_attn_vV, L1_attn_pK, L1_attn_pV, L1_attn_fK, L1_attn_fV)
    x = x + _L1_ffn_ref(_layernorm(x, axis=-1), L1_ffn_router_w, L1_ffn_router_b, L1_ffn_W, L1_ffn_V, L1_ffn_W_out)
    return x

_drawn_inputs = setup_inputs


def setup_inputs(seed=0):
    import zlib

    import numpy as np

    out = dict(_drawn_inputs(seed))
    spreads = {'L0_ffn_ln_g': (1.0, 0.2),
     'L0_ffn_ln_b': (0.0, 0.1),
     'L0_ffn_abel_b': (0.0, 0.418),
     'L0_ffn_gate_b_moe': (0.0, 0.1),
     'L0_ffn_b1': (0.0, 0.392),
     'L0_ffn_b2': (0.0, 0.313),
     'L1_xattn_bq': (0.0, 0.493),
     'L1_xattn_bk': (0.0, 2.0),
     'L1_xattn_bv': (0.0, 0.1),
     'L1_xattn_bo': (0.0, 0.1),
     'L1_ffn_router_b': (0.0, 0.1)}
    factors = {'L0_xattn_bq': 7.697,
     'L0_xattn_bk': 64.0,
     'L1_attn_qK': 8.0,
     'L1_attn_qV': 8.0,
     'L1_attn_kK': 8.0,
     'L1_attn_kV': 8.0,
     'L1_attn_vK': 8.0,
     'L1_attn_vV': 7.973,
     'L1_attn_pK': 8.0,
     'L1_attn_fK': 2.685}
    for name, (base, spread) in spreads.items():
        noise = np.random.default_rng([zlib.crc32(name.encode()), seed]).standard_normal(out[name].shape)
        drawn = base * np.exp(spread * noise) if base else spread * noise
        out[name] = jnp.asarray(drawn.astype(out[name].dtype))
    for name, factor in factors.items():
        out[name] = (out[name] * factor).astype(out[name].dtype)
    return out
```

```python
import concourse.bass as bass
from concourse import mybir
from contextlib import ExitStack

NB, NQ, NK, D = 32, 32, 257, 128
TOKENS = NB * NQ
P = 128
TILES = TOKENS // P
BPT = P // NQ
GROUPS = 2
TPG = TILES // GROUPS
GW = TPG * P
H, HD = 16, D // 16
HG = 4
HPG = H // HG
KC = NK // P
LAST = KC * P
NE, DF, DH = 8, 4 * D, 256
CAPACITY = 2 * 512 * 2 // NE
EPS = 1e-5
NEG = -1e30
SQUARINGS, ORDER = 3, 10


def perceiver(nc, io, out_d, stop_after=None):
    fp32, i32, u32 = mybir.dt.float32, mybir.dt.int32, mybir.dt.uint32
    ALU, ACT, AX = mybir.AluOpType, mybir.ActivationFunctionType, mybir.AxisListType.X

    ctx = ExitStack()
    with ctx:
        def sb(name, shape, dt=fp32):
            return ctx.enter_context(nc.sbuf_tensor(name, shape, dt))

        sems = {}

        norms = ("b", "c", "d", "e", "f", "f2", "g")
        in_stages = {name: {st: GROUPS for st in norms} for name in ("var", "rstd", "h", "hT_p", "hT")}
        in_stages.update({name: {"b": n, "c": m, "f": m} for name, n, m in
                          (("scores", TILES, GROUPS), ("exp", TILES, GROUPS), ("inv", TILES, GROUPS), ("pT", TILES, TILES), ("probsT", TILES, TILES))})
        in_stages.update({name: {"c": n, "f": n} for name, n in
                          (("v_in", TILES), ("v", TILES), ("v_heads", TILES), ("k_heads", TILES), ("shifted", GROUPS * HG), ("inv_tok", GROUPS),
                           ("out", GROUPS), ("inv_rows", GROUPS), ("oT", GROUPS), ("k_p", GROUPS), ("kT", GROUPS))})
        in_stages.update({
            "q_p": {st: GROUPS for st in "bcef"}, "qT": {st: GROUPS for st in "bcef"},
            "x_bias": {st: GROUPS for st in "bce"}, "obT": {st: GROUPS for st in "ce"}, "projected": {st: GROUPS for st in "ce"},
            "x": {st: GROUPS for st in "cdef"}, "x_res": {st: GROUPS for st in "df"},
            "wT_p": {"b": 1, "m": 1, "d": 1, "f": 2, "g": 1}, "wT": {"b": 1, "m": 1, "d": 1, "f": 2, "g": 1},
            "logits": {"d": 1, "g": 1}, "top_diff": {"d": 1, "g": 1}, "top_exp": {"d": 1, "g": 1},
            "up": {"d": 8 * NE, "g": 4 * NE}, "down": {st: GROUPS * NE for st in "dg"}, "acc": {st: GROUPS * (NE + 1) for st in "dg"},
        })
        in_stages.update({f"{w}_loaded{slot}": {"d": 16 * NE // 2, "g": n * 16 * NE // 2} for w, n in (("w1", 2), ("w2", 1)) for slot in range(2)})

        def stage_of(name):
            stage, _, rest = name.partition("_")
            return (stage, rest) if rest in in_stages and stage in in_stages[rest] else (None, name)

        def sem(name):
            name = stage_of(name)[1]
            if name not in sems:
                sems[name] = ctx.enter_context(nc.semaphore(name))
            return sems[name]

        def nth(name, n):
            stage, rest = stage_of(name)
            if stage is not None:
                stages = list(in_stages[rest])
                n = n + sum(in_stages[rest][st] for st in stages[:stages.index(stage)])
            return sem(name), n

        x = sb("x", [P, TILES, D])
        res = sb("res", [P, TILES, D])
        h = sb("h", [P, TILES, D])
        hT = sb("hT", [P, TOKENS])
        qT = sb("qT", [P, TOKENS])
        kT = sb("kT", [P, TOKENS])
        oT = sb("oT", [P, TOKENS])
        aT = sb("aT", [P, TOKENS])
        r1 = sb("r1", [P, NB * KC * D])
        ctxT = sb("ctxT", [P, NB, NK])
        r3 = sb("r3", [P, 4096])
        r4 = sb("r4", [P, 4096])
        r5 = sb("r5", [P, 4096])
        r6 = sb("r6", [P, 4096])
        ctx_last = sb("ctx_last", [NB, D])
        ident = sb("ident", [P, P])
        ones = sb("ones", [P, P])
        blk = sb("blk", [P, HG, HPG])
        head_mask = sb("head_mask", [P, HPG])
        v_mask = sb("v_mask", [P, HG, HPG, HD])
        causal4 = sb("causal4", [P, BPT, NQ])
        causal = sb("causal", [P, NQ])
        last_mask = sb("last_mask", [P, TILES, NB])
        stats = sb("stats", [P, TILES, 6])
        mean_var = sb("mean_var", [P, TILES, 2])
        var_eps = sb("var_eps", [P, 2, TILES])
        rstd = sb("rstd", [P, 2, TILES])
        minus_half = sb("minus_half", [P, 2 * TILES])
        w_a = sb("w_a", [P, 4, D])
        w_aT = sb("w_aT", [P, 4, D])
        w_b = sb("w_b", [P, 4, D])
        w_bT = sb("w_bT", [P, 4, D])
        wk0 = sb("wk0", [P, D])
        w_qkv = sb("w_qkv", [P, 3 * D])
        w_proj = sb("w_proj", [P, D])
        cols = sb("cols", [P, 16])
        bo_row = sb("bo_row", [P, D])
        bproj_row = sb("bproj_row", [P, D])
        q_bk = sb("q_bk", [P, TILES])
        row_max = sb("row_max", [P, 4 * TILES])
        row_sum = sb("row_sum", [P, 4 * TILES])
        row_inv = sb("row_inv", [P, 4 * TILES])
        head_max = sb("head_max", [P, GROUPS, HG, TPG * HPG])
        head_sum = sb("head_sum", [P, GROUPS, HG, TPG * HPG])
        head_inv = sb("head_inv", [P, GROUPS, HG, TPG * HPG])
        taylor = sb("taylor", [P, 3, D])
        gen = sb("gen", [P, 3, D])
        genT = sb("genT", [P, 3, D])
        taylorT = sb("taylorT", [P, 3, D])
        pair = sb("pair", [P, D])
        rot = sb("rot", [P, D])
        abel_w = sb("abel_w", [P, D])
        abel_row = sb("abel_row", [P, D])
        gate_w = sb("gate_w", [P, NE])
        gate_row = sb("gate_row", [P, NE])
        mix_row = sb("mix_row", [P, 2 * D])
        mix_b = sb("mix_b", [P, 1])
        mix_z = sb("mix_z", [P, 3, TILES])
        mix_g = sb("mix_g", [P, TILES])
        b1_rows = sb("b1_rows", [NE * 4, D])
        b1_cols = sb("b1_cols", [P, NE * 4])
        b1_now = sb("b1_now", [P, 2, 4])
        b2_rows = sb("b2_rows", [NE, D])
        w1 = sb("w1", [P, 2, DF])
        w2 = sb("w2", [P, 2, 4, D])
        iota_i = sb("iota_i", [P, NE], i32)
        iota8 = sb("iota8", [P, NE])
        logits = sb("logits", [P, TILES, NE])
        top8 = sb("top8", [P, TILES, 8])
        top_index = sb("top_index", [P, TILES, 8], u32)
        top_f = sb("top_f", [P, TILES, 2])
        top_p = sb("top_p", [P, 3, TILES])
        pick = sb("pick", [P, 2, TILES, NE])
        w_token = sb("w_token", [P, NE, TILES])
        w_tokenT = sb("w_tokenT", [NE, TOKENS])
        w_e = sb("w_e", [P, 4, D])
        bo1_row = sb("bo1_row", [P, D])
        e_group16 = sb("e_group16", [4 * HG, BPT, HG])
        e_group = sb("e_group", [4 * HG, HG])
        e_last_in = sb("e_last_in", [P, 2, BPT * HG])
        e_v_last = sb("e_v_last", [BPT * HG, 2, D])
        e_p_last = sb("e_p_last", [P, BPT, BPT * HG])
        e_p_lastT = sb("e_p_lastT", [BPT * HG, 2, P])
        e_max = sb("e_max", [P, BPT * HG])
        e_nmax = sb("e_nmax", [P, BPT * HG])
        e_sum = sb("e_sum", [P, BPT * HG])
        e_inv = sb("e_inv", [P, BPT * HG])
        f_max = sb("f_max", [P, 5, TILES])
        f_nmax = sb("f_nmax", [P, 5, TILES])
        f_sum = sb("f_sum", [P, 5, TILES])
        f_inv = sb("f_inv", [P, 5, TILES])
        routerT = sb("routerT", [P, NE])
        router_row = sb("router_row", [P, NE])
        bank = [ctx.enter_context(nc.psum_tensor(f"bank{i}", [P, 512], fp32)) for i in range(8)]

        ctx_keys = r1[:, :].rearrange("p (b c d) -> p b c d", b=NB, c=KC)
        BQ0, BV0, BQ, BK, BV, BK0, LN_G, LN_B, BQ1, BK1, BV1 = range(11)

        def group_bank(g, k):
            return bank[4 * g + k]

        def gx(t, g):
            return t[:, g * TPG:(g + 1) * TPG, :] if len(t.shape) == 3 else t[:, g * GW:(g + 1) * GW]

        step_count = {"v": 0, "g": 0, "a": 0}

        def link(eng, key, ins):
            step_count[key] += 1
            ins.then_inc(sem("step_" + key), 1)
            eng.wait_ge(sem("step_" + key), step_count[key])

        def k_heads(g):
            return (r4 if g == 0 else r5)[:, 0:TPG * 512].rearrange("p (j b n) -> p j b n", j=TPG, b=BPT)

        def v_heads(g):
            return (r4 if g == 0 else r5)[:, TPG * 512:2 * TPG * 512].rearrange("p (j b n) -> p j b n", j=TPG, b=BPT)

        def probs(g):
            return r3[:, g * 2048:(g + 1) * 2048].rearrange("p (a j n) -> p a j n", a=HG, j=TPG)

        def v_in(g):
            return r3[:, g * 2048:(g + 1) * 2048].rearrange("p (j b n) -> p j b n", j=TPG, b=BPT)

        def probsT(g):
            return r6[:, g * 2048:(g + 1) * 2048].rearrange("p (j a n) -> p j a n", j=TPG, a=HG)

        def b_probs(t):
            return r3[:, t * NK:(t + 1) * NK]

        def b_probsT(t):
            return r5[:, t * LAST:(t + 1) * LAST]

        b_last = r6[:, 0:TILES * NB].rearrange("p (t b) -> p t b", t=TILES)
        b_lastT = r6[0:NB, 512:512 + TILES * P].rearrange("p (t n) -> p t n", t=TILES)
        b_mask = r4[:, 0:TILES * NK].rearrange("p (t k) -> p t k", t=TILES)

        def in_slots(t, at, n):
            return [t[:, at + i * n:at + (i + 1) * n] for i in range(2)]

        e_k = [a.rearrange("p (b k) -> p b k", b=BPT) for a in in_slots(r1, 0, BPT * NK)]
        e_keep = [a.rearrange("p (b k) -> p b k", b=BPT) for a in in_slots(r1, 2 * BPT * NK, BPT * NK)]
        e_add = [a.rearrange("p (b k) -> p b k", b=BPT) for a in
                 (r1[:, 4 * BPT * NK:5 * BPT * NK], r6[:, 0:BPT * NK])]
        e_mask = [a.bitcast(i32).rearrange("p (b k) -> p b k", b=BPT) for a in in_slots(r6, BPT * NK, BPT * NK)]
        e_q = [a.rearrange("p (b h q) -> p b h q", b=BPT, h=HPG) for a in in_slots(res[:, :, :].rearrange("p t d -> p (t d)"), 0, 512)]
        e_probs = [(r3[:, b * HG * NK:(b + 1) * HG * NK] if b < 3 else r4[:, 0:HG * NK]).rearrange("p (g k) -> p g k", g=HG)
                   for b in range(BPT)]
        e_ctx = [a.rearrange("p (b k) -> p b k", b=BPT) for a in in_slots(r4, NK * HG, BPT * LAST)]
        e_v = [a.rearrange("p (b c d) -> p b c d", b=BPT, c=KC) for a in in_slots(r5, 0, BPT * LAST)]
        e_probsT = [a.rearrange("p (c g n) -> p c g n", c=KC, g=HG) for a in in_slots(r5, 2 * BPT * LAST, KC * 512)]
        e_inv_tok = aT[:, :].rearrange("p (s b n) -> p s b n", s=2, b=BPT)
        e_scale = h[:, 0:TPG, :].rearrange("p b (g q) -> p b g q", g=HPG)
        e_out = h[:, TPG:TILES, :].rearrange("p b (g q) -> p b g q", g=HPG)

        F0 = 5 * BPT * NK
        w_v = r1[:, F0:F0 + 4 * D].rearrange("p (i d) -> p i d", i=4)
        f_k = r1[:, F0 + 4 * D:F0 + 8 * D].rearrange("p (i d) -> p i d", i=4)
        f_kT = r1[:, F0 + 8 * D:F0 + 12 * D]
        f_v = r1[:, F0 + 12 * D:F0 + 16 * D].rearrange("p (i d) -> p i d", i=4)

        G0 = F0 + 16 * D
        before = r1[:, G0:G0 + P]
        router_rows = r1[0:NE, G0 + P:G0 + P + D]
        picked, picked_before, kept = (r1[:, G0 + P + D + i * TILES * NE:G0 + P + D + (i + 1) * TILES * NE].rearrange("p (t e) -> p t e", t=TILES)
                                       for i in range(3))

        def patterns(g):
            return r3[:, g * 2048:g * 2048 + 1536].rearrange("p (j i n) -> p j i n", j=TPG, i=3)

        def p_probs(g):
            return r3[:, g * 2048:g * 2048 + 512].rearrange("p (j n) -> p j n", j=TPG)

        def f_probs(g):
            return (r4 if g == 0 else r5)[:, 0:2048].rearrange("p (j c n) -> p j c n", j=TPG, c=4)

        def silu_b(n):
            return r5[:, n * 512:(n + 1) * 512]

        abel = oT[:, :].rearrange("p (t d) -> p t d", t=TILES)
        moe = kT[:, :].rearrange("p (t d) -> p t d", t=TILES)
        moeT = aT
        mixed = h

        def hidden(slot):
            return (r3 if slot == 0 else r4)[:, :].rearrange("p (c n) -> p c n", c=4)

        block = ctx.enter_context(nc.Block())

        def w1_d(e):
            return io["L0_ffn_w1"].rearrange("e p f -> (e p) f")[bass.ds(e * D, D), :]

        def w2_d(e):
            return io["L0_ffn_w2"].rearrange("e f d -> (e f) d")[bass.ds(e * DF, DF), :].rearrange("(c p) d -> p c d", c=4)

        @block.sync
        def _(sp):
            sp.dma_start(x[:, :, :], io["x"].rearrange("(t b) q d -> (b q) t d", t=TILES)).then_inc(sem("x_loaded"), 16)
            for i, name in enumerate(("L0_xattn_Wq", "L0_xattn_Wv", "L0_xattn_Wo", "L1_attn_pK")):
                sp.dma_start(w_a[:, i, :], io[name]).then_inc(sem("w_a_loaded"), 16)
            sp.dma_start(wk0[:, :], io["L0_xattn_Wk"]).then_inc(sem("b_w_loaded"), 16)
            for c, name in ((BQ0, "L0_xattn_bq"), (BV0, "L0_xattn_bv"), (BK0, "L0_xattn_bk")):
                sp.dma_start(cols[:, c:c + 1], io[name].rearrange("(p a) -> p a", a=1)).then_inc(sem("b_w_loaded"), 16)
            sp.dma_start(bo_row[:, :], io["L0_xattn_bo"].rearrange("(a n) -> a n", a=1).broadcast_to([P, D])).then_inc(sem("b_w_loaded"), 16)
            mask_i = r4[:, 0:TILES * NK].bitcast(i32).rearrange("p (t k) -> p t k", t=TILES)
            sp.dma_start(mask_i, io["mask_BxSxS2_ik0"].rearrange("(t b) q k -> (b q) t k", t=TILES)).then_inc(sem("mask0_loaded"), 16)
            sp.dma_start(gen[:, :, :], io["L0_ffn_gens"].rearrange("i p n -> p i n")).then_inc(sem("gen_loaded"), 16)
            sp.dma_start(ctx_last[:, :], io["ctx_1024"][:, LAST, :]).then_inc(sem("ctx_last_loaded"), 16)
            for b in range(0, NB, 8):
                for c in range(KC):
                    sp.dma_start(ctx_keys[:, b:b + 8, c, :], io["ctx_1024"][b:b + 8, c * P:(c + 1) * P, :].rearrange("b k d -> k b d")).then_inc(sem(f"ctx_loaded{b // 8}"), 16)
            sp.dma_start(w_qkv[:, :], io["L0_attn_w_qkv"]).then_inc(sem("c_w_loaded"), 16)
            sp.dma_start(w_proj[:, :], io["L0_attn_w_proj"]).then_inc(sem("c_w_loaded"), 16)
            for i, c in enumerate((BQ, BK, BV)):
                sp.dma_start(cols[:, c:c + 1], io["L0_attn_b_qkv"][i * D:(i + 1) * D].rearrange("(p a) -> p a", a=1)).then_inc(sem("c_w_loaded"), 16)
            sp.dma_start(bproj_row[:, :], io["L0_attn_b_proj"].rearrange("(a n) -> a n", a=1).broadcast_to([P, D])).then_inc(sem("c_w_loaded"), 16)
            for name, dst, src in (
                ("d", abel_w[:, :], io["L0_ffn_abel_w"]), ("d", gate_w[:, :], io["L0_ffn_gate_w_moe"]),
                ("d", cols[:, LN_G:LN_G + 1], io["L0_ffn_ln_g"].rearrange("(p a) -> p a", a=1)),
                ("d", cols[:, LN_B:LN_B + 1], io["L0_ffn_ln_b"].rearrange("(p a) -> p a", a=1)),
                ("d", abel_row[:, :], io["L0_ffn_abel_b"].rearrange("(a n) -> a n", a=1).broadcast_to([P, D])),
                ("d", gate_row[:, :], io["L0_ffn_gate_b_moe"].rearrange("(a n) -> a n", a=1).broadcast_to([P, NE])),
                ("d", mix_row[:, :], io["L0_ffn_mix_w"].rearrange("n a -> a n").broadcast_to([P, 2 * D])),
                ("d", mix_b[:, :], io["L0_ffn_mix_b"].rearrange("(a n) -> a n", a=1).broadcast_to([P, 1])),
                ("d", b1_rows[:, :], io["L0_ffn_b1"].rearrange("e (c p) -> (e c) p", c=4)),
                ("d", b2_rows[:, :], io["L0_ffn_b2"]),
            ):
                sp.dma_start(dst, src).then_inc(sem("d_w_loaded"), 16)

            for i, name in enumerate(("Wq", "Wk", "Wv", "Wo")):
                sp.dma_start(w_e[:, i, :], io["L1_xattn_" + name]).then_inc(sem("e_w_loaded"), 16)
            for c, name in ((BQ1, "bq"), (BK1, "bk"), (BV1, "bv")):
                sp.dma_start(cols[:, c:c + 1], io["L1_xattn_" + name].rearrange("(p a) -> p a", a=1)).then_inc(sem("e_w_loaded"), 16)
            sp.dma_start(bo1_row[:, :], io["L1_xattn_bo"].rearrange("(a n) -> a n", a=1).broadcast_to([P, D])).then_inc(sem("e_w_loaded"), 16)

            for i, name in enumerate(("qK", "kK", "vK")):
                sp.dma_start(w_b[:, i, :], io["L1_attn_" + name]).then_inc(sem("f_w_loaded"), 16)
            sp.dma_start(router_row[:, :], io["L1_ffn_router_b"].rearrange("(a n) -> a n", a=1).broadcast_to([P, NE])).then_inc(sem("g_w_loaded"), 16)
            sp.wait_ge(sem("b_av"), TILES)
            sp.dma_start(router_rows[:, :], io["L1_ffn_router_w"]).then_inc(sem("g_w_loaded"), 16)
            for i, name in enumerate(("qV", "kV", "vV", "pV")):
                sp.dma_start(w_v[:, i, :], io["L1_attn_" + name]).then_inc(sem("f_w_loaded"), 16)
            sp.dma_start(f_k, io["L1_attn_fK"].rearrange("(i p) d -> p i d", i=4)).then_inc(sem("f_w_loaded"), 16)
            sp.dma_start(f_v, io["L1_attn_fV"].rearrange("(i p) d -> p i d", i=4)).then_inc(sem("f_w_loaded"), 16)

            def load_expert(e, slot):
                sp.dma_start(w1[:, slot, :], w1_d(e)).then_inc(sem(f"d_w1_loaded{slot}"), 16)
                sp.dma_start(w2[:, slot, :, :], w2_d(e)).then_inc(sem(f"d_w2_loaded{slot}"), 16)

            load_expert(0, 0)
            load_expert(1, 1)
            with sp.Fori(1, NE // 2) as pair_of_experts:
                e = 2 * pair_of_experts
                for slot in range(2):
                    sp.wait_ge(*nth("d_up", 8 * (e + (slot - 1))))
                    sp.dma_start(w1[:, slot, :], w1_d(e + slot)).then_inc(sem(f"d_w1_loaded{slot}"), 16)
                    sp.wait_ge(*nth("d_down", 2 * (e + (slot - 1))))
                    sp.dma_start(w2[:, slot, :, :], w2_d(e + slot)).then_inc(sem(f"d_w2_loaded{slot}"), 16)
            def load_mask(t, slot):
                src = io["mask_Bx1x1xS2_ik0"].rearrange("b a c k -> (a c) (b k)")[:, bass.ds(t * BPT * NK, BPT * NK)]
                sp.dma_start(r6[:, (1 + slot) * BPT * NK:(2 + slot) * BPT * NK].bitcast(i32),
                             src.broadcast_to([P, BPT * NK])).then_inc(sem(f"e_mask_loaded{slot}"), 16)

            sp.wait_ge(sem("d_done"), 1)
            load_mask(0, 0)
            load_mask(1, 1)
            with sp.Fori(1, TILES // 2) as pair_of_tiles:
                for slot in range(2):
                    t = 2 * pair_of_tiles + slot
                    sp.wait_ge(sem("e_prep"), t - 1)
                    load_mask(t, slot)
            def load_gated(e, slot):
                for i, name in enumerate(("W", "V")):
                    sp.dma_start(w1[:, slot, i * DH:(i + 1) * DH],
                                 io["L1_ffn_" + name].rearrange("e p f -> (e p) f")[bass.ds(e * D, D), :]).then_inc(sem(f"g_w1_loaded{slot}"), 16)

            def load_gated_out(e, slot):
                sp.dma_start(w2[:, slot, 0:2, :], io["L1_ffn_W_out"].rearrange("e f d -> (e f) d")[bass.ds(e * DH, DH), :]
                             .rearrange("(c p) d -> p c d", c=2)).then_inc(sem(f"g_w2_loaded{slot}"), 16)

            for e in range(2):
                load_gated(e, e)
                load_gated_out(e, e)
            with sp.Fori(1, NE // 2) as pair_of_experts:
                e = 2 * pair_of_experts
                for slot in range(2):
                    sp.wait_ge(*nth("g_up", 4 * (e + (slot - 1))))
                    load_gated(e + slot, slot)
                    sp.wait_ge(*nth("g_down", 2 * (e + (slot - 1))))
                    load_gated_out(e + slot, slot)
            for g in range(GROUPS):
                sp.wait_ge(sem("x_final"), g + 1)
                sp.dma_start(out_d.rearrange("(t b) q d -> (b q) t d", t=TILES)[:, g * TPG:(g + 1) * TPG, :], gx(x, g)).then_inc(sem("stored"), 16)
            sp.wait_ge(sem("stored"), 16 * GROUPS)

        def pool_rstd(gp, ph, g, n):
            gp.wait_ge(*nth(ph + "_var", g + 1))
            sl = slice(g * TPG, (g + 1) * TPG)
            mh = minus_half[:, 0:n * TPG].rearrange("p (n t) -> p n t", n=n)
            nc.gpsimd.tensor_tensor(rstd[:, 0:n, sl], var_eps[:, 0:n, sl], mh, ALU.pow).then_inc(sem(ph + "_rstd"), 1)

        def pool_add_row(gp, ph, g, row, loaded):
            gp.wait_ge(*nth(loaded[0], loaded[1]))
            gp.wait_ge(*nth(ph + "_h", g + 1))
            nc.gpsimd.tensor_tensor(gx(x, g), gx(x, g), row[:, :].unsqueeze(1).broadcast_to([P, TPG, D]), ALU.add).then_inc(sem(ph + "_x_bias"), 1)

        def pool_k_heads(gp, ph, g):
            kx = r4 if g == 0 else r5
            gp.wait_ge(*nth(ph + "_kT", g + 1))
            for j in range(TPG):
                src = kT[:, g * GW + j * P:g * GW + (j + 1) * P].rearrange("p (b k) -> p b k", b=BPT)
                for b in range(BPT):
                    i = nc.gpsimd.tensor_tensor(
                        k_heads(g)[:, j, b, :].rearrange("p (h k) -> p h k", h=HPG),
                        src[:, b, :].unsqueeze(1).broadcast_to([P, HPG, NQ]),
                        head_mask[:, :].unsqueeze(2).broadcast_to([P, HPG, NQ]), ALU.mult)
                i.then_inc(sem(ph + "_k_heads"), 1)

        def pool_v_in(gp, ph, g, src, ready):
            gp.wait_ge(*nth(ready, g + 1))
            for j in range(TPG):
                for b in range(BPT):
                    at = g * GW + j * P + b * NQ
                    i = nc.gpsimd.tensor_copy(v_in(g)[:, j, b, :].rearrange("p (h k) -> p h k", h=HPG),
                                              src[:, at:at + NQ].unsqueeze(1).broadcast_to([P, HPG, NQ]))
                i.then_inc(sem(ph + "_v_in"), 1)

        def pool_inv_tok(gp, ph, g):
            gp.wait_ge(*nth(ph + "_inv", g + 1))
            for j in range(TPG):
                dst = h[:, g * TPG + j, :].rearrange("p (a h d) -> p a h d", a=HG, h=HPG)
                i = nc.gpsimd.tensor_copy(dst, head_inv[:, g, :, j * HPG:(j + 1) * HPG].unsqueeze(3).broadcast_to([P, HG, HPG, HD]))
            i.then_inc(sem(ph + "_inv_tok"), 1)

        @block.gpsimd
        def _(gp):
            nc.gpsimd.memset(minus_half[:, :], -0.5)
            nc.gpsimd.memset(ident[:, :], 0.0)
            nc.gpsimd.memset(ones[:, :], 1.0)
            nc.gpsimd.memset(blk[:, :, :], 1.0)
            nc.gpsimd.memset(v_mask[:, :, :, :], 1.0)
            nc.gpsimd.memset(causal4[:, :, :], 0.0)
            nc.gpsimd.memset(e_group16[:, :, :], 1.0)
            nc.gpsimd.memset(e_p_last[:, :, :], 0.0)
            link(gp, "g", nc.gpsimd.memset(last_mask[:, :, :], 1.0))

            def keep(t, pattern, base, chan, fill, op=ALU.is_ge):
                link(gp, "g", nc.gpsimd.affine_select(out=t, in_=t, compare_op=op, fill=fill, base=base,
                                                      pattern=pattern, channel_multiplier=chan))

            keep(ident[:, :], [[-1, P]], 0, 1, 1.0, ALU.not_equal)
            keep(blk[:, :, :], [[-NQ, HG], [-HD, HPG]], 0, 1, 0.0)
            keep(blk[:, :, :], [[NQ, HG], [HD, HPG]], HD - 1, -1, 0.0)
            keep(v_mask[:, :, :, :], [[0, HG], [-NQ, HPG], [0, HD]], 0, 1, 0.0)
            keep(v_mask[:, :, :, :], [[0, HG], [NQ, HPG], [0, HD]], NQ - 1, -1, 0.0)
            keep(causal4[:, :, :], [[-NQ, BPT], [-1, NQ]], 0, 1, NEG)
            keep(causal4[:, :, :], [[-NQ, BPT], [0, NQ]], 0, 1, 0.0)
            keep(last_mask[:, :, :], [[P, TILES], [-NQ, NB]], 0, 1, 0.0)
            keep(last_mask[:, :, :], [[-P, TILES], [NQ, NB]], NQ - 1, -1, 0.0)
            keep(e_group16[:, :, :], [[-HG, BPT], [-1, HG]], 0, 1, 0.0, ALU.is_equal)
            link(gp, "g", nc.gpsimd.iota(iota_i[:, :], pattern=[[1, NE]], base=0, channel_multiplier=0))
            gp.sem_inc(sem("constants"), 1)
            for g in range(GROUPS):
                pool_rstd(gp, "b", g, 1)
            for g in range(GROUPS):
                pool_add_row(gp, "b", g, bo_row, ("b_w_loaded", 16 * 5))
            gp.wait_ge(sem("b_av"), TILES)
            link(gp, "g", nc.gpsimd.memset(before[:, :], 1.0))
            nc.gpsimd.affine_select(out=before[:, :], in_=before[:, :], compare_op=ALU.is_ge, fill=0.0, base=-1,
                                    pattern=[[1, P]], channel_multiplier=-1).then_inc(sem("g_before"), 1)
            for g in range(GROUPS):
                pool_rstd(gp, "c", g, 1)
            for g in range(GROUPS):
                pool_add_row(gp, "c", g, bproj_row, ("c_w_loaded", 16 * 6))
            for g in range(GROUPS):
                pool_v_in(gp, "c", g, hT, "c_hT")
            for g in range(GROUPS):
                pool_k_heads(gp, "c", g)
            for g in range(GROUPS):
                pool_inv_tok(gp, "c", g)
            for g in range(GROUPS):
                pool_rstd(gp, "d", g, 2)
            for g in range(GROUPS):
                gp.wait_ge(*nth("d_h", g + 1))
                nc.gpsimd.tensor_tensor(gx(x, g), gx(x, g), gx(res, g), ALU.add).then_inc(sem("d_x_res"), 1)
            for g in range(GROUPS):
                pool_rstd(gp, "e", g, 1)
            for g in range(GROUPS):
                pool_add_row(gp, "e", g, bo1_row, ("e_w_loaded", 16 * 8))
            gp.wait_ge(*nth("e_qT", GROUPS))
            with gp.Fori(0, TILES // 2) as pair_of_tiles:
                for slot in range(2):
                    t = 2 * pair_of_tiles + slot
                    gp.wait_ge(sem("e_done"), t + 1)
                    gp.wait_ge(sem(f"e_mask_loaded{slot}"), 16 * (pair_of_tiles + 1))
                    nc.gpsimd.tensor_tensor(e_q[slot],
                                            qT[:, bass.ds(t * P, P)].rearrange("p (b q) -> p b q", b=BPT).unsqueeze(2).broadcast_to([P, BPT, HPG, NQ]),
                                            head_mask[:, :].unsqueeze(1).unsqueeze(3).broadcast_to([P, BPT, HPG, NQ]),
                                            ALU.mult)
                    nc.gpsimd.tensor_scalar(e_keep[slot], e_mask[slot], 0, 0.0, ALU.is_equal, ALU.is_equal)
                    nc.gpsimd.tensor_scalar(e_add[slot], e_mask[slot], 0, -10000.0 * HD ** 0.5, ALU.is_equal, ALU.mult)
                    nc.gpsimd.tensor_copy(e_ctx[slot], ctxT[:, bass.ds(BPT * t, BPT), 0:LAST])
                    nc.gpsimd.tensor_copy(e_last_in[:, slot, :].rearrange("p (b g) -> p b g", b=BPT),
                                          ctxT[:, bass.ds(BPT * t, BPT), LAST:NK].broadcast_to([P, BPT, HG])).then_inc(sem("e_prep"), 1)
                    for b in range(BPT):
                        gp.wait_ge(*nth("e_exp", BPT * t + (b + 1)))
                        nc.gpsimd.tensor_tensor(e_p_last[:, b, b * HG:(b + 1) * HG], e_probs[b][:, :, LAST:NK].rearrange("p g a -> p (g a)"),
                                                ones[:, 0:HG], ALU.mult).then_inc(sem("e_p_last"), 1)
                        gp.wait_ge(*nth("e_inv", BPT * t + (b + 1)))
                        nc.gpsimd.tensor_tensor(e_inv_tok[:, slot, b, :].rearrange("p (g f) -> p g f", g=HG),
                                                e_inv[:, b * HG:(b + 1) * HG].unsqueeze(2).broadcast_to([P, HG, NQ]),
                                                ones[:, :].rearrange("p (g f) -> p g f", g=HG), ALU.mult).then_inc(sem("e_inv_tok"), 1)
            for g in range(GROUPS):
                pool_rstd(gp, "f", g, 2)
            for g in range(GROUPS):
                pool_v_in(gp, "f", g, oT, "f_vT")
            for g in range(GROUPS):
                pool_k_heads(gp, "f", g)
            for g in range(GROUPS):
                pool_inv_tok(gp, "f", g)
            for g in range(GROUPS):
                pool_rstd(gp, "f2", g, 1)
            for g in range(GROUPS):
                gp.wait_ge(sem("f_x2"), g + 1)
                nc.gpsimd.tensor_tensor(gx(x, g), gx(x, g), gx(res, g), ALU.add).then_inc(sem("f_x_res"), 1)
            for g in range(GROUPS):
                pool_rstd(gp, "g", g, 1)

        def dve_layer_norm(v, ph, g, src, twice=False):
            t0 = g * TPG
            for j in range(t0, t0 + TPG):
                i = nc.vector.bn_stats(stats[:, j, :], src[:, j, :])
            link(v, "v", i)
            for j in range(t0, t0 + TPG):
                i = nc.vector.bn_aggr(mean_var[:, j, :], stats[:, j, :])
            link(v, "v", i)
            var = mean_var[:, t0:t0 + TPG, 1:2].rearrange("p t a -> p (t a)")
            i = nc.vector.tensor_scalar(var_eps[:, 0, t0:t0 + TPG], var, EPS, None, ALU.add)
            if twice:
                i = nc.vector.tensor_scalar(var_eps[:, 1, t0:t0 + TPG], var, 1.0 + EPS, EPS * EPS, ALU.mult, ALU.add)
            i.then_inc(sem(ph + "_var"), 1)

        def dve_normalise(v, ph, g, src, twice=False):
            t0 = g * TPG
            v.wait_ge(*nth(ph + "_rstd", g + 1))
            for n, dst in (((0, res), (1, h)) if twice else ((0, h),)):
                for j in range(t0, t0 + TPG):
                    i = nc.vector.tensor_scalar(dst[:, j, :], src[:, j, :], mean_var[:, j, 0:1], rstd[:, n, j:j + 1],
                                                ALU.subtract, ALU.mult)
            i.then_inc(sem(ph + "_h"), 1)

        def pe_transpose_group(pe, g, src, k, ready):
            for s, n in ready:
                pe.wait_ge(*nth(s, n))
            for j in range(TPG):
                i = nc.tensor.transpose(group_bank(g, k)[:, j * P:(j + 1) * P], src[:, g * TPG + j, :], ident[:, :])
            return i

        def pe_self_attention(pe, ph, vw):
            for g in range(GROUPS):
                for j in range(TPG):
                    pe.wait_ge(*nth(ph + "_v_in", g * TPG + j + 1))
                    for b in range(BPT):
                        i = nc.tensor.matmul(group_bank(g, j)[:, b * P:(b + 1) * P], v_in(g)[:, j, b, :], vw, start=True, stop=True)
                    i.then_inc(sem(ph + "_v"), 1)
            for g in range(GROUPS):
                pe.wait_ge(*nth(ph + "_v_heads", TPG * (g + 1)))
                pe.wait_ge(*nth(ph + "_qT", g + 1))
                pe.wait_ge(*nth(ph + "_k_heads", TPG * (g + 1)))
                for j in range(TPG):
                    for b in range(BPT):
                        for a in range(HG):
                            at = g * GW + j * P + b * NQ
                            i = nc.tensor.matmul(group_bank(g, a)[b * NQ:(b + 1) * NQ, j * P:(j + 1) * P],
                                                 qT[a * NQ:(a + 1) * NQ, at:at + NQ],
                                                 k_heads(g)[a * NQ:(a + 1) * NQ, j, b, :],
                                                 start=True, stop=True, tile_position=(a * NQ, b * NQ))
                i.then_inc(sem(ph + "_scores"), 1)
            for g in range(GROUPS):
                pe.wait_ge(*nth(ph + "_exp", g + 1))
                for j in range(TPG):
                    for a in range(HG):
                        i = nc.tensor.transpose(group_bank(g, j)[:, a * P:(a + 1) * P], probs(g)[:, a, j, :], ident[:, :])
                    i.then_inc(sem(ph + "_pT"), 1)
            for g in range(GROUPS):
                for j in range(TPG):
                    pe.wait_ge(*nth(ph + "_probsT", g * TPG + TPG))
                    for b in range(BPT):
                        for a in range(HG):
                            at = j * P + b * NQ
                            i = nc.tensor.matmul(group_bank(g, 0)[a * NQ:(a + 1) * NQ, at:at + NQ],
                                                 v_heads(g)[:, j, b, a * NQ:(a + 1) * NQ],
                                                 probsT(g)[:, j, a, b * NQ:(b + 1) * NQ],
                                                 start=True, stop=True, tile_position=(0, a * NQ))
                pe.wait_ge(*nth(ph + "_inv_tok", g + 1))
                for j in range(TPG):
                    i = nc.tensor.transpose(group_bank(g, 1)[:, j * P:(j + 1) * P], h[:, g * TPG + j, :], ident[:, :])
                i.then_inc(sem(ph + "_out"), 1)

        def dve_self_attention(v, ph, causal_mask):
            for g in range(GROUPS):
                for j in range(TPG):
                    v.wait_ge(*nth(ph + "_v", g * TPG + j + 1))
                    nc.vector.tensor_tensor(v_heads(g)[:, j, :, :], group_bank(g, j)[:, :].rearrange("p (b n) -> p b n", b=BPT),
                                            v_mask[:, :, :, :].rearrange("p g h d -> p (g h d)").unsqueeze(1).broadcast_to([P, BPT, P]),
                                            ALU.mult).then_inc(sem(ph + "_v_heads"), 1)
            for g in range(GROUPS):
                v.wait_ge(*nth(ph + "_scores", g + 1))
                for a in range(HG):
                    s = group_bank(g, a)[:, :].rearrange("p (m k) -> p m k", k=NQ)
                    d = probs(g)[:, a, :, :].rearrange("p j n -> p (j n)").rearrange("p (m k) -> p m k", k=NQ)
                    if causal_mask:
                        link(v, "v", nc.vector.tensor_tensor(d, s, causal[:, :].unsqueeze(1).broadcast_to([P, TPG * HPG, NQ]), ALU.add))
                        s = d
                    link(v, "v", nc.vector.tensor_reduce(head_max[:, g, a, :], s, AX, ALU.max))
                    nc.vector.tensor_tensor(d, s, head_max[:, g, a, :].unsqueeze(2).broadcast_to([P, TPG * HPG, NQ]),
                                            ALU.subtract).then_inc(sem(ph + "_shifted"), 1)
            for g in range(GROUPS):
                v.wait_ge(*nth(ph + "_exp", g + 1))
                link(v, "v", nc.vector.tensor_reduce(head_sum[:, g, :, :], r3[:, g * 2048:(g + 1) * 2048].rearrange("p (m k) -> p m k", k=NQ), AX, ALU.add))
                nc.vector.reciprocal(head_inv[:, g, :, :], head_sum[:, g, :, :]).then_inc(sem(ph + "_inv"), 1)
            for g in range(GROUPS):
                v.wait_ge(*nth(ph + "_inv_rows", g + 1))
                nc.vector.tensor_tensor(oT[:, g * GW:(g + 1) * GW], group_bank(g, 0)[:, :], aT[:, g * GW:(g + 1) * GW],
                                        ALU.mult).then_inc(sem(ph + "_oT"), 1)

        def act_self_attention(a_, ph):
            for g in range(GROUPS):
                for a in range(HG):
                    a_.wait_ge(*nth(ph + "_shifted", g * HG + a + 1))
                    p = probs(g)[:, a, :, :]
                    i = nc.scalar.activation(p, p, ACT.Exp, scale=HD ** -0.5)
                i.then_inc(sem(ph + "_exp"), 1)
            for g in range(GROUPS):
                for j in range(TPG):
                    a_.wait_ge(*nth(ph + "_pT", g * TPG + j + 1))
                    nc.scalar.activation(probsT(g)[:, j, :, :], group_bank(g, j)[:, :].rearrange("p (a n) -> p a n", a=HG),
                                         ACT.Copy).then_inc(sem(ph + "_probsT"), 1)
            for g in range(GROUPS):
                a_.wait_ge(*nth(ph + "_out", g + 1))
                nc.scalar.activation(aT[:, g * GW:(g + 1) * GW], group_bank(g, 1)[:, :], ACT.Copy).then_inc(sem(ph + "_inv_rows"), 1)

        def dve_top2(v, ph):
            for t in range(TILES):
                i = nc.vector.max(out=top8[:, t, :], in_=logits[:, t, :])
            link(v, "v", i)
            for t in range(TILES):
                i = nc.vector.max_index(top_index[:, t, :], top8[:, t, :], logits[:, t, :])
            nc.vector.tensor_tensor(top_p[:, 0, :], top8[:, :, 1:2].rearrange("p t a -> p (t a)"), top8[:, :, 0:1].rearrange("p t a -> p (t a)"),
                                    ALU.subtract).then_inc(sem(ph + "_top_diff"), 1)
            v.wait_ge(*nth(ph + "_top_diff", 1))
            link(v, "v", nc.vector.tensor_copy(top_f[:, :, :], top_index[:, :, 0:2]))
            for k in range(2):
                i = nc.vector.tensor_tensor(pick[:, k, :, :], iota8[:, :].unsqueeze(1).broadcast_to([P, TILES, NE]),
                                            top_f[:, :, k:k + 1].broadcast_to([P, TILES, NE]), ALU.is_equal)
            if ph == "g":
                link(v, "v", i)
                nc.vector.tensor_tensor(picked[:, :, :], pick[:, 0, :, :], pick[:, 1, :, :], ALU.add).then_inc(sem("g_picked_before"), 1)
                for t in range(1, TILES):
                    v.wait_ge(sem("g_picked_before"), t)
                    nc.vector.tensor_tensor(picked_before[:, t, :], picked_before[:, t - 1, :], picked[:, t - 1, :], ALU.add).then_inc(sem("g_picked_before"), 1)
            v.wait_ge(*nth(ph + "_top_exp", 1))
            link(v, "v", nc.vector.tensor_scalar(top_p[:, 2, :], top_p[:, 1, :], 1.0, None, ALU.add))
            link(v, "v", nc.vector.reciprocal(top_p[:, 0, :], top_p[:, 2, :]))
            link(v, "v", nc.vector.tensor_tensor(top_p[:, 1, :], top_p[:, 1, :], top_p[:, 0, :], ALU.mult))
            for k in range(2):
                i = nc.vector.tensor_tensor(pick[:, k, :, :], pick[:, k, :, :], top_p[:, k, :].unsqueeze(2).broadcast_to([P, TILES, NE]), ALU.mult)
            link(v, "v", i)

        def dve_accumulate(v, ph, banks):
            with v.Fori(0, NE) as e:
                for g in range(GROUPS):
                    v.wait_ge(*nth(ph + "_down", 2 * e + (g + 1)))
                    v.wait_ge(*nth(ph + "_acc", 2 * e + (g + 1)))
                    for j in range(TPG):
                        t = g * TPG + j
                        i = nc.vector.scalar_tensor_tensor(moe[:, t, :], banks[4 + g][:, j * P:(j + 1) * P],
                                                           w_token[:, :, :].rearrange("p e t -> p (e t)")[:, bass.ds(e * TILES + t, 1)],
                                                           moe[:, t, :], ALU.mult, ALU.add)
                    i.then_inc(sem(ph + "_acc"), 1)

        @block.tensor
        def _(pe):
            pe.wait_ge(sem("constants"), 1)
            pe.wait_ge(sem("w_a_loaded"), 16 * 4)
            for i_ in range(4):
                i = nc.tensor.transpose(bank[0][:, i_ * P:(i_ + 1) * P], w_a[:, i_, :], ident[:, :])
            i.then_inc(sem("b_wT_p"), 1)
            for g in range(GROUPS):
                pe_transpose_group(pe, g, h, 1, [("b_h", g + 1)]).then_inc(sem("b_hT_p"), 1)
            for g in range(GROUPS):
                pe.wait_ge(*nth("b_wT", 1))
                pe.wait_ge(*nth("b_hT", g + 1))
                nc.tensor.matmul(group_bank(g, 2)[:, :], w_aT[:, 0, :], gx(hT, g), start=True, stop=True).then_inc(sem("b_q_p"), 1)
            pe.wait_ge(sem("b_w_loaded"), 16 * 5)
            for g in range(GROUPS):
                pe.wait_ge(*nth("b_qT", g + 1))
                for j in range(TPG):
                    t = g * TPG + j
                    i = nc.tensor.matmul(group_bank(g, 3)[:, j:j + 1], qT[:, t * P:(t + 1) * P], cols[:, BK0:BK0 + 1], start=True, stop=True)
                i.then_inc(sem("b_qbk_p"), 1)
                nc.tensor.matmul(group_bank(g, 1)[:, :], wk0[:, :], gx(qT, g), start=True, stop=True).then_inc(sem("b_q2_p"), 1)
            pe.wait_ge(sem("b_q2"), GROUPS)
            pe.wait_ge(sem("b_qbk"), GROUPS)
            pe.wait_ge(sem("ctx_last_loaded"), 16)
            nc.tensor.transpose(bank[7][:, 0:NB], ctx_last[:, :], ident[0:NB, 0:NB]).then_inc(sem("ctx_last_p"), 1)
            pe.wait_ge(sem("gen_loaded"), 16)
            for i_ in range(3):
                i = nc.tensor.transpose(bank[4][:, i_ * P:(i_ + 1) * P], gen[:, i_, :], ident[:, :])
            i.then_inc(sem("m_wT_p"), 1)
            pe.wait_ge(*nth("m_wT", 1))

            def pe_expm_step(n):
                if n < ORDER - 1:
                    pe.wait_ge(sem("taylor"), n + 1)
                    for i_ in range(3):
                        i = nc.tensor.matmul(bank[4][:, i_ * P:(i_ + 1) * P], genT[:, i_, :], taylor[:, i_, :], start=True, stop=True)
                    i.then_inc(sem("taylor_p"), 1)
                elif n == ORDER - 1:
                    pe.wait_ge(sem("taylor"), n + 1)
                    for i_ in range(3):
                        i = nc.tensor.transpose(bank[5][:, i_ * P:(i_ + 1) * P], taylor[:, i_, :], ident[:, :])
                    i.then_inc(sem("taylorT_p"), 1)
                elif n < ORDER + SQUARINGS:
                    pe.wait_ge(sem("taylor"), n)
                    pe.wait_ge(sem("taylorT"), n - ORDER + 1)
                    for i_ in range(3):
                        i = nc.tensor.matmul(bank[4][:, i_ * P:(i_ + 1) * P], taylorT[:, i_, :], taylor[:, i_, :], start=True, stop=True)
                    i.then_inc(sem("taylor_p"), 1)
                    for i_ in range(3):
                        i = nc.tensor.matmul(bank[5][:, i_ * P:(i_ + 1) * P], taylor[:, i_, :], taylorT[:, i_, :], start=True, stop=True)
                    i.then_inc(sem("taylorT_p"), 1)
                elif n == ORDER + SQUARINGS:
                    pe.wait_ge(sem("taylor"), ORDER + SQUARINGS)
                    pe.wait_ge(sem("taylorT"), SQUARINGS + 1)
                    nc.tensor.matmul(bank[4][:, 0:P], taylorT[:, 1, :], taylor[:, 2, :], start=True, stop=True).then_inc(sem("taylor_p"), 1)
                elif n == ORDER + SQUARINGS + 1:
                    pe.wait_ge(sem("pair"), 1)
                    nc.tensor.matmul(bank[4][:, 0:P], taylorT[:, 0, :], pair[:, :], start=True, stop=True).then_inc(sem("taylor_p"), 1)

            for n in range(NB // 2):
                pe_expm_step(n)
                pe.wait_ge(sem(f"ctx_loaded{2 * n // 8}"), 16 * KC)
                if n >= 4:
                    pe.wait_ge(sem("ctxT_a" if n % 2 == 0 else "ctxT_v"), (n - 4) // 2 + 1 + n % 2)
                for b in range(2):
                    for c in range(KC):
                        i = nc.tensor.transpose(bank[n % 4][:, (b * KC + c) * P:(b * KC + c + 1) * P], ctx_keys[:, 2 * n + b, c, :], ident[:, :])
                i.then_inc(sem("ctxT_p"), 1)
            pe.wait_ge(sem("rot"), 1)
            pe.wait_ge(sem("ctxT_a"), NB // 4)
            pe.wait_ge(sem("ctxT_v"), NB // 4 + 1)
            for g in range(GROUPS):
                for j in range(TPG):
                    t = g * TPG + j
                    for b in range(BPT):
                        i = nc.tensor.matmul(group_bank(g, j)[b * NQ:(b + 1) * NQ, 0:NK], kT[:, t * P + b * NQ:t * P + (b + 1) * NQ],
                                             ctxT[:, BPT * t + b, :], start=True, stop=True, tile_position=(0, b * NQ))
                    i.then_inc(sem("b_scores"), 1)
            for t in range(TILES):
                pe.wait_ge(*nth("b_exp", t + 1))
                for c in range(KC):
                    nc.tensor.transpose(bank[t][:, c * P:(c + 1) * P], b_probs(t)[:, c * P:(c + 1) * P], ident[:, :])
                pe.wait_ge(sem("b_last"), t + 1)
                nc.tensor.transpose(bank[t][0:NB, KC * P:KC * P + P], b_last[:, t, :], ident[:, :]).then_inc(sem("b_pT"), 1)
            for t in range(TILES):
                pe.wait_ge(*nth("b_probsT", t + 1))
                nc.tensor.matmul(bank[t][:, 0:D], b_lastT[:, t, :], ctx_last[:, :], start=True, stop=False)
                for c in range(KC):
                    for b in range(BPT):
                        i = nc.tensor.matmul(bank[t][b * NQ:(b + 1) * NQ, 0:D], b_probsT(t)[:, c * P + b * NQ:c * P + (b + 1) * NQ],
                                             ctx_keys[:, BPT * t + b, c, :], start=False, stop=c == KC - 1,
                                             tile_position=(0, b * NQ))
                i.then_inc(sem("b_av"), 1)
            for g in range(GROUPS):
                pe_transpose_group(pe, g, h, 1, [("b_o", TPG * (g + 1))]).then_inc(sem("b_oT_p"), 1)
            for g in range(GROUPS):
                pe.wait_ge(*nth("b_oT", g + 1))
                nc.tensor.matmul(group_bank(g, 2)[:, :], w_aT[:, 1, :], gx(oT, g), start=True, stop=True).then_inc(sem("b_vo_p"), 1)
            for g in range(GROUPS):
                pe.wait_ge(sem("b_voT"), g + 1)
                for j in range(TPG):
                    t = g * TPG + j
                    i = nc.tensor.matmul(group_bank(g, 3)[:, j * P:(j + 1) * P], aT[:, t * P:(t + 1) * P], w_aT[:, 2, :], start=True, stop=True)
                i.then_inc(sem("b_out"), 1)

            pe.wait_ge(sem("c_w_loaded"), 16 * 6)
            for g in range(GROUPS):
                pe_transpose_group(pe, g, h, 0, [("c_h", g + 1)]).then_inc(sem("c_hT_p"), 1)
            for g in range(GROUPS):
                pe.wait_ge(*nth("c_hT", g + 1))
                nc.tensor.matmul(group_bank(g, 1)[:, :], w_qkv[:, D:2 * D], gx(hT, g), start=True, stop=True).then_inc(sem("c_k_p"), 1)
                nc.tensor.matmul(group_bank(g, 2)[:, :], w_qkv[:, 0:D], gx(hT, g), start=True, stop=True).then_inc(sem("c_q_p"), 1)
            for g in range(GROUPS):
                pe.wait_ge(*nth("c_qT", g + 1))
            pe_self_attention(pe, "c", w_qkv[:, 2 * D:3 * D])
            for g in range(GROUPS):
                pe.wait_ge(*nth("c_obT", g + 1))
                for j in range(TPG):
                    t = g * TPG + j
                    i = nc.tensor.matmul(group_bank(g, 2)[:, j * P:(j + 1) * P], oT[:, t * P:(t + 1) * P], w_proj[:, :], start=True, stop=True)
                i.then_inc(sem("c_projected"), 1)

            pe.wait_ge(sem("d_w_loaded"), 160)
            for g in range(GROUPS):
                pe_transpose_group(pe, g, h, 0, [("d_h", g + 1)]).then_inc(sem("d_hT_p"), 1)
            nc.tensor.transpose(group_bank(1, 1)[:, 0:4 * NE], b1_rows[:, :], ident[0:4 * NE, 0:4 * NE]).then_inc(sem("d_wT_p"), 1)
            for g in range(GROUPS):
                pe.wait_ge(*nth("d_hT", g + 1))
                for j in range(TPG):
                    t = g * TPG + j
                    i = nc.tensor.matmul(group_bank(0, 2)[:, t * NE:(t + 1) * NE], hT[:, t * P:(t + 1) * P], gate_w[:, :], start=True, stop=True)
            i.then_inc(sem("d_logits"), 1)
            for g in range(GROUPS):
                pe.wait_ge(*nth("d_wT", 1))
                for j in range(TPG):
                    t = g * TPG + j
                    i = nc.tensor.matmul(group_bank(g, 1)[:, j * P:(j + 1) * P], hT[:, t * P:(t + 1) * P], abel_w[:, :], start=True, stop=True)
                i.then_inc(sem("d_abel_p"), 1)
            pe.wait_ge(sem("d_w_token"), 1)
            for g in range(GROUPS):
                for j in range(TPG):
                    t = g * TPG + j
                    i = nc.tensor.transpose(group_bank(g, 3)[0:NE, j * P:(j + 1) * P], w_token[:, :, t], ident[:, :])
                i.then_inc(sem("d_w_tokenT_p"), 1)
            for g in range(GROUPS):
                pe.wait_ge(sem("d_w_tokenT"), g + 1)
                for j in range(TPG):
                    t = g * TPG + j
                    i = nc.tensor.matmul(group_bank(g, 2)[:, j * P:(j + 1) * P], w_tokenT[:, t * P:(t + 1) * P], b2_rows[:, :], start=True, stop=True)
                i.then_inc(sem("d_moe_b2"), 1)
            pe.wait_ge(sem("d_abel_s"), GROUPS)
            pe.wait_ge(*nth("d_acc", GROUPS))

            def up(e, slot, first):
                pe.wait_ge(*nth(f"d_w1_loaded{slot}", 8 * (e - slot) + 16))
                for n in range(8):
                    if not (first and n < 4):
                        pe.wait_ge(sem("d_gelu"), 8 * e + (n - 3))
                    c, g = n // GROUPS, n % GROUPS
                    nc.tensor.matmul(bank[n % 4][:, :], w1[:, slot, c * P:(c + 1) * P], gx(hT, g), start=True, stop=True).then_inc(sem("d_up"), 1)

            def down(e, slot):
                pe.wait_ge(*nth(f"d_w2_loaded{slot}", 8 * (e - slot) + 16))
                pe.wait_ge(sem("d_gelu"), 8 * e + 8)
                for g in range(GROUPS):
                    pe.wait_ge(*nth("d_acc", 2 * e + g + 1))
                    for j in range(TPG):
                        t = g * TPG + j
                        for c in range(4):
                            i = nc.tensor.matmul(bank[4 + g][:, j * P:(j + 1) * P], hidden(slot)[:, c, t * P:(t + 1) * P], w2[:, slot, c, :],
                                                 start=c == 0, stop=c == 3)
                    i.then_inc(sem("d_down"), 1)

            up(0, 0, True)
            up(1, 1, False)
            down(0, 0)
            with pe.Fori(1, NE // 2) as pair_of_experts:
                e = 2 * pair_of_experts
                up(e, 0, False)
                down(e - 1, 1)
                up(e + 1, 1, False)
                down(e, 0)
            down(NE - 1, 1)
            for g in range(GROUPS):
                pe_transpose_group(pe, g, moe, 3, [("d_acc", 2 * NE + g + 1)]).then_inc(sem("d_moeT_p"), 1)
            for g in range(GROUPS):
                pe.wait_ge(sem("d_moeT"), g + 1)
                for j in range(TPG):
                    t = g * TPG + j
                    i = nc.tensor.matmul(group_bank(g, 2)[:, j * P:(j + 1) * P], moeT[:, t * P:(t + 1) * P], rot[:, :], start=True, stop=True)
                i.then_inc(sem("d_nonabel"), 1)

            pe.wait_ge(sem("e_w_loaded"), 16 * 8)
            for g in range(GROUPS):
                pe_transpose_group(pe, g, h, 0, [("e_h", g + 1)]).then_inc(sem("e_hT_p"), 1)
            for g in range(GROUPS):
                pe.wait_ge(*nth("e_hT", g + 1))
                nc.tensor.matmul(group_bank(g, 1)[:, :], w_e[:, 0, :], gx(hT, g), start=True, stop=True).then_inc(sem("e_q_p"), 1)
            pe.wait_ge(*nth("e_qT", GROUPS))

            def keys_values(t, slot):
                for b in range(BPT):
                    nc.tensor.matmul(bank[b][:, 0:NK], w_e[:, 1, :], ctxT[:, bass.ds(BPT * t + b, 1), :].rearrange("p a k -> p (a k)"),
                                     start=True, stop=True).then_inc(sem("e_k_p"), 1)
                pe.wait_ge(sem("e_prep"), t + 1)
                for b in range(BPT):
                    for c in range(KC):
                        i = nc.tensor.matmul(bank[5 + b // 2][:, ((b % 2) * KC + c) * D:((b % 2) * KC + c + 1) * D],
                                             e_ctx[slot][:, b, c * P:(c + 1) * P], w_e[:, 2, :], start=True, stop=True)
                    if b % 2:
                        i.then_inc(sem("e_v_p"), 1)
                pe.wait_ge(sem("e_done"), t + 2)
                nc.tensor.matmul(bank[4][0:BPT * HG, 0:D], e_last_in[:, slot, :], w_e[:, 2, :], start=True, stop=True).then_inc(sem("e_v_last_p"), 1)

            def scores(t, slot, b):
                if b == 0:
                    pe.wait_ge(sem("e_k"), BPT * t + BPT)
                else:
                    pe.wait_ge(sem("e_masked"), BPT * t + b)
                for g in range(HG):
                    i = nc.tensor.matmul(bank[g][:, 0:NK], e_q[slot][g * NQ:(g + 1) * NQ, b, :, :].rearrange("p h q -> p (h q)"),
                                         e_k[slot][g * NQ:(g + 1) * NQ, b, :], start=True, stop=True, tile_position=(g * NQ, 0))
                i.then_inc(sem("e_scores"), 1)

            def transpose_probs(t, slot, b):
                pe.wait_ge(*nth("e_exp", BPT * t + (b + 1)))
                if b == 0:
                    pe.wait_ge(*nth("e_v", 2 * t + 2))
                    pe.wait_ge(sem("e_v_last"), t + 1)
                else:
                    pe.wait_ge(sem("e_pT_a"), BPT * t + b)
                    pe.wait_ge(sem("e_pT_v"), BPT * t + b)
                for c in range(KC):
                    for g in range(HG):
                        i = nc.tensor.transpose(bank[5 + c][:, g * P:(g + 1) * P], e_probs[b][:, g, c * P:(c + 1) * P], ident[:, :])
                    i.then_inc(sem(f"e_pT{c}"), 1)
                pe.wait_ge(sem("e_p_last"), BPT * t + (b + 1))
                nc.tensor.transpose(bank[4][0:BPT * HG, P:2 * P], e_p_last[:, b, :], ident[:, :]).then_inc(sem("e_p_last_p"), 1)

            def outputs(t, slot, b):
                pe.wait_ge(sem("e_p_lastT"), BPT * t + (b + 1))
                pe.wait_ge(sem("e_pT_a"), BPT * t + (b + 1))
                pe.wait_ge(sem("e_pT_v"), BPT * t + (b + 1))
                nc.tensor.matmul(bank[7][:, b * P:(b + 1) * P], e_v_last[:, slot, :], e_p_lastT[:, b % 2, :], start=True, stop=False)
                for c in range(KC):
                    for g in range(HG):
                        i = nc.tensor.matmul(bank[7][g * NQ:(g + 1) * NQ, b * P:(b + 1) * P], e_v[slot][:, b, c, g * NQ:(g + 1) * NQ],
                                             e_probsT[b % 2][:, c, g, :], start=False, stop=c == KC - 1, tile_position=(0, g * NQ))
                i.then_inc(sem("e_out"), 1)

            with pe.Fori(0, TILES // 2) as pair_of_tiles:
                for slot in range(2):
                    t = 2 * pair_of_tiles + slot
                    keys_values(t, slot)
                    scores(t, slot, 0)
                    for b in range(1, BPT):
                        scores(t, slot, b)
                        transpose_probs(t, slot, b - 1)
                        outputs(t, slot, b - 1)
                    transpose_probs(t, slot, BPT - 1)
                    outputs(t, slot, BPT - 1)
                    pe.wait_ge(*nth("e_inv_tok", BPT * t + BPT))
                    for b in range(BPT):
                        i = nc.tensor.transpose(bank[4][:, b * P:(b + 1) * P], e_inv_tok[:, slot, b, :], ident[:, :])
                    i.then_inc(sem("e_inv_p"), 1)
            for g in range(GROUPS):
                pe.wait_ge(*nth("e_obT", g + 1))
                for j in range(TPG):
                    t = g * TPG + j
                    i = nc.tensor.matmul(group_bank(g, 0)[:, j * P:(j + 1) * P], oT[:, t * P:(t + 1) * P], w_e[:, 3, :], start=True, stop=True)
                i.then_inc(sem("e_projected"), 1)

            pe.wait_ge(sem("f_w_loaded"), 16 * 9)
            for i_ in range(3):
                i = nc.tensor.transpose(bank[2][:, i_ * P:(i_ + 1) * P], w_b[:, i_, :], ident[:, :])
            i.then_inc(sem("f_wT_p"), 1)
            for i_ in range(4):
                i = nc.tensor.transpose(bank[3][:, i_ * P:(i_ + 1) * P], f_k[:, i_, :], ident[:, :])
            i.then_inc(sem("f_wT_p"), 1)
            for g in range(GROUPS):
                pe_transpose_group(pe, g, h, 1, [("f_h", g + 1)]).then_inc(sem("f_hT_p"), 1)
            pe.wait_ge(*nth("f_wT", 2))
            for g in range(GROUPS):
                pe.wait_ge(*nth("f_hT", g + 1))
                for j in range(TPG):
                    t = g * TPG + j
                    nc.tensor.matmul(group_bank(g, j)[:, 0:3 * D], hT[:, t * P:(t + 1) * P], w_bT[:, 0:3, :].rearrange("p i n -> p (i n)"),
                                     start=True, stop=True).then_inc(sem("f_scores3"), 1)
            for g in range(GROUPS):
                pe.wait_ge(sem("f_patterns"), g + 1)
                for k in range(3):
                    for j in range(TPG):
                        i = nc.tensor.transpose(group_bank(g, k)[:, j * P:(j + 1) * P], patterns(g)[:, j, k, :], ident[:, :])
                    i.then_inc(sem("f_patterns_T"), 1)
            for g in range(GROUPS):
                pe.wait_ge(sem("f_aqT"), g + 1)
                nc.tensor.matmul(group_bank(g, 3)[:, :], w_v[:, 0, :], gx(hT, g), start=True, stop=True).then_inc(sem("f_q_p"), 1)
                pe.wait_ge(sem("f_akT"), g + 1)
                nc.tensor.matmul(group_bank(g, 0)[:, :], w_v[:, 1, :], gx(aT, g), start=True, stop=True).then_inc(sem("f_k_p"), 1)
            for g in range(GROUPS):
                pe.wait_ge(*nth("f_qT", g + 1))
                pe.wait_ge(*nth("f_kT", g + 1))
            pe_self_attention(pe, "f", w_v[:, 2, :])
            for g in range(GROUPS):
                pe.wait_ge(*nth("f_oT", g + 1))
                for j in range(TPG):
                    t = g * TPG + j
                    i = nc.tensor.matmul(group_bank(g, 2)[:, j * P:(j + 1) * P], oT[:, t * P:(t + 1) * P], w_aT[:, 3, :], start=True, stop=True)
                i.then_inc(sem("f_p_scores"), 1)
            for g in range(GROUPS):
                pe.wait_ge(sem("f_p_exp"), g + 1)
                for j in range(TPG):
                    i = nc.tensor.transpose(group_bank(g, 3)[:, j * P:(j + 1) * P], p_probs(g)[:, j, :], ident[:, :])
                i.then_inc(sem("f_pp_T_p"), 1)
            for g in range(GROUPS):
                pe.wait_ge(sem("f_ppT"), g + 1)
                for j in range(TPG):
                    t = g * TPG + j
                    i = nc.tensor.matmul(group_bank(g, 0)[:, j * P:(j + 1) * P], aT[:, t * P:(t + 1) * P], w_v[:, 3, :], start=True, stop=True)
                i.then_inc(sem("f_p_out"), 1)
            for g in range(GROUPS):
                pe_transpose_group(pe, g, h, 1, [("f2_h", g + 1)]).then_inc(sem("f2_hT_p"), 1)
            for g in range(GROUPS):
                pe.wait_ge(*nth("f2_hT", g + 1))
                for j in range(TPG):
                    t = g * TPG + j
                    nc.tensor.matmul(group_bank(g, j)[:, :], hT[:, t * P:(t + 1) * P], f_kT, start=True, stop=True).then_inc(sem("f_f_scores"), 1)
            for g in range(GROUPS):
                for j in range(TPG):
                    pe.wait_ge(sem("f_f_exp"), g * TPG + j + 1)
                    for c in range(4):
                        i = nc.tensor.transpose(group_bank(g, j)[:, c * P:(c + 1) * P], f_probs(g)[:, j, c, :], ident[:, :])
                    i.then_inc(sem("f_f_T"), 1)
            for g in range(GROUPS):
                pe.wait_ge(sem("f_fT"), TPG * (g + 1))
                for j in range(TPG):
                    for c in range(4):
                        i = nc.tensor.matmul(group_bank(g, 0)[:, j * P:(j + 1) * P], probsT(g)[:, j, c, :], f_v[:, c, :], start=c == 0, stop=c == 3)
                i.then_inc(sem("f_f_out"), 1)

            pe.wait_ge(sem("g_w_loaded"), 32)
            nc.tensor.transpose(bank[2][:, 0:NE], router_rows[:, :], ident[0:NE, 0:NE]).then_inc(sem("g_wT_p"), 1)
            for g in range(GROUPS):
                pe_transpose_group(pe, g, h, 1, [("g_h", g + 1)]).then_inc(sem("g_hT_p"), 1)
            pe.wait_ge(*nth("g_wT", 1))
            for g in range(GROUPS):
                pe.wait_ge(*nth("g_hT", g + 1))
                for j in range(TPG):
                    t = g * TPG + j
                    i = nc.tensor.matmul(bank[2][:, t * NE:(t + 1) * NE], hT[:, t * P:(t + 1) * P], routerT[:, :], start=True, stop=True)
            i.then_inc(sem("g_logits"), 1)
            pe.wait_ge(sem("g_before"), 1)
            pe.wait_ge(sem("g_picked_before"), TILES)
            nc.tensor.matmul(bank[6][:, 0:TILES * NE], before[:, :], picked[:, :, :].rearrange("p t e -> p (t e)"), start=True, stop=False)
            nc.tensor.matmul(bank[6][:, 0:TILES * NE], ones[:, :], picked_before[:, :, :].rearrange("p t e -> p (t e)"),
                             start=False, stop=True).then_inc(sem("g_rank"), 1)

            def gated_up(e, slot, first):
                pe.wait_ge(*nth(f"g_w1_loaded{slot}", 16 * (e - slot) + 32))
                for n in range(4):
                    if not (first and n < 2):
                        pe.wait_ge(sem("g_hidden"), 4 * e + (n - 1))
                    c, g = n // GROUPS, n % GROUPS
                    for i_ in range(2):
                        i = nc.tensor.matmul(bank[2 * (n % 2) + i_][:, :], w1[:, slot, i_ * DH + c * P:i_ * DH + (c + 1) * P], gx(hT, g), start=True, stop=True)
                    i.then_inc(sem("g_up"), 1)

            def gated_down(e, slot):
                pe.wait_ge(*nth(f"g_w2_loaded{slot}", 8 * (e - slot) + 16))
                pe.wait_ge(sem("g_hidden"), 4 * e + 4)
                for g in range(GROUPS):
                    pe.wait_ge(*nth("g_acc", 2 * e + (g + 1)))
                    for j in range(TPG):
                        t = g * TPG + j
                        for c in range(2):
                            i = nc.tensor.matmul(bank[4 + g][:, j * P:(j + 1) * P], hidden(slot)[:, c, t * P:(t + 1) * P], w2[:, slot, c, :],
                                                 start=c == 0, stop=c == 1)
                    i.then_inc(sem("g_down"), 1)

            gated_up(0, 0, True)
            gated_up(1, 1, False)
            gated_down(0, 0)
            with pe.Fori(1, NE // 2) as pair_of_experts:
                e = 2 * pair_of_experts
                gated_up(e, 0, False)
                gated_down(e - 1, 1)
                gated_up(e + 1, 1, False)
                gated_down(e, 0)
            gated_down(NE - 1, 1)

        @block.scalar
        def _(a_):
            def out_of_bank(dst, src, wait, done, bias=None, scale=None):
                a_.wait_ge(*nth(wait[0], wait[1]))
                if bias is None and scale is None:
                    i = nc.scalar.activation(dst, src, ACT.Copy)
                else:
                    i = nc.scalar.activation(dst, src, ACT.Identity, bias=bias if bias is not None else 0.0,
                                             scale=scale if scale is not None else 1.0)
                i.then_inc(sem(done), 1)

            out_of_bank(w_aT[:, :, :], bank[0][:, :].rearrange("p (i n) -> p i n", i=4), ("b_wT_p", 1), "b_wT")
            for g in range(GROUPS):
                out_of_bank(gx(hT, g), group_bank(g, 1)[:, :], ("b_hT_p", g + 1), "b_hT")
            a_.wait_ge(sem("b_w_loaded"), 16 * 5)
            for g in range(GROUPS):
                out_of_bank(gx(qT, g), group_bank(g, 2)[:, :], ("b_q_p", g + 1), "b_qT", bias=cols[:, BQ0:BQ0 + 1])
            for g in range(GROUPS):
                out_of_bank(gx(kT, g), group_bank(g, 1)[:, :], ("b_q2_p", g + 1), "b_q2")
            out_of_bank(genT[:, :, :], bank[4][:, 0:3 * P].rearrange("p (i n) -> p i n", i=3), ("m_wT_p", 1), "m_wT")
            for n in range(0, NB // 2, 2):
                if n >= ORDER:
                    for m in (n - 1, n):
                        if m - ORDER + 1 <= SQUARINGS:
                            out_of_bank(taylorT[:, :, :], bank[5][:, 0:3 * P].rearrange("p (i n) -> p i n", i=3), ("taylorT_p", m - ORDER + 2), "taylorT")
                out_of_bank(ctxT[:, 2 * n:2 * n + 2, 0:LAST], bank[n % 4][:, :].rearrange("p (b k) -> p b k", b=2), ("ctxT_p", n + 1), "ctxT_a")
            for t in range(TILES):
                a_.wait_ge(sem("b_max"), t + 1)
                nc.scalar.activation(b_probs(t), b_probs(t), ACT.Exp, bias=row_max[:, TILES + t:TILES + t + 1], scale=D ** -0.5,
                                     accum_out=row_sum[:, t:t + 1]).then_inc(sem("b_exp"), 1)
            for t in range(TILES):
                a_.wait_ge(sem("b_lastT"), t + 1)
                out_of_bank(b_probsT(t), bank[t][:, 0:LAST], ("b_pT", t + 1), "b_probsT")
            for t in range(TILES):
                a_.wait_ge(*nth("b_inv", t + 1))
                out_of_bank(h[:, t, :], bank[t][:, 0:D], ("b_av", t + 1), "b_o", scale=row_inv[:, t:t + 1])
            for g in range(GROUPS):
                out_of_bank(gx(oT, g), group_bank(g, 1)[:, :], ("b_oT_p", g + 1), "b_oT")
            for g in range(GROUPS):
                out_of_bank(gx(aT, g), group_bank(g, 2)[:, :], ("b_vo_p", g + 1), "b_voT", bias=cols[:, BV0:BV0 + 1])

            a_.wait_ge(sem("c_w_loaded"), 16 * 6)
            for g in range(GROUPS):
                out_of_bank(gx(hT, g), group_bank(g, 0)[:, :], ("c_hT_p", g + 1), "c_hT")
            for g in range(GROUPS):
                out_of_bank(gx(kT, g), group_bank(g, 1)[:, :], ("c_k_p", g + 1), "c_kT", bias=cols[:, BK:BK + 1])
                out_of_bank(gx(qT, g), group_bank(g, 2)[:, :], ("c_q_p", g + 1), "c_qT", bias=cols[:, BQ:BQ + 1])
            act_self_attention(a_, "c")
            for g in range(GROUPS):
                a_.wait_ge(*nth("c_oT", g + 1))
                nc.scalar.activation(gx(oT, g), gx(oT, g), ACT.Identity, bias=cols[:, BV:BV + 1]).then_inc(sem("c_obT"), 1)

            a_.wait_ge(sem("d_w_loaded"), 160)
            for g in range(GROUPS):
                out_of_bank(gx(hT, g), group_bank(g, 0)[:, :], ("d_hT_p", g + 1), "d_hT", bias=cols[:, LN_B:LN_B + 1], scale=cols[:, LN_G:LN_G + 1])
            out_of_bank(b1_cols[:, :], group_bank(1, 1)[:, 0:4 * NE], ("d_wT_p", 1), "d_wT")
            a_.wait_ge(*nth("d_top_diff", 1))
            nc.scalar.activation(top_p[:, 1, :], top_p[:, 0, :], ACT.Exp).then_inc(sem("d_top_exp"), 1)
            for g in range(GROUPS):
                out_of_bank(w_tokenT[:, g * GW:(g + 1) * GW], group_bank(g, 3)[0:NE, :], ("d_w_tokenT_p", g + 1), "d_w_tokenT")
            for g in range(GROUPS):
                a_.wait_ge(sem("d_abel_s"), g + 1)
                nc.scalar.activation(gx(abel, g), gx(abel, g), ACT.Gelu).then_inc(sem("d_abel"), 1)

            def gelu(e, slot):
                nc.scalar.activation(b1_now[:, slot, :], b1_cols[:, bass.ds(4 * e, 4)], ACT.Copy).then_inc(sem("b1_now"), 1)
                a_.wait_ge(sem("b1_now"), e + 1)
                for n in range(8):
                    c, g = n // GROUPS, n % GROUPS
                    a_.wait_ge(*nth("d_up", 8 * e + (n + 1)))
                    nc.scalar.activation(hidden(slot)[:, c, g * GW:(g + 1) * GW], bank[n % 4][:, :], ACT.Gelu,
                                         bias=b1_now[:, slot, c:c + 1]).then_inc(sem("d_gelu"), 1)

            a_.wait_ge(*nth("d_wT", 1))
            with a_.Fori(0, NE // 2) as pair_of_experts:
                e = 2 * pair_of_experts
                gelu(e, 0)
                gelu(e + 1, 1)
            for g in range(GROUPS):
                out_of_bank(gx(moeT, g), group_bank(g, 3)[:, :], ("d_moeT_p", g + 1), "d_moeT")
            a_.wait_ge(sem("d_mix_z"), 1)
            nc.scalar.activation(mix_g[:, :], mix_z[:, 2, :], ACT.Sigmoid, bias=mix_b[:, 0:1]).then_inc(sem("d_mix_g"), 1)

            for g in range(GROUPS):
                out_of_bank(gx(hT, g), group_bank(g, 0)[:, :], ("e_hT_p", g + 1), "e_hT")
            for g in range(GROUPS):
                out_of_bank(gx(qT, g), group_bank(g, 1)[:, :], ("e_q_p", g + 1), "e_qT", bias=cols[:, BQ1:BQ1 + 1])

            def exps(t, slot, b):
                a_.wait_ge(sem("e_masked"), BPT * t + (b + 1))
                for g in range(HG):
                    n = b * HG + g
                    i = nc.scalar.activation(e_probs[b][:, g, :], e_probs[b][:, g, :], ACT.Exp, bias=e_nmax[:, n:n + 1], scale=HD ** -0.5,
                                             accum_out=e_sum[:, n:n + 1])
                i.then_inc(sem("e_exp"), 1)

            def probs_out(t, slot, b):
                a_.wait_ge(sem("e_pT0"), BPT * t + (b + 1))
                nc.scalar.activation(e_probsT[b % 2][:, 0, :, :], bank[5][:, :].rearrange("p (g n) -> p g n", g=HG), ACT.Copy).then_inc(sem("e_pT_a"), 1)

            with a_.Fori(0, TILES // 2) as pair_of_tiles:
                for slot in range(2):
                    t = 2 * pair_of_tiles + slot
                    for k in range(2):
                        a_.wait_ge(sem("e_v_p"), 2 * t + (k + 1))
                        nc.scalar.activation(e_v[slot][:, 2 * k:2 * k + 2, :, :], bank[5 + k][:, :].rearrange("p (b c d) -> p b c d", b=2, c=KC),
                                             ACT.Copy).then_inc(sem("e_v"), 1)
                    exps(t, slot, 0)
                    for b in range(1, BPT):
                        exps(t, slot, b)
                        probs_out(t, slot, b - 1)
                    probs_out(t, slot, BPT - 1)
            for g in range(GROUPS):
                a_.wait_ge(sem("e_done"), 2 + TPG * (g + 1))
                nc.scalar.activation(gx(oT, g), gx(oT, g), ACT.Identity, bias=cols[:, BV1:BV1 + 1]).then_inc(sem("e_obT"), 1)

            out_of_bank(w_bT[:, 0:3, :], bank[2][:, 0:3 * P].rearrange("p (i n) -> p i n", i=3), ("f_wT_p", 1), "f_wT")
            out_of_bank(f_kT, bank[3][:, :], ("f_wT_p", 2), "f_wT")
            for g in range(GROUPS):
                out_of_bank(gx(hT, g), group_bank(g, 1)[:, :], ("f_hT_p", g + 1), "f_hT")
            for g in range(GROUPS):
                a_.wait_ge(sem("f_max3"), g + 1)
                for j in range(TPG):
                    t = g * TPG + j
                    for k in range(3):
                        i = nc.scalar.activation(patterns(g)[:, j, k, :], group_bank(g, j)[:, k * D:(k + 1) * D], ACT.Exp,
                                                 bias=f_nmax[:, k, t:t + 1], scale=D ** -0.5, accum_out=f_sum[:, k, t:t + 1])
                i.then_inc(sem("f_exp3"), 1)
            for g in range(GROUPS):
                for k, (dst, name) in enumerate(((hT, "f_aqT"), (aT, "f_akT"), (oT, "f_vT"))):
                    out_of_bank(gx(dst, g), group_bank(g, k)[:, :], ("f_patterns_T", 3 * g + k + 1), name)
            for g in range(GROUPS):
                out_of_bank(gx(qT, g), group_bank(g, 3)[:, :], ("f_q_p", g + 1), "f_qT")
                out_of_bank(gx(kT, g), group_bank(g, 0)[:, :], ("f_k_p", g + 1), "f_kT")
            act_self_attention(a_, "f")
            for g in range(GROUPS):
                a_.wait_ge(sem("f_p_max"), g + 1)
                for j in range(TPG):
                    t = g * TPG + j
                    i = nc.scalar.activation(p_probs(g)[:, j, :], group_bank(g, 2)[:, j * D:(j + 1) * D], ACT.Exp,
                                             bias=f_nmax[:, 3, t:t + 1], scale=D ** -0.5, accum_out=f_sum[:, 3, t:t + 1])
                i.then_inc(sem("f_p_exp"), 1)
            for g in range(GROUPS):
                out_of_bank(gx(aT, g), group_bank(g, 3)[:, :], ("f_pp_T_p", g + 1), "f_ppT")
            for g in range(GROUPS):
                out_of_bank(gx(hT, g), group_bank(g, 1)[:, :], ("f2_hT_p", g + 1), "f2_hT")
            for g in range(GROUPS):
                for j in range(TPG):
                    t = g * TPG + j
                    a_.wait_ge(sem("f_f_max"), t + 1)
                    nc.scalar.activation(f_probs(g)[:, j, :, :].rearrange("p c n -> p (c n)"), group_bank(g, j)[:, :], ACT.Exp,
                                         bias=f_nmax[:, 4, t:t + 1], scale=D ** -0.5, accum_out=f_sum[:, 4, t:t + 1]).then_inc(sem("f_f_exp"), 1)
            for g in range(GROUPS):
                for j in range(TPG):
                    out_of_bank(probsT(g)[:, j, :, :], group_bank(g, j)[:, :].rearrange("p (c n) -> p c n", c=4), ("f_f_T", g * TPG + j + 1), "f_fT")

            out_of_bank(routerT[:, :], bank[2][:, 0:NE], ("g_wT_p", 1), "g_wT")
            for g in range(GROUPS):
                out_of_bank(gx(hT, g), group_bank(g, 1)[:, :], ("g_hT_p", g + 1), "g_hT")
            a_.wait_ge(*nth("g_top_diff", 1))
            nc.scalar.activation(top_p[:, 1, :], top_p[:, 0, :], ACT.Exp).then_inc(sem("g_top_exp"), 1)
            with a_.Fori(0, NE) as e:
                for n in range(4):
                    a_.wait_ge(*nth("g_up", 4 * e + (n + 1)))
                    nc.scalar.activation(silu_b(n), bank[2 * (n % 2) + 1][:, :], ACT.Silu).then_inc(sem("g_silu"), 1)

        @block.vector
        def _(v):
            v.wait_ge(sem("x_loaded"), 16)
            for g in range(GROUPS):
                dve_layer_norm(v, "b", g, x)
            for g in range(GROUPS):
                dve_normalise(v, "b", g, x)
            v.wait_ge(sem("constants"), 1)
            link(v, "v", nc.vector.tensor_reduce(head_mask[:, :], blk[:, :, :].rearrange("p g h -> p h g"), AX, ALU.add))
            link(v, "v", nc.vector.tensor_reduce(causal[:, :], causal4[:, :, :].rearrange("p b k -> p k b"), AX, ALU.add))
            i = nc.vector.tensor_copy(iota8[:, :], iota_i[:, :])
            link(v, "v", nc.vector.tensor_reduce(e_group[:, :], e_group16[:, :, :].rearrange("p b g -> p g b"), AX, ALU.add))
            v.wait_ge(sem("mask0_loaded"), 16)
            link(v, "v", nc.vector.tensor_scalar(b_mask, b_mask.bitcast(i32), 0, NEG, ALU.is_equal, ALU.mult))
            for g in range(GROUPS):
                v.wait_ge(sem("b_qbk_p"), g + 1)
                nc.vector.tensor_copy(q_bk[:, g * TPG:(g + 1) * TPG], group_bank(g, 3)[:, 0:TPG]).then_inc(sem("b_qbk"), 1)
            v.wait_ge(sem("b_qbk"), GROUPS)
            v.wait_ge(sem("ctx_last_p"), 1)
            nc.vector.tensor_copy(ctxT[:, :, LAST:NK].rearrange("p b a -> p (b a)"), bank[7][:, 0:NB]).then_inc(sem("ctxT_v"), 1)
            eye3 = ident[:, :].unsqueeze(1).broadcast_to([P, 3, D])
            bank3 = bank[4][:, 0:3 * P].rearrange("p (i n) -> p i n", i=3)

            def dve_expm_step(n):
                if n == 0:
                    v.wait_ge(sem("gen_loaded"), 16)
                    nc.vector.scalar_tensor_tensor(taylor[:, :, :], gen[:, :, :], 1.0 / (ORDER << SQUARINGS), eye3, ALU.mult, ALU.add).then_inc(sem("taylor"), 1)
                elif n < ORDER:
                    v.wait_ge(sem("taylor_p"), n)
                    nc.vector.scalar_tensor_tensor(taylor[:, :, :], bank3, 1.0 / ((ORDER - n) << SQUARINGS), eye3, ALU.mult, ALU.add).then_inc(sem("taylor"), 1)
                elif n < ORDER + SQUARINGS:
                    v.wait_ge(sem("taylor_p"), n)
                    v.wait_ge(sem("taylorT_p"), n - ORDER + 2)
                    nc.vector.tensor_copy(taylor[:, :, :], bank3).then_inc(sem("taylor"), 1)
                elif n < ORDER + SQUARINGS + 2:
                    v.wait_ge(sem("taylor_p"), n)
                    last = n > ORDER + SQUARINGS
                    nc.vector.tensor_copy((rot if last else pair)[:, :], bank[4][:, 0:P]).then_inc(sem("rot" if last else "pair"), 1)

            for n in range(0, NB // 2):
                dve_expm_step(n)
                if n % 2 == 0:
                    continue
                v.wait_ge(sem("ctxT_p"), n + 1)
                nc.vector.tensor_copy(ctxT[:, 2 * n:2 * n + 2, 0:LAST], bank[n % 4][:, :].rearrange("p (b k) -> p b k", b=2)).then_inc(sem("ctxT_v"), 1)
            for t in range(TILES):
                v.wait_ge(*nth("b_scores", t + 1))
                link(v, "v", nc.vector.scalar_tensor_tensor(b_probs(t), bank[t][:, 0:NK], q_bk[:, t:t + 1], b_mask[:, t, :], ALU.add, ALU.add))
                link(v, "v", nc.vector.tensor_reduce(row_max[:, t:t + 1], b_probs(t), AX, ALU.max))
                nc.vector.tensor_scalar(row_max[:, TILES + t:TILES + t + 1], row_max[:, t:t + 1], -D ** -0.5, None, ALU.mult).then_inc(sem("b_max"), 1)
            for t in range(TILES):
                v.wait_ge(*nth("b_exp", t + 1))
                nc.vector.tensor_scalar(b_last[:, t, :], last_mask[:, t, :], b_probs(t)[:, LAST:NK], None, ALU.mult).then_inc(sem("b_last"), 1)
                nc.vector.reciprocal(row_inv[:, t:t + 1], row_sum[:, t:t + 1]).then_inc(sem("b_inv"), 1)
            for t in range(TILES):
                v.wait_ge(*nth("b_pT", t + 1))
                nc.vector.tensor_copy(b_lastT[:, t, :], bank[t][0:NB, KC * P:KC * P + P]).then_inc(sem("b_lastT"), 1)
            for g in range(GROUPS):
                v.wait_ge(*nth("b_x_bias", g + 1))
                v.wait_ge(*nth("b_out", g + 1))
                link(v, "v", nc.vector.tensor_tensor(gx(x, g), gx(x, g), group_bank(g, 3)[:, :].rearrange("p (j n) -> p j n", j=TPG), ALU.add))
            for g in range(GROUPS):
                dve_layer_norm(v, "c", g, x)
            for g in range(GROUPS):
                dve_normalise(v, "c", g, x)
            dve_self_attention(v, "c", False)
            for g in range(GROUPS):
                v.wait_ge(*nth("c_x_bias", g + 1))
                v.wait_ge(*nth("c_projected", g + 1))
                nc.vector.tensor_tensor(gx(x, g), gx(x, g), group_bank(g, 2)[:, :].rearrange("p (j n) -> p j n", j=TPG), ALU.add).then_inc(sem("c_x"), 1)
            v.wait_ge(*nth("c_x", GROUPS))
            for g in range(GROUPS):
                dve_layer_norm(v, "d", g, x, twice=True)
            for g in range(GROUPS):
                dve_normalise(v, "d", g, x, twice=True)
            v.wait_ge(sem("d_w_loaded"), 160)
            v.wait_ge(*nth("d_logits", 1))
            link(v, "v", nc.vector.tensor_tensor(logits[:, :, :], group_bank(0, 2)[:, 0:TILES * NE].rearrange("p (t e) -> p t e", t=TILES),
                                                 gate_row[:, :].unsqueeze(1).broadcast_to([P, TILES, NE]), ALU.add))
            dve_top2(v, "d")
            by_expert = w_token[:, :, :].rearrange("p e t -> p t e")
            nc.vector.tensor_tensor(by_expert, pick[:, 0, :, :], pick[:, 1, :, :], ALU.add).then_inc(sem("d_w_token"), 1)
            for g in range(GROUPS):
                v.wait_ge(sem("d_abel_p"), g + 1)
                nc.vector.tensor_tensor(gx(abel, g), group_bank(g, 1)[:, :].rearrange("p (j n) -> p j n", j=TPG),
                                        abel_row[:, :].unsqueeze(1).broadcast_to([P, TPG, D]), ALU.add).then_inc(sem("d_abel_s"), 1)
            for g in range(GROUPS):
                v.wait_ge(sem("d_moe_b2"), g + 1)
                nc.vector.tensor_copy(gx(moe, g), group_bank(g, 2)[:, :].rearrange("p (j n) -> p j n", j=TPG)).then_inc(sem("d_acc"), 1)
            v.wait_ge(sem("d_abel"), GROUPS)
            for t in range(TILES):
                i = nc.vector.tensor_tensor_reduce(out=gx(mixed, 0)[:, 0, :], in0=abel[:, t, :], in1=mix_row[:, 0:D], scale=1.0, scalar=0.0,
                                                   op0=ALU.mult, op1=ALU.add, accum_out=mix_z[:, 0, t:t + 1])
                link(v, "v", i)
            dve_accumulate(v, "d", bank)
            for g in range(GROUPS):
                v.wait_ge(sem("d_nonabel"), g + 1)
                for j in range(TPG):
                    t = g * TPG + j
                    nc_bank = group_bank(g, 2)[:, j * P:(j + 1) * P]
                    link(v, "v", nc.vector.tensor_tensor_reduce(out=mixed[:, t, :], in0=nc_bank, in1=mix_row[:, D:2 * D], scale=1.0, scalar=0.0,
                                                                op0=ALU.mult, op1=ALU.add, accum_out=mix_z[:, 1, t:t + 1]))
            nc.vector.tensor_tensor(mix_z[:, 2, :], mix_z[:, 0, :], mix_z[:, 1, :], ALU.add).then_inc(sem("d_mix_z"), 1)
            for g in range(GROUPS):
                i = nc.vector.tensor_tensor(gx(mixed, g), group_bank(g, 2)[:, :].rearrange("p (j n) -> p j n", j=TPG), gx(abel, g), ALU.subtract)
            link(v, "v", i)
            v.wait_ge(sem("d_mix_g"), 1)
            for t in range(TILES):
                i = nc.vector.scalar_tensor_tensor(mixed[:, t, :], mixed[:, t, :], mix_g[:, t:t + 1], abel[:, t, :], ALU.mult, ALU.add)
            link(v, "v", i)
            v.wait_ge(*nth("d_x_res", GROUPS))
            for g in range(GROUPS):
                nc.vector.tensor_tensor(gx(x, g), gx(x, g), gx(mixed, g), ALU.add).then_inc(sem("d_x"), 1)

            v.wait_ge(*nth("d_x", GROUPS))
            v.sem_inc(sem("d_done"), 1)
            v.sem_inc(sem("e_done"), 2)
            for g in range(GROUPS):
                dve_layer_norm(v, "e", g, x)
            for g in range(GROUPS):
                dve_normalise(v, "e", g, x)

            def masked(t, slot, b):
                v.wait_ge(sem("constants"), 1)
                v.wait_ge(*nth("e_scores", BPT * t + (b + 1)))
                for g in range(HG):
                    n = b * HG + g
                    i = nc.vector.tensor_tensor_reduce(out=e_probs[b][:, g, :], in0=bank[g][:, 0:NK], in1=e_add[slot][:, b, :], scale=1.0,
                                                       scalar=-3e38, op0=ALU.add, op1=ALU.max, accum_out=e_max[:, n:n + 1])
                i.then_inc(sem("e_max"), 1)
                v.wait_ge(sem("e_max"), BPT * t + (b + 1))
                nc.vector.tensor_scalar(e_nmax[:, b * HG:(b + 1) * HG], e_max[:, b * HG:(b + 1) * HG], -HD ** -0.5, None, ALU.mult).then_inc(sem("e_masked"), 1)

            def probs_in(t, slot, b):
                v.wait_ge(*nth("e_exp", BPT * t + (b + 1)))
                nc.vector.reciprocal(e_inv[:, b * HG:(b + 1) * HG], e_sum[:, b * HG:(b + 1) * HG]).then_inc(sem("e_inv"), 1)
                v.wait_ge(sem("e_pT1"), BPT * t + (b + 1))
                nc.vector.tensor_copy(e_probsT[b % 2][:, 1, :, :], bank[6][:, :].rearrange("p (g n) -> p g n", g=HG)).then_inc(sem("e_pT_v"), 1)
                v.wait_ge(sem("e_p_last_p"), BPT * t + (b + 1))
                nc.vector.tensor_copy(e_p_lastT[:, b % 2, :], bank[4][0:BPT * HG, P:2 * P]).then_inc(sem("e_p_lastT"), 1)

            with v.Fori(0, TILES // 2) as pair_of_tiles:
                for slot in range(2):
                    t = 2 * pair_of_tiles + slot
                    v.wait_ge(sem("e_prep"), t + 1)
                    for b in range(BPT):
                        v.wait_ge(*nth("e_k_p", BPT * t + (b + 1)))
                        nc.vector.scalar_tensor_tensor(e_k[slot][:, b, :], bank[b][:, 0:NK], cols[:, BK1:BK1 + 1], e_keep[slot][:, b, :],
                                                       ALU.add, ALU.mult).then_inc(sem("e_k"), 1)
                    v.wait_ge(sem("e_v_last_p"), t + 1)
                    nc.vector.tensor_tensor(e_v_last[:, slot, :].rearrange("p (g f) -> p g f", g=HG), bank[4][0:BPT * HG, 0:D].rearrange("p (g f) -> p g f", g=HG),
                                            e_group[:, :].unsqueeze(2).broadcast_to([BPT * HG, HG, NQ]), ALU.mult).then_inc(sem("e_v_last"), 1)
                    masked(t, slot, 0)
                    for b in range(1, BPT):
                        masked(t, slot, b)
                        probs_in(t, slot, b - 1)
                    probs_in(t, slot, BPT - 1)
                    v.wait_ge(sem("e_inv_p"), t + 1)
                    head = head_mask[:, :].unsqueeze(1).unsqueeze(3).broadcast_to([P, BPT, HPG, NQ])
                    nc.vector.tensor_tensor(e_scale, bank[4][:, :].rearrange("p (b h q) -> p b h q", b=BPT, h=HPG), head, ALU.mult).then_inc(sem("e_scale"), 1)
                    v.wait_ge(sem("e_scale"), t + 1)
                    nc.vector.tensor_tensor(e_out, bank[7][:, :].rearrange("p (b h q) -> p b h q", b=BPT, h=HPG), e_scale, ALU.mult).then_inc(sem("e_scaled"), 1)
                    v.wait_ge(sem("e_scaled"), t + 1)
                    nc.vector.tensor_reduce(oT[:, bass.ds(t * P, P)].rearrange("p (b q) -> p b q", b=BPT), e_out.rearrange("p b h q -> p b q h"),
                                            AX, ALU.add).then_inc(sem("e_done"), 1)
            for g in range(GROUPS):
                v.wait_ge(*nth("e_x_bias", g + 1))
                v.wait_ge(*nth("e_projected", g + 1))
                nc.vector.tensor_tensor(gx(x, g), gx(x, g), group_bank(g, 0)[:, :].rearrange("p (j n) -> p j n", j=TPG), ALU.add).then_inc(sem("e_x"), 1)

            v.wait_ge(*nth("e_x", GROUPS))
            for g in range(GROUPS):
                dve_layer_norm(v, "f", g, x, twice=True)
            for g in range(GROUPS):
                dve_normalise(v, "f", g, x, twice=True)

            def negative_max(ph, kinds, tiles, scores_of, done):
                k0, k1 = kinds
                for t in tiles:
                    i = nc.vector.tensor_reduce(f_max[:, k0:k1, t:t + 1], scores_of(t), AX, ALU.max)
                link(v, "v", i)
                a, b = tiles[0], tiles[-1] + 1
                nc.vector.tensor_scalar(f_nmax[:, k0:k1, a:b], f_max[:, k0:k1, a:b], -D ** -0.5, None, ALU.mult).then_inc(sem(done), 1)

            for g in range(GROUPS):
                v.wait_ge(sem("f_scores3"), TPG * (g + 1))
                negative_max("f", (0, 3), range(g * TPG, (g + 1) * TPG),
                             lambda t: group_bank(t // TPG, t % TPG)[:, 0:3 * D].rearrange("p (k n) -> p k n", k=3), "f_max3")
            for g in range(GROUPS):
                v.wait_ge(sem("f_exp3"), g + 1)
                sl = slice(g * TPG, (g + 1) * TPG)
                link(v, "v", nc.vector.reciprocal(f_inv[:, 0:3, sl], f_sum[:, 0:3, sl]))
                for k in range(3):
                    i = nc.vector.tensor_tensor(patterns(g)[:, :, k, :], patterns(g)[:, :, k, :],
                                                f_inv[:, k, sl].unsqueeze(2).broadcast_to([P, TPG, D]), ALU.mult)
                i.then_inc(sem("f_patterns"), 1)
            dve_self_attention(v, "f", True)
            for g in range(GROUPS):
                v.wait_ge(sem("f_p_scores"), g + 1)
                sl = slice(g * TPG, (g + 1) * TPG)
                link(v, "v", nc.vector.tensor_reduce(f_max[:, 3, sl], group_bank(g, 2)[:, :].rearrange("p (j n) -> p j n", j=TPG), AX, ALU.max))
                nc.vector.tensor_scalar(f_nmax[:, 3, sl], f_max[:, 3, sl], -D ** -0.5, None, ALU.mult).then_inc(sem("f_p_max"), 1)
            for g in range(GROUPS):
                v.wait_ge(sem("f_p_exp"), g + 1)
                sl = slice(g * TPG, (g + 1) * TPG)
                link(v, "v", nc.vector.reciprocal(f_inv[:, 3, sl], f_sum[:, 3, sl]))
                v.wait_ge(sem("f_p_out"), g + 1)
                for j in range(TPG):
                    t = g * TPG + j
                    i = nc.vector.scalar_tensor_tensor(res[:, t, :], group_bank(g, 0)[:, j * P:(j + 1) * P], f_inv[:, 3, t:t + 1], res[:, t, :], ALU.mult, ALU.add)
                i.then_inc(sem("f_x2"), 1)
                v.wait_ge(sem("f_x2"), g + 1)
                dve_layer_norm(v, "f2", g, res)
            for g in range(GROUPS):
                dve_normalise(v, "f2", g, res)
            for t in range(TILES):
                v.wait_ge(sem("f_f_scores"), t + 1)
                link(v, "v", nc.vector.tensor_reduce(f_max[:, 4, t:t + 1], group_bank(t // TPG, t % TPG)[:, :], AX, ALU.max))
                nc.vector.tensor_scalar(f_nmax[:, 4, t:t + 1], f_max[:, 4, t:t + 1], -D ** -0.5, None, ALU.mult).then_inc(sem("f_f_max"), 1)
            for g in range(GROUPS):
                v.wait_ge(sem("f_f_exp"), TPG * (g + 1))
                sl = slice(g * TPG, (g + 1) * TPG)
                link(v, "v", nc.vector.reciprocal(f_inv[:, 4, sl], f_sum[:, 4, sl]))
                v.wait_ge(*nth("f_x_res", g + 1))
                v.wait_ge(sem("f_f_out"), g + 1)
                for j in range(TPG):
                    t = g * TPG + j
                    i = nc.vector.scalar_tensor_tensor(x[:, t, :], group_bank(g, 0)[:, j * P:(j + 1) * P], f_inv[:, 4, t:t + 1], x[:, t, :], ALU.mult, ALU.add)
                i.then_inc(sem("f_x"), 1)
                v.wait_ge(*nth("f_x", g + 1))
                dve_layer_norm(v, "g", g, x)

            for g in range(GROUPS):
                dve_normalise(v, "g", g, x)
            for g in range(GROUPS):
                nc.vector.memset(gx(moe, g), 0.0).then_inc(sem("g_acc"), 1)
            nc.vector.memset(picked_before[:, 0, :], 0.0)
            v.wait_ge(sem("g_w_loaded"), 32)
            v.wait_ge(*nth("g_logits", 1))
            link(v, "v", nc.vector.tensor_tensor(logits[:, :, :], bank[2][:, 0:TILES * NE].rearrange("p (t e) -> p t e", t=TILES),
                                                 router_row[:, :].unsqueeze(1).broadcast_to([P, TILES, NE]), ALU.add))
            dve_top2(v, "g")
            v.wait_ge(sem("g_rank"), 1)
            nc.vector.tensor_scalar(kept[:, :, :], bank[6][:, 0:TILES * NE].rearrange("p (t e) -> p t e", t=TILES), float(CAPACITY), None, ALU.is_lt)
            link(v, "v", nc.vector.tensor_tensor(pick[:, 0, :, :], pick[:, 0, :, :], pick[:, 1, :, :], ALU.add))
            link(v, "v", nc.vector.tensor_tensor(by_expert, pick[:, 0, :, :], kept[:, :, :], ALU.mult))

            def gated_hidden(e, slot):
                for n in range(4):
                    c, g = n // GROUPS, n % GROUPS
                    v.wait_ge(sem("g_silu"), 4 * e + (n + 1))
                    nc.vector.tensor_tensor(hidden(slot)[:, c, g * GW:(g + 1) * GW], bank[2 * (n % 2)][:, :], silu_b(n), ALU.mult).then_inc(sem("g_hidden"), 1)

            def accumulate(e):
                for g in range(GROUPS):
                    v.wait_ge(*nth("g_down", 2 * e + (g + 1)))
                    v.wait_ge(*nth("g_acc", 2 * e + (g + 1)))
                    for j in range(TPG):
                        t = g * TPG + j
                        i = nc.vector.scalar_tensor_tensor(moe[:, t, :], bank[4 + g][:, j * P:(j + 1) * P],
                                                           w_token[:, :, :].rearrange("p e t -> p (e t)")[:, bass.ds(e * TILES + t, 1)],
                                                           moe[:, t, :], ALU.mult, ALU.add)
                    i.then_inc(sem("g_acc"), 1)

            gated_hidden(0, 0)
            gated_hidden(1, 1)
            accumulate(0)
            with v.Fori(1, NE // 2) as pair_of_experts:
                e = 2 * pair_of_experts
                gated_hidden(e, 0)
                accumulate(e - 1)
                gated_hidden(e + 1, 1)
                accumulate(e)
            accumulate(NE - 1)
            for g in range(GROUPS):
                v.wait_ge(*nth("g_acc", 2 * NE + (g + 1)))
                nc.vector.tensor_tensor(gx(x, g), gx(x, g), gx(moe, g), ALU.add).then_inc(sem("x_final"), 1)


_OUT = ((32, 32, 128), "float32")


def kernel(**inputs):
    import numpy as _np
    import concourse.bacc as _bacc
    from concourse import mybir as _mybir
    from concourse.bass_utils import run_bass_kernel_spmd as _run

    nc = _bacc.Bacc("TRN2", target_bir_lowering=False, num_devices=1)
    arrays, io = {}, {}
    for name, value in inputs.items():
        a = _np.ascontiguousarray(value)
        arrays[f"in_{name}"] = a
        io[name] = nc.dram_tensor(f"in_{name}", a.shape, _mybir.dt.from_np(a.dtype), kind="ExternalInput").ap()
    out = nc.dram_tensor("out_0", _OUT[0], _mybir.dt.from_np(_np.dtype(_OUT[1])), kind="ExternalOutput").ap()
    perceiver(nc, io, out)
    r = _run(nc, [arrays], core_ids=[0])
    return r.results[0]["out_0"]
```

```python
import concourse.bass as bass
from concourse import mybir
from contextlib import ExitStack

NB, NQ, NK, D = 32, 32, 257, 128
TOKENS = NB * NQ
P = 128
TILES = TOKENS // P
BPT = P // NQ
GROUPS = 2
TPG = TILES // GROUPS
GW = TPG * P
H, HD = 16, D // 16
HG = 4
HPG = H // HG
KC = NK // P
LAST = KC * P
NE, DF, DH = 8, 4 * D, 256
CAPACITY = 2 * 512 * 2 // NE
EPS = 1e-5
NEG = -1e30
SQUARINGS, ORDER = NE // 2 - 1, 10


def perceiver(nc, io, out_d):
    fp32, fp32r, i32, u32 = mybir.dt.float32, mybir.dt.float32r, mybir.dt.int32, mybir.dt.uint32
    ALU, ACT, AX = mybir.AluOpType, mybir.ActivationFunctionType, mybir.AxisListType.X

    ctx = ExitStack()
    with ctx:
        def sb(name, shape, dt=fp32):
            return ctx.enter_context(nc.sbuf_tensor(name, shape, dt))

        sems = {}

        norms = ("b", "c", "d", "e", "f", "f2", "g")
        in_stages = {name: {st: GROUPS for st in norms} for name in ("var", "rstd", "h", "hT_p", "hT")}
        in_stages.update({name: {"b": n, "c": m, "f": m} for name, n, m in
                          (("scores", TILES, GROUPS), ("exp", TILES, GROUPS), ("inv", TILES, GROUPS), ("pT", TILES, TILES), ("probsT", TILES, TILES))})
        in_stages.update({name: {"c": n, "f": n} for name, n in
                          (("v_in", GROUPS), ("v", TILES), ("v_heads", TILES), ("k_heads", GROUPS), ("shifted", GROUPS * HG), ("inv_tok", GROUPS),
                           ("out", GROUPS), ("inv_rows", GROUPS), ("oT", GROUPS), ("k_p", GROUPS), ("kT", GROUPS))})
        in_stages.update({
            "q_p": {st: GROUPS for st in "bcef"}, "qT": {st: GROUPS for st in "bcef"},
            "x_bias": {st: GROUPS for st in "bce"}, "obT": {st: GROUPS for st in "ce"}, "projected": {st: GROUPS for st in "ce"},
            "x": {st: GROUPS for st in "cdef"}, "x_res": {st: GROUPS for st in "df"},
            "wT_p": {"m": 1, "b": 1, "d": 1, "f": 2, "g": 1}, "wT": {"m": 1, "b": 1, "d": 1, "f": 2, "g": 1},
            "logits": {"d": 1, "g": 1}, "top_diff": {"d": 1, "g": 1}, "top_exp": {"d": 1, "g": 1},
            "x_high": {st: GROUPS for st in "dg"}, "x_split": {st: GROUPS for st in "dg"}, "w1_high": {st: NE for st in "dg"}, "w1_split": {st: NE for st in "dg"},
            "up": {"d": 8 * NE, "g": 4 * NE}, "down": {st: GROUPS * NE for st in "dg"}, "acc": {st: GROUPS * (NE + 1) for st in "dg"},
        })
        in_stages.update({f"{w}_loaded{slot}": {"d": 16 * NE // 2, "g": n * 16 * NE // 2} for w, n in (("w1", 2), ("w2", 1)) for slot in range(2)})

        def stage_of(name):
            stage, _, rest = name.partition("_")
            return (stage, rest) if rest in in_stages and stage in in_stages[rest] else (None, name)

        def sem(name):
            name = stage_of(name)[1]
            if name not in sems:
                sems[name] = ctx.enter_context(nc.semaphore(name))
            return sems[name]

        def nth(name, n):
            stage, rest = stage_of(name)
            if stage is not None:
                stages = list(in_stages[rest])
                n = n + sum(in_stages[rest][st] for st in stages[:stages.index(stage)])
            return sem(name), n

        x = sb("x", [P, TILES, D])
        res = sb("res", [P, TILES, D])
        h = sb("h", [P, TILES, D])
        hT = sb("hT", [P, TOKENS])
        qT = sb("qT", [P, TOKENS])
        kT = sb("kT", [P, TOKENS])
        oT = sb("oT", [P, TOKENS])
        aT = sb("aT", [P, TOKENS])
        r1 = sb("r1", [P, NB * KC * D])
        ctxT = sb("ctxT", [P, NB, NK])
        r3 = sb("r3", [P, 4096])
        r4 = sb("r4", [P, 4096])
        parts = sb("parts", [P, 4096])
        r6 = sb("r6", [P, 4096])
        ctx_last = sb("ctx_last", [NB, D])
        ident = sb("ident", [P, P])
        ones = sb("ones", [P, P])
        blk = sb("blk", [P, HG, HPG])
        head_mask = sb("head_mask", [P, HPG])
        v_mask = sb("v_mask", [P, HG, HPG, HD])
        causal4 = sb("causal4", [P, BPT, NQ])
        causal = sb("causal", [P, NQ])
        last_mask = sb("last_mask", [P, TILES, NB])
        stats = sb("stats", [P, TILES, 6])
        mean_var = sb("mean_var", [P, TILES, 2])
        var_eps = sb("var_eps", [P, 2, TILES])
        rstd = sb("rstd", [P, 2, TILES])
        minus_half = sb("minus_half", [P, 2 * TILES])
        w_a = sb("w_a", [P, 4, D])
        w_aT = sb("w_aT", [P, 4, D])
        w_b = sb("w_b", [P, 4, D])
        w_bT = sb("w_bT", [P, 4, D])
        wk0 = sb("wk0", [P, D])
        w_qkv = sb("w_qkv", [P, 3 * D])
        w_proj = sb("w_proj", [P, D])
        cols = sb("cols", [P, 16])
        bo_row = sb("bo_row", [P, D])
        bproj_row = sb("bproj_row", [P, D])
        q_bk = sb("q_bk", [P, TILES])
        row_max = sb("row_max", [P, 4 * TILES])
        row_sum = sb("row_sum", [P, 4 * TILES])
        row_inv = sb("row_inv", [P, 4 * TILES])
        head_max = sb("head_max", [P, GROUPS, HG, TPG * HPG])
        head_sum = sb("head_sum", [P, GROUPS, HG, TPG * HPG])
        head_inv = sb("head_inv", [P, GROUPS, HG, TPG * HPG])
        taylor = sb("taylor", [P, 3, D])
        gen = sb("gen", [P, 3, D])
        genT = sb("genT", [P, 3, D])
        taylorT = sb("taylorT", [P, 3, D])
        pair = sb("pair", [P, D])
        rot = sb("rot", [P, D])
        abel_w = sb("abel_w", [P, D])
        abel_row = sb("abel_row", [P, D])
        gate_w = sb("gate_w", [P, NE])
        gate_row = sb("gate_row", [P, NE])
        mix_row = sb("mix_row", [P, 2 * D])
        mix_b = sb("mix_b", [P, 1])
        mix_z = sb("mix_z", [P, 3, TILES])
        mix_g = sb("mix_g", [P, TILES])
        b1_rows = sb("b1_rows", [NE * 4, D])
        b1_cols = sb("b1_cols", [P, NE * 4])
        b1_now = sb("b1_now", [P, 2, 4])
        b2_rows = sb("b2_rows", [NE, D])
        w1 = sb("w1", [P, 2, DF])
        w2 = sb("w2", [P, 2, 4, D])
        iota_i = sb("iota_i", [P, NE], i32)
        iota8 = sb("iota8", [P, NE])
        logits = sb("logits", [P, TILES, NE])
        top8 = sb("top8", [P, TILES, 8])
        top_index = sb("top_index", [P, TILES, 8], u32)
        top_f = sb("top_f", [P, TILES, 2])
        top_p = sb("top_p", [P, 3, TILES])
        pick = sb("pick", [P, 2, TILES, NE])
        w_token = sb("w_token", [P, NE, TILES])
        w_tokenT = sb("w_tokenT", [NE, TOKENS])
        w_e = sb("w_e", [P, 4, D])
        bo1_row = sb("bo1_row", [P, D])
        e_group16 = sb("e_group16", [4 * HG, BPT, HG])
        e_group = sb("e_group", [4 * HG, HG])
        e_last_in = sb("e_last_in", [P, 2, BPT * HG])
        e_v_last = sb("e_v_last", [BPT * HG, 2, D])
        e_p_last = sb("e_p_last", [P, BPT, BPT * HG])
        e_p_lastT = sb("e_p_lastT", [BPT * HG, 2, P])
        e_max = sb("e_max", [P, BPT * HG])
        e_nmax = sb("e_nmax", [P, BPT * HG])
        e_sum = sb("e_sum", [P, BPT * HG])
        e_inv = sb("e_inv", [P, BPT * HG])
        f_max = sb("f_max", [P, 5, TILES])
        f_nmax = sb("f_nmax", [P, 5, TILES])
        f_sum = sb("f_sum", [P, 5, TILES])
        f_inv = sb("f_inv", [P, 5, TILES])
        routerT = sb("routerT", [P, NE])
        router_row = sb("router_row", [P, NE])
        bank = [ctx.enter_context(nc.psum_tensor(f"bank{i}", [P, 512], fp32)) for i in range(8)]

        ctx_keys = r1[:, :].rearrange("p (b c d) -> p b c d", b=NB, c=KC)
        BQ0, BV0, BQ, BK, BV, BK0, LN_G, LN_B, BQ1, BK1, BV1 = range(11)

        def group_bank(g, k):
            return bank[4 * g + k]

        def gx(t, g):
            return t[:, g * TPG:(g + 1) * TPG, :] if len(t.shape) == 3 else t[:, g * GW:(g + 1) * GW]

        def first_batches(t):
            return isinstance(t, int) and t == 0

        def later(step, t, slot, b, n):
            t, slot = (t, slot) if b + n < BPT else (t + 1, 1 - slot)
            if not (isinstance(t, int) and t == TILES):
                step(t, slot, (b + n) % BPT)

        def wait_alone(eng, name, n):
            eng.wait_ge(*nth(name, n))
            if not isinstance(n, int):
                eng.nop(nofuse=True)

        def over_batches(eng, step):
            def pair(t0):
                for slot in range(2):
                    for b in range(BPT):
                        step(t0 + slot, slot, b)

            pair(0)
            with eng.Fori(1, TILES // 2 - 1) as pair_of_tiles:
                pair(2 * pair_of_tiles)
            pair(TILES - 2)

        step_count = {"v": 0, "g": 0, "a": 0}

        def mark(key, ins):
            step_count[key] += 1
            ins.then_inc(sem("step_" + key), 1)
            return step_count[key]

        def link(eng, key, ins):
            eng.wait_ge(sem("step_" + key), mark(key, ins))

        def k_heads(g):
            return (r4 if g == 0 else r1)[:, 0:TPG * 512].rearrange("p (j b n) -> p j b n", j=TPG, b=BPT)

        def v_heads(g):
            return (r4 if g == 0 else r1)[:, TPG * 512:2 * TPG * 512].rearrange("p (j b n) -> p j b n", j=TPG, b=BPT)

        def probs(g):
            return r3[:, g * 2048:(g + 1) * 2048].rearrange("p (a j n) -> p a j n", a=HG, j=TPG)

        def v_in(g):
            return r6[:, g * 2048:(g + 1) * 2048].rearrange("p (j b n) -> p j b n", j=TPG, b=BPT)

        def probsT(g):
            return r6[:, g * 2048:(g + 1) * 2048].rearrange("p (j a n) -> p j a n", j=TPG, a=HG)

        def b_probs(t):
            return r3[:, t * NK:(t + 1) * NK]

        def b_probsT(t):
            return r6[:, 1536 + t * LAST:1536 + (t + 1) * LAST]

        b_last = r6[:, 0:TILES * NB].rearrange("p (t b) -> p t b", t=TILES)
        b_lastT = r6[0:NB, 512:512 + TILES * P].rearrange("p (t n) -> p t n", t=TILES)
        b_mask = r4[:, 0:TILES * NK].rearrange("p (t k) -> p t k", t=TILES)

        def ring(t, at, n):
            return t[:, at:at + BPT * n].rearrange("p (b n) -> p b n", b=BPT)

        e_k, e_keep, e_add = (ring(r1, i * BPT * NK, NK) for i in range(3))
        e_q = ring(r1, 3 * BPT * NK, HG * P)
        e_mask = [r6[:, i * BPT * NK:(i + 1) * BPT * NK].bitcast(i32).rearrange("p (b k) -> p b k", b=BPT) for i in range(2)]
        e_ctx = ring(r6, 2 * BPT * NK, LAST)
        e_probs = [(r3[:, b * HG * NK:(b + 1) * HG * NK] if b < 3 else r4[:, 0:HG * NK]).rearrange("p (g k) -> p g k", g=HG)
                   for b in range(BPT)]
        e_v = ring(kT, 0, LAST).rearrange("p b (c d) -> p b c d", c=KC)
        e_probsT = [r4[:, HG * NK + i * KC * 512:HG * NK + (i + 1) * KC * 512].rearrange("p (c g n) -> p c g n", c=KC, g=HG) for i in range(2)]
        e_inv_tok = aT[:, 0:2 * P].rearrange("p (s n) -> p s n", s=2)
        e_scaled = h[:, 0:2, :].rearrange("p s (h q) -> p s h q", h=HPG)

        F0 = 5 * BPT * NK
        w_v = r1[:, F0:F0 + 4 * D].rearrange("p (i d) -> p i d", i=4)
        f_k = r1[:, F0 + 4 * D:F0 + 8 * D].rearrange("p (i d) -> p i d", i=4)
        f_kT = r1[:, F0 + 8 * D:F0 + 12 * D]
        f_v = r1[:, F0 + 12 * D:F0 + 16 * D].rearrange("p (i d) -> p i d", i=4)

        G0 = F0 + 16 * D
        before = r1[:, G0:G0 + P]
        router_rows = r1[0:NE, G0 + P:G0 + P + D]
        picked, picked_before, kept = (r1[:, G0 + P + D + i * TILES * NE:G0 + P + D + (i + 1) * TILES * NE].rearrange("p (t e) -> p t e", t=TILES)
                                       for i in range(3))

        def patterns(g):
            return r3[:, g * 2048:g * 2048 + 1536].rearrange("p (j i n) -> p j i n", j=TPG, i=3)

        def p_probs(g):
            return r3[:, g * 2048:g * 2048 + 512].rearrange("p (j n) -> p j n", j=TPG)

        def f_probs(g):
            return (r4 if g == 0 else r1)[:, 0:2048].rearrange("p (j c n) -> p j c n", j=TPG, c=4)

        def silu_b(n):
            return r1[:, n * 512:(n + 1) * 512]

        abel = oT[:, :].rearrange("p (t d) -> p t d", t=TILES)
        moe = kT[:, :].rearrange("p (t d) -> p t d", t=TILES)
        moeT = aT
        mixed = h

        def hidden(slot):
            return (r3 if slot == 0 else r4)[:, :].rearrange("p (c n) -> p c n", c=4)

        def x_part(part):
            return parts[:, part * TOKENS:(part + 1) * TOKENS]

        def w1_part(slot, part):
            at = 2 * TOKENS + (2 * slot + part) * DF
            return parts[:, at:at + DF]

        def split_product(out, slot, cols_, g):
            for n, (w, a) in enumerate(((0, 0), (0, 1), (1, 0))):
                i = nc.tensor.matmul(out, w1_part(slot, w)[:, cols_].bitcast(fp32r), gx(x_part(a), g).bitcast(fp32r), start=n == 0, stop=n == 2)
            return i

        block = ctx.enter_context(nc.Block())

        def w1_d(e):
            return io["L0_ffn_w1"].rearrange("e p f -> (e p) f")[bass.ds(e * D, D), :]

        def w2_d(e):
            return io["L0_ffn_w2"].rearrange("e f d -> (e f) d")[bass.ds(e * DF, DF), :].rearrange("(c p) d -> p c d", c=4)

        @block.sync
        def _(sp):
            sp.dma_start(x[:, :, :], io["x"].rearrange("(t b) q d -> (b q) t d", t=TILES)).then_inc(sem("x_loaded"), 16)
            sp.dma_start(gen[:, :, :], io["L0_ffn_gens"].rearrange("i p n -> p i n")).then_inc(sem("gen_loaded"), 16)
            for i, name in enumerate(("L0_xattn_Wq", "L0_xattn_Wv", "L0_xattn_Wo", "L1_attn_pK")):
                sp.dma_start(w_a[:, i, :], io[name]).then_inc(sem("w_a_loaded"), 16)
            sp.dma_start(wk0[:, :], io["L0_xattn_Wk"]).then_inc(sem("b_w_loaded"), 16)
            for c, name in ((BQ0, "L0_xattn_bq"), (BV0, "L0_xattn_bv"), (BK0, "L0_xattn_bk")):
                sp.dma_start(cols[:, c:c + 1], io[name].rearrange("(p a) -> p a", a=1)).then_inc(sem("b_w_loaded"), 16)
            sp.dma_start(bo_row[:, :], io["L0_xattn_bo"].rearrange("(a n) -> a n", a=1).broadcast_to([P, D])).then_inc(sem("b_w_loaded"), 16)
            sp.dma_start(ctx_last[:, :], io["ctx_1024"][:, LAST, :]).then_inc(sem("ctx_last_loaded"), 16)
            for b in range(0, NB, 8):
                for c in range(KC):
                    sp.dma_start(ctx_keys[:, b:b + 8, c, :], io["ctx_1024"][b:b + 8, c * P:(c + 1) * P, :].rearrange("b k d -> k b d")).then_inc(sem(f"ctx_loaded{b // 8}"), 16)
            mask_i = r4[:, 0:TILES * NK].bitcast(i32).rearrange("p (t k) -> p t k", t=TILES)
            sp.dma_start(mask_i, io["mask_BxSxS2_ik0"].rearrange("(t b) q k -> (b q) t k", t=TILES)).then_inc(sem("mask0_loaded"), 16)
            sp.dma_start(w_qkv[:, :], io["L0_attn_w_qkv"]).then_inc(sem("c_w_loaded"), 16)
            sp.dma_start(w_proj[:, :], io["L0_attn_w_proj"]).then_inc(sem("c_w_loaded"), 16)
            for i, c in enumerate((BQ, BK, BV)):
                sp.dma_start(cols[:, c:c + 1], io["L0_attn_b_qkv"][i * D:(i + 1) * D].rearrange("(p a) -> p a", a=1)).then_inc(sem("c_w_loaded"), 16)
            sp.dma_start(bproj_row[:, :], io["L0_attn_b_proj"].rearrange("(a n) -> a n", a=1).broadcast_to([P, D])).then_inc(sem("c_w_loaded"), 16)
            for name, dst, src in (
                ("d", abel_w[:, :], io["L0_ffn_abel_w"]), ("d", gate_w[:, :], io["L0_ffn_gate_w_moe"]),
                ("d", cols[:, LN_G:LN_G + 1], io["L0_ffn_ln_g"].rearrange("(p a) -> p a", a=1)),
                ("d", cols[:, LN_B:LN_B + 1], io["L0_ffn_ln_b"].rearrange("(p a) -> p a", a=1)),
                ("d", abel_row[:, :], io["L0_ffn_abel_b"].rearrange("(a n) -> a n", a=1).broadcast_to([P, D])),
                ("d", gate_row[:, :], io["L0_ffn_gate_b_moe"].rearrange("(a n) -> a n", a=1).broadcast_to([P, NE])),
                ("d", mix_row[:, :], io["L0_ffn_mix_w"].rearrange("n a -> a n").broadcast_to([P, 2 * D])),
                ("d", mix_b[:, :], io["L0_ffn_mix_b"].rearrange("(a n) -> a n", a=1).broadcast_to([P, 1])),
                ("d", b1_rows[:, :], io["L0_ffn_b1"].rearrange("e (c p) -> (e c) p", c=4)),
                ("d", b2_rows[:, :], io["L0_ffn_b2"]),
            ):
                sp.dma_start(dst, src).then_inc(sem("d_w_loaded"), 16)

            for i, name in enumerate(("Wq", "Wk", "Wv", "Wo")):
                sp.dma_start(w_e[:, i, :], io["L1_xattn_" + name]).then_inc(sem("e_w_loaded"), 16)
            for c, name in ((BQ1, "bq"), (BK1, "bk"), (BV1, "bv")):
                sp.dma_start(cols[:, c:c + 1], io["L1_xattn_" + name].rearrange("(p a) -> p a", a=1)).then_inc(sem("e_w_loaded"), 16)
            sp.dma_start(bo1_row[:, :], io["L1_xattn_bo"].rearrange("(a n) -> a n", a=1).broadcast_to([P, D])).then_inc(sem("e_w_loaded"), 16)

            for i, name in enumerate(("qK", "kK", "vK")):
                sp.dma_start(w_b[:, i, :], io["L1_attn_" + name]).then_inc(sem("f_w_loaded"), 16)
            sp.dma_start(router_row[:, :], io["L1_ffn_router_b"].rearrange("(a n) -> a n", a=1).broadcast_to([P, NE])).then_inc(sem("g_w_loaded"), 16)
            sp.wait_ge(sem("b_av"), TILES)
            sp.dma_start(router_rows[:, :], io["L1_ffn_router_w"]).then_inc(sem("g_w_loaded"), 16)
            for i, name in enumerate(("qV", "kV", "vV", "pV")):
                sp.dma_start(w_v[:, i, :], io["L1_attn_" + name]).then_inc(sem("f_w_loaded"), 16)
            sp.dma_start(f_k, io["L1_attn_fK"].rearrange("(i p) d -> p i d", i=4)).then_inc(sem("f_w_loaded"), 16)
            sp.dma_start(f_v, io["L1_attn_fV"].rearrange("(i p) d -> p i d", i=4)).then_inc(sem("f_w_loaded"), 16)

            def load_expert(e, slot):
                sp.dma_start(w1[:, slot, :], w1_d(e)).then_inc(sem(f"d_w1_loaded{slot}"), 16)
                sp.dma_start(w2[:, slot, :, :], w2_d(e)).then_inc(sem(f"d_w2_loaded{slot}"), 16)

            load_expert(0, 0)
            load_expert(1, 1)
            with sp.Fori(1, NE // 2) as pair_of_experts:
                e = 2 * pair_of_experts
                for slot in range(2):
                    sp.wait_ge(*nth("d_w1_split", e + (slot - 1)))
                    sp.dma_start(w1[:, slot, :], w1_d(e + slot)).then_inc(sem(f"d_w1_loaded{slot}"), 16)
                    sp.wait_ge(*nth("d_down", 2 * (e + (slot - 1))))
                    sp.dma_start(w2[:, slot, :, :], w2_d(e + slot)).then_inc(sem(f"d_w2_loaded{slot}"), 16)
            def load_mask(t, slot):
                src = io["mask_Bx1x1xS2_ik0"].rearrange("b a c k -> (a c) (b k)")[:, bass.ds(t * BPT * NK, BPT * NK)]
                sp.dma_start(r6[:, slot * BPT * NK:(slot + 1) * BPT * NK].bitcast(i32),
                             src.broadcast_to([P, BPT * NK])).then_inc(sem(f"e_mask_loaded{slot}"), 16)

            load_mask(0, 0)
            load_mask(1, 1)
            with sp.Fori(1, TILES // 2) as pair_of_tiles:
                for slot in range(2):
                    t = 2 * pair_of_tiles + slot
                    sp.wait_ge(sem("e_prep"), BPT * t - BPT)
                    load_mask(t, slot)
            def load_gated(e, slot):
                for i, name in enumerate(("W", "V")):
                    sp.dma_start(w1[:, slot, i * DH:(i + 1) * DH],
                                 io["L1_ffn_" + name].rearrange("e p f -> (e p) f")[bass.ds(e * D, D), :]).then_inc(sem(f"g_w1_loaded{slot}"), 16)

            def load_gated_out(e, slot):
                sp.dma_start(w2[:, slot, 0:2, :], io["L1_ffn_W_out"].rearrange("e f d -> (e f) d")[bass.ds(e * DH, DH), :]
                             .rearrange("(c p) d -> p c d", c=2)).then_inc(sem(f"g_w2_loaded{slot}"), 16)

            for e in range(2):
                load_gated(e, e)
                load_gated_out(e, e)
            with sp.Fori(1, NE // 2) as pair_of_experts:
                e = 2 * pair_of_experts
                for slot in range(2):
                    sp.wait_ge(*nth("g_w1_split", e + (slot - 1)))
                    load_gated(e + slot, slot)
                    sp.wait_ge(*nth("g_down", 2 * (e + (slot - 1))))
                    load_gated_out(e + slot, slot)
            for g in range(GROUPS):
                sp.wait_ge(sem("x_final"), g + 1)
                sp.dma_start(out_d.rearrange("(t b) q d -> (b q) t d", t=TILES)[:, g * TPG:(g + 1) * TPG, :], gx(x, g)).then_inc(sem("stored"), 16)
            sp.wait_ge(sem("stored"), 16 * GROUPS)

        def pool_rstd(gp, ph, g, n):
            gp.wait_ge(*nth(ph + "_var", g + 1))
            sl = slice(g * TPG, (g + 1) * TPG)
            mh = minus_half[:, 0:n * TPG].rearrange("p (n t) -> p n t", n=n)
            nc.gpsimd.tensor_tensor(rstd[:, 0:n, sl], var_eps[:, 0:n, sl], mh, ALU.pow).then_inc(sem(ph + "_rstd"), 1)

        def pool_add_row(gp, ph, g, row, loaded):
            gp.wait_ge(*nth(loaded[0], loaded[1]))
            gp.wait_ge(*nth(ph + "_h", g + 1))
            nc.gpsimd.tensor_tensor(gx(x, g), gx(x, g), row[:, :].unsqueeze(1).broadcast_to([P, TPG, D]), ALU.add).then_inc(sem(ph + "_x_bias"), 1)

        def dve_k_heads(v, ph, g):
            v.wait_ge(*nth(ph + "_kT", g + 1))
            for j in range(TPG):
                src = kT[:, g * GW + j * P:g * GW + (j + 1) * P].rearrange("p (b k) -> p b k", b=BPT)
                i = nc.vector.tensor_tensor(
                    k_heads(g)[:, j, :, :].rearrange("p b (h k) -> p b h k", h=HPG),
                    src.unsqueeze(2).broadcast_to([P, BPT, HPG, NQ]),
                    head_mask[:, :].unsqueeze(1).unsqueeze(3).broadcast_to([P, BPT, HPG, NQ]), ALU.mult)
            i.then_inc(sem(ph + "_k_heads"), 1)

        def act_v_in(a_, ph, g, src, ready):
            a_.wait_ge(*nth(ready, g + 1))
            for j in range(TPG):
                tile = src[:, g * GW + j * P:g * GW + (j + 1) * P].rearrange("p (b k) -> p b k", b=BPT)
                i = nc.scalar.activation(v_in(g)[:, j, :, :].rearrange("p b (h k) -> p b h k", h=HPG),
                                         tile.unsqueeze(2).broadcast_to([P, BPT, HPG, NQ]), ACT.Copy)
            i.then_inc(sem(ph + "_v_in"), 1)

        def pool_inv_tok(gp, ph, g):
            gp.wait_ge(*nth(ph + "_inv", g + 1))
            for j in range(TPG):
                dst = h[:, g * TPG + j, :].rearrange("p (a h d) -> p a h d", a=HG, h=HPG)
                i = nc.gpsimd.tensor_copy(dst, head_inv[:, g, :, j * HPG:(j + 1) * HPG].unsqueeze(3).broadcast_to([P, HG, HPG, HD]))
            i.then_inc(sem(ph + "_inv_tok"), 1)

        def pool_split_w1(gp, ph, e, slot):
            loads, ups = (16, 8) if ph == "d" else (32, 4)
            w, high, low = w1[:, slot, :], w1_part(slot, 0), w1_part(slot, 1)
            if not (isinstance(e, int) and e < 2):
                gp.wait_ge(*nth(ph + "_up", ups * (e - 1)))
            wait_alone(gp, ph + f"_w1_loaded{slot}", loads // 2 * (e - slot) + loads)
            nc.gpsimd.tensor_copy(high.bitcast(fp32r), w).then_inc(sem(ph + "_w1_high"), 1)
            gp.wait_ge(*nth(ph + "_w1_high", e + 1))
            nc.gpsimd.tensor_tensor(low.bitcast(fp32r), w, high, ALU.subtract).then_inc(sem(ph + "_w1_split"), 1)

        def pool_split_other_w1(gp, ph):
            with gp.Fori(1, NE // 2) as pair_of_experts:
                for slot in range(2):
                    pool_split_w1(gp, ph, 2 * pair_of_experts + slot, slot)

        @block.gpsimd
        def _(gp):
            nc.gpsimd.memset(minus_half[:, :], -0.5)
            nc.gpsimd.memset(ident[:, :], 0.0)
            nc.gpsimd.memset(ones[:, :], 1.0)
            nc.gpsimd.memset(blk[:, :, :], 1.0)
            nc.gpsimd.memset(v_mask[:, :, :, :], 1.0)
            nc.gpsimd.memset(causal4[:, :, :], 0.0)
            nc.gpsimd.memset(e_group16[:, :, :], 1.0)
            nc.gpsimd.memset(e_p_last[:, :, :], 0.0)
            link(gp, "g", nc.gpsimd.memset(last_mask[:, :, :], 1.0))

            def keep(t, pattern, base, chan, fill, op=ALU.is_ge):
                link(gp, "g", nc.gpsimd.affine_select(out=t, in_=t, compare_op=op, fill=fill, base=base,
                                                      pattern=pattern, channel_multiplier=chan))

            keep(ident[:, :], [[-1, P]], 0, 1, 1.0, ALU.not_equal)
            keep(blk[:, :, :], [[-NQ, HG], [-HD, HPG]], 0, 1, 0.0)
            keep(blk[:, :, :], [[NQ, HG], [HD, HPG]], HD - 1, -1, 0.0)
            keep(v_mask[:, :, :, :], [[0, HG], [-NQ, HPG], [0, HD]], 0, 1, 0.0)
            keep(v_mask[:, :, :, :], [[0, HG], [NQ, HPG], [0, HD]], NQ - 1, -1, 0.0)
            keep(causal4[:, :, :], [[-NQ, BPT], [-1, NQ]], 0, 1, NEG)
            keep(causal4[:, :, :], [[-NQ, BPT], [0, NQ]], 0, 1, 0.0)
            keep(last_mask[:, :, :], [[P, TILES], [-NQ, NB]], 0, 1, 0.0)
            keep(last_mask[:, :, :], [[-P, TILES], [NQ, NB]], NQ - 1, -1, 0.0)
            keep(e_group16[:, :, :], [[-HG, BPT], [-1, HG]], 0, 1, 0.0, ALU.is_equal)
            link(gp, "g", nc.gpsimd.iota(iota_i[:, :], pattern=[[1, NE]], base=0, channel_multiplier=0))
            gp.sem_inc(sem("constants"), 1)
            for g in range(GROUPS):
                pool_rstd(gp, "b", g, 1)
            for g in range(GROUPS):
                pool_add_row(gp, "b", g, bo_row, ("b_w_loaded", 16 * 5))
            gp.wait_ge(sem("b_av"), TILES)
            link(gp, "g", nc.gpsimd.memset(before[:, :], 1.0))
            nc.gpsimd.affine_select(out=before[:, :], in_=before[:, :], compare_op=ALU.is_ge, fill=0.0, base=-1,
                                    pattern=[[1, P]], channel_multiplier=-1).then_inc(sem("g_before"), 1)
            for g in range(GROUPS):
                pool_rstd(gp, "c", g, 1)
            for g in range(GROUPS):
                pool_add_row(gp, "c", g, bproj_row, ("c_w_loaded", 16 * 6))
            for g in range(GROUPS):
                pool_inv_tok(gp, "c", g)
            for g in range(GROUPS):
                pool_rstd(gp, "d", g, 2)
            for e in range(2):
                pool_split_w1(gp, "d", e, e)
            for g in range(GROUPS):
                gp.wait_ge(*nth("d_h", g + 1))
                nc.gpsimd.tensor_tensor(gx(x, g), gx(x, g), gx(res, g), ALU.add).then_inc(sem("d_x_res"), 1)
            for g in range(GROUPS):
                gp.wait_ge(*nth("d_x_res", g + 1))
                gp.wait_ge(sem("d_abel"), g + 1)
                nc.gpsimd.tensor_tensor(gx(x, g), gx(x, g), gx(abel, g), ALU.add).then_inc(sem("d_x_abel"), 1)
            pool_split_other_w1(gp, "d")

            def prepare_keys(t, slot, b):
                if not first_batches(t):
                    wait_alone(gp, "e_scores", HG * (BPT * t + (b - BPT + 1)))
                if b == 0:
                    wait_alone(gp, f"e_mask_loaded{slot}", 8 * (t - slot) + 16)
                nc.gpsimd.tensor_scalar(e_keep[:, b, :], e_mask[slot][:, b, :], 0, 0.0, ALU.is_equal, ALU.is_equal)
                if b == 0:
                    nc.gpsimd.tensor_copy(e_last_in[:, slot, :].rearrange("p (b g) -> p b g", b=BPT),
                                          ctxT[:, bass.ds(BPT * t, BPT), LAST:NK].broadcast_to([P, BPT, HG]))
                nc.gpsimd.tensor_copy(e_ctx[:, b, :], ctxT[:, bass.ds(BPT * t + b, 1), 0:LAST].rearrange("p a k -> p (a k)")).then_inc(sem("e_prep"), 1)

            def prepare_queries(t, slot, b):
                nc.gpsimd.tensor_tensor(e_q[:, b, :].rearrange("p (g h q) -> p g h q", g=HG, h=HPG),
                                        qT[:, bass.ds(t * P + b * NQ, NQ)].unsqueeze(1).unsqueeze(1).broadcast_to([P, HG, HPG, NQ]),
                                        blk[:, :, :].unsqueeze(3).broadcast_to([P, HG, HPG, NQ]), ALU.mult).then_inc(sem("e_q"), 1)

            def pool_step(t, slot, b):
                gp.wait_ge(sem("e_exp"), BPT * t + (b + 1))
                nc.gpsimd.tensor_tensor(e_p_last[:, b, b * HG:(b + 1) * HG], e_probs[b][:, :, LAST:NK].rearrange("p g a -> p (g a)"),
                                        ones[:, 0:HG], ALU.mult).then_inc(sem("e_p_last"), 1)
                gp.wait_ge(sem("e_inv"), BPT * t + (b + 1))
                nc.gpsimd.tensor_tensor(e_inv_tok[:, b % 2, :].rearrange("p (g f) -> p g f", g=HG),
                                        e_inv[:, b * HG:(b + 1) * HG].unsqueeze(2).broadcast_to([P, HG, NQ]),
                                        v_mask[:, :, :, :].rearrange("p g h d -> p g (h d)"), ALU.mult).then_inc(sem("e_inv_tok"), 1)
                later(prepare_keys, t, slot, b, 3)
                later(prepare_queries, t, slot, b, 3)

            for b in range(3):
                prepare_keys(0, 0, b)
            for g in range(GROUPS):
                pool_rstd(gp, "e", g, 1)
            gp.wait_ge(*nth("e_qT", GROUPS))
            for b in range(3):
                prepare_queries(0, 0, b)
            for g in range(GROUPS):
                pool_add_row(gp, "e", g, bo1_row, ("e_w_loaded", 16 * 8))
            over_batches(gp, pool_step)
            for g in range(GROUPS):
                pool_rstd(gp, "f", g, 2)
            for e in range(2):
                pool_split_w1(gp, "g", e, e)
            for g in range(GROUPS):
                pool_inv_tok(gp, "f", g)
            for g in range(GROUPS):
                pool_rstd(gp, "f2", g, 1)
            for g in range(GROUPS):
                gp.wait_ge(sem("f_x2"), g + 1)
                nc.gpsimd.tensor_tensor(gx(x, g), gx(x, g), gx(res, g), ALU.add).then_inc(sem("f_x_res"), 1)
            for g in range(GROUPS):
                pool_rstd(gp, "g", g, 1)
            pool_split_other_w1(gp, "g")

        def dve_layer_norm(v, ph, g, src, twice=False):
            t0 = g * TPG
            for j in range(t0, t0 + TPG):
                i = nc.vector.bn_stats(stats[:, j, :], src[:, j, :])
            link(v, "v", i)
            for j in range(t0, t0 + TPG):
                i = nc.vector.bn_aggr(mean_var[:, j, :], stats[:, j, :])
            link(v, "v", i)
            var = mean_var[:, t0:t0 + TPG, 1:2].rearrange("p t a -> p (t a)")
            i = nc.vector.tensor_scalar(var_eps[:, 0, t0:t0 + TPG], var, EPS, None, ALU.add)
            if twice:
                i = nc.vector.tensor_scalar(var_eps[:, 1, t0:t0 + TPG], var, 1.0 + EPS, EPS * EPS, ALU.mult, ALU.add)
            i.then_inc(sem(ph + "_var"), 1)

        def dve_normalise(v, ph, g, src, twice=False):
            t0 = g * TPG
            v.wait_ge(*nth(ph + "_rstd", g + 1))
            for n, dst in (((0, res), (1, h)) if twice else ((0, h),)):
                for j in range(t0, t0 + TPG):
                    i = nc.vector.tensor_scalar(dst[:, j, :], src[:, j, :], mean_var[:, j, 0:1], rstd[:, n, j:j + 1],
                                                ALU.subtract, ALU.mult)
            i.then_inc(sem(ph + "_h"), 1)

        def pe_transpose_group(pe, g, src, k, ready):
            for s, n in ready:
                pe.wait_ge(*nth(s, n))
            for j in range(TPG):
                i = nc.tensor.transpose(group_bank(g, k)[:, j * P:(j + 1) * P], src[:, g * TPG + j, :], ident[:, :])
            return i

        def pe_self_attention(pe, ph, vw):
            for g in range(GROUPS):
                pe.wait_ge(*nth(ph + "_qT", g + 1))
                pe.wait_ge(*nth(ph + "_k_heads", g + 1))
                for j in range(TPG):
                    for a in range(HG):
                        for b in range(BPT):
                            at = g * GW + j * P + b * NQ
                            i = nc.tensor.matmul(group_bank(g, a)[b * NQ:(b + 1) * NQ, j * P:(j + 1) * P],
                                                 qT[a * NQ:(a + 1) * NQ, at:at + NQ],
                                                 k_heads(g)[a * NQ:(a + 1) * NQ, j, b, :],
                                                 start=True, stop=True, tile_position=(a * NQ, b * NQ))
                i.then_inc(sem(ph + "_scores"), 1)
            for g in range(GROUPS):
                pe.wait_ge(*nth(ph + "_v_in", g + 1))
                pe.wait_ge(*nth(ph + "_shifted", HG * (g + 1)))
                for j in range(TPG):
                    for b in range(BPT):
                        i = nc.tensor.matmul(group_bank(g, j)[:, b * P:(b + 1) * P], v_in(g)[:, j, b, :], vw, start=True, stop=True)
                    i.then_inc(sem(ph + "_v"), 1)
            for g in range(GROUPS):
                pe.wait_ge(*nth(ph + "_v_heads", TPG * (g + 1)))
                pe.wait_ge(*nth(ph + "_exp", g + 1))
                for j in range(TPG):
                    for a in range(HG):
                        i = nc.tensor.transpose(group_bank(g, j)[:, a * P:(a + 1) * P], probs(g)[:, a, j, :], ident[:, :])
                    i.then_inc(sem(ph + "_pT"), 1)
            for g in range(GROUPS):
                for j in range(TPG):
                    pe.wait_ge(*nth(ph + "_probsT", g * TPG + TPG))
                    for b in range(BPT):
                        for a in range(HG):
                            at = j * P + b * NQ
                            i = nc.tensor.matmul(group_bank(g, 0)[a * NQ:(a + 1) * NQ, at:at + NQ],
                                                 v_heads(g)[:, j, b, a * NQ:(a + 1) * NQ],
                                                 probsT(g)[:, j, a, b * NQ:(b + 1) * NQ],
                                                 start=True, stop=True, tile_position=(0, a * NQ))
                pe.wait_ge(*nth(ph + "_inv_tok", g + 1))
                for j in range(TPG):
                    i = nc.tensor.transpose(group_bank(g, 1)[:, j * P:(j + 1) * P], h[:, g * TPG + j, :], ident[:, :])
                i.then_inc(sem(ph + "_out"), 1)

        def dve_self_attention(v, ph, causal_mask):
            for g in range(GROUPS):
                dve_k_heads(v, ph, g)
            for g in range(GROUPS):
                v.wait_ge(*nth(ph + "_scores", g + 1))
                for a in range(HG):
                    s = group_bank(g, a)[:, :].rearrange("p (m k) -> p m k", k=NQ)
                    d = probs(g)[:, a, :, :].rearrange("p j n -> p (j n)").rearrange("p (m k) -> p m k", k=NQ)
                    if causal_mask:
                        link(v, "v", nc.vector.tensor_tensor(d, s, causal[:, :].unsqueeze(1).broadcast_to([P, TPG * HPG, NQ]), ALU.add))
                        s = d
                    link(v, "v", nc.vector.tensor_reduce(head_max[:, g, a, :], s, AX, ALU.max))
                    nc.vector.tensor_tensor(d, s, head_max[:, g, a, :].unsqueeze(2).broadcast_to([P, TPG * HPG, NQ]),
                                            ALU.subtract).then_inc(sem(ph + "_shifted"), 1)
            for g in range(GROUPS):
                for j in range(TPG):
                    v.wait_ge(*nth(ph + "_v", g * TPG + j + 1))
                    nc.vector.tensor_tensor(v_heads(g)[:, j, :, :], group_bank(g, j)[:, :].rearrange("p (b n) -> p b n", b=BPT),
                                            v_mask[:, :, :, :].rearrange("p g h d -> p (g h d)").unsqueeze(1).broadcast_to([P, BPT, P]),
                                            ALU.mult).then_inc(sem(ph + "_v_heads"), 1)
            for g in range(GROUPS):
                v.wait_ge(*nth(ph + "_exp", g + 1))
                link(v, "v", nc.vector.tensor_reduce(head_sum[:, g, :, :], r3[:, g * 2048:(g + 1) * 2048].rearrange("p (m k) -> p m k", k=NQ), AX, ALU.add))
                nc.vector.reciprocal(head_inv[:, g, :, :], head_sum[:, g, :, :]).then_inc(sem(ph + "_inv"), 1)
            for g in range(GROUPS):
                v.wait_ge(*nth(ph + "_inv_rows", g + 1))
                nc.vector.tensor_tensor(oT[:, g * GW:(g + 1) * GW], group_bank(g, 0)[:, :], aT[:, g * GW:(g + 1) * GW],
                                        ALU.mult).then_inc(sem(ph + "_oT"), 1)

        def act_self_attention(a_, ph, v_src, v_ready):
            for g in range(GROUPS):
                act_v_in(a_, ph, g, v_src, v_ready)
            for g in range(GROUPS):
                for a in range(HG):
                    a_.wait_ge(*nth(ph + "_shifted", g * HG + a + 1))
                    p = probs(g)[:, a, :, :]
                    i = nc.scalar.activation(p, p, ACT.Exp, scale=HD ** -0.5)
                i.then_inc(sem(ph + "_exp"), 1)
            for g in range(GROUPS):
                for j in range(TPG):
                    a_.wait_ge(*nth(ph + "_pT", g * TPG + j + 1))
                    nc.scalar.activation(probsT(g)[:, j, :, :], group_bank(g, j)[:, :].rearrange("p (a n) -> p a n", a=HG),
                                         ACT.Copy).then_inc(sem(ph + "_probsT"), 1)
            for g in range(GROUPS):
                a_.wait_ge(*nth(ph + "_out", g + 1))
                nc.scalar.activation(aT[:, g * GW:(g + 1) * GW], group_bank(g, 1)[:, :], ACT.Copy).then_inc(sem(ph + "_inv_rows"), 1)

        def dve_split_x(v, ph):
            for g in range(GROUPS):
                high, low = gx(x_part(0), g), gx(x_part(1), g)
                v.wait_ge(*nth(ph + "_hT", g + 1))
                nc.vector.tensor_copy(high.bitcast(fp32r), gx(hT, g)).then_inc(sem(ph + "_x_high"), 1)
                v.wait_ge(*nth(ph + "_x_high", g + 1))
                nc.vector.tensor_tensor(low.bitcast(fp32r), gx(hT, g), high, ALU.subtract).then_inc(sem(ph + "_x_split"), 1)

        def dve_top2(v, ph):
            for t in range(TILES):
                i = nc.vector.max(out=top8[:, t, :], in_=logits[:, t, :])
            link(v, "v", i)
            for t in range(TILES):
                i = nc.vector.max_index(top_index[:, t, :], top8[:, t, :], logits[:, t, :])
            nc.vector.tensor_tensor(top_p[:, 0, :], top8[:, :, 1:2].rearrange("p t a -> p (t a)"), top8[:, :, 0:1].rearrange("p t a -> p (t a)"),
                                    ALU.subtract).then_inc(sem(ph + "_top_diff"), 1)
            v.wait_ge(*nth(ph + "_top_diff", 1))
            link(v, "v", nc.vector.tensor_copy(top_f[:, :, :], top_index[:, :, 0:2]))
            for k in range(2):
                i = nc.vector.tensor_tensor(pick[:, k, :, :], iota8[:, :].unsqueeze(1).broadcast_to([P, TILES, NE]),
                                            top_f[:, :, k:k + 1].broadcast_to([P, TILES, NE]), ALU.is_equal)
            if ph == "g":
                link(v, "v", i)
                nc.vector.tensor_tensor(picked[:, :, :], pick[:, 0, :, :], pick[:, 1, :, :], ALU.add).then_inc(sem("g_picked_before"), 1)
                for t in range(1, TILES):
                    v.wait_ge(sem("g_picked_before"), t)
                    nc.vector.tensor_tensor(picked_before[:, t, :], picked_before[:, t - 1, :], picked[:, t - 1, :], ALU.add).then_inc(sem("g_picked_before"), 1)
            v.wait_ge(*nth(ph + "_top_exp", 1))
            link(v, "v", nc.vector.tensor_scalar(top_p[:, 2, :], top_p[:, 1, :], 1.0, None, ALU.add))
            link(v, "v", nc.vector.reciprocal(top_p[:, 0, :], top_p[:, 2, :]))
            link(v, "v", nc.vector.tensor_tensor(top_p[:, 1, :], top_p[:, 1, :], top_p[:, 0, :], ALU.mult))
            for k in range(2):
                i = nc.vector.tensor_tensor(pick[:, k, :, :], pick[:, k, :, :], top_p[:, k, :].unsqueeze(2).broadcast_to([P, TILES, NE]), ALU.mult)
            link(v, "v", i)

        def dve_accumulate(v, ph, e):
            for g in range(GROUPS):
                v.wait_ge(*nth(ph + "_down", 2 * e + (g + 1)))
                v.wait_ge(*nth(ph + "_acc", 2 * e + (g + 1)))
                for j in range(TPG):
                    t = g * TPG + j
                    i = nc.vector.scalar_tensor_tensor(moe[:, t, :], bank[4 + g][:, j * P:(j + 1) * P],
                                                       w_token[:, :, :].rearrange("p e t -> p (e t)")[:, bass.ds(e * TILES + t, 1)],
                                                       moe[:, t, :], ALU.mult, ALU.add)
                i.then_inc(sem(ph + "_acc"), 1)

        @block.tensor
        def _(pe):
            pe.wait_ge(sem("constants"), 1)
            pe.wait_ge(sem("gen_loaded"), 16)
            for i_ in range(3):
                i = nc.tensor.transpose(bank[4][:, i_ * P:(i_ + 1) * P], gen[:, i_, :], ident[:, :])
            i.then_inc(sem("m_wT_p"), 1)
            pe.wait_ge(*nth("m_wT", 1))

            def pe_expm_step(n):
                if n < ORDER - 1:
                    pe.wait_ge(sem("taylor"), n + 1)
                    for i_ in range(3):
                        i = nc.tensor.matmul(bank[4][:, i_ * P:(i_ + 1) * P], genT[:, i_, :], taylor[:, i_, :], start=True, stop=True)
                    i.then_inc(sem("taylor_p"), 1)
                elif n == ORDER - 1:
                    pe.wait_ge(sem("taylor"), n + 1)
                    for i_ in range(3):
                        i = nc.tensor.transpose(bank[5][:, i_ * P:(i_ + 1) * P], taylor[:, i_, :], ident[:, :])
                    i.then_inc(sem("taylorT_p"), 1)

            pe.wait_ge(sem("w_a_loaded"), 16 * 4)
            for i_ in range(4):
                i = nc.tensor.transpose(bank[0][:, i_ * P:(i_ + 1) * P], w_a[:, i_, :], ident[:, :])
            i.then_inc(sem("b_wT_p"), 1)
            pe_expm_step(0)
            for g in range(GROUPS):
                pe_transpose_group(pe, g, h, 1, [("b_h", g + 1)]).then_inc(sem("b_hT_p"), 1)
            pe_expm_step(1)
            for g in range(GROUPS):
                pe.wait_ge(*nth("b_wT", 1))
                pe.wait_ge(*nth("b_hT", g + 1))
                nc.tensor.matmul(group_bank(g, 2)[:, :], w_aT[:, 0, :], gx(hT, g), start=True, stop=True).then_inc(sem("b_q_p"), 1)
            pe_expm_step(2)
            pe.wait_ge(sem("b_w_loaded"), 16 * 5)
            for g in range(GROUPS):
                pe.wait_ge(*nth("b_qT", g + 1))
                for j in range(TPG):
                    t = g * TPG + j
                    i = nc.tensor.matmul(group_bank(g, 3)[:, j:j + 1], qT[:, t * P:(t + 1) * P], cols[:, BK0:BK0 + 1], start=True, stop=True)
                i.then_inc(sem("b_qbk_p"), 1)
                nc.tensor.matmul(group_bank(g, 1)[:, :], wk0[:, :], gx(qT, g), start=True, stop=True).then_inc(sem("b_q2_p"), 1)
                pe_expm_step(3 + g)
            pe.wait_ge(sem("b_q2"), GROUPS)
            pe.wait_ge(sem("b_qbk"), GROUPS)
            pe.wait_ge(sem("ctx_last_loaded"), 16)
            nc.tensor.transpose(bank[7][:, 0:NB], ctx_last[:, :], ident[0:NB, 0:NB]).then_inc(sem("ctx_last_p"), 1)
            for n in range(NB // 2):
                pe_expm_step(5 + n)
                pe.wait_ge(sem(f"ctx_loaded{2 * n // 8}"), 16 * KC)
                if n >= 4:
                    pe.wait_ge(sem("ctxT_a" if n % 2 == 0 else "ctxT_v"), (n - 4) // 2 + 1 + n % 2)
                for b in range(2):
                    for c in range(KC):
                        i = nc.tensor.transpose(bank[n % 4][:, (b * KC + c) * P:(b * KC + c + 1) * P], ctx_keys[:, 2 * n + b, c, :], ident[:, :])
                i.then_inc(sem("ctxT_p"), 1)
            pe.wait_ge(sem("taylorT"), 1)
            pe.wait_ge(sem("ctxT_a"), NB // 4)
            pe.wait_ge(sem("ctxT_v"), NB // 4 + 1)
            for g in range(GROUPS):
                for j in range(TPG):
                    t = g * TPG + j
                    for b in range(BPT):
                        i = nc.tensor.matmul(group_bank(g, j)[b * NQ:(b + 1) * NQ, 0:NK], kT[:, t * P + b * NQ:t * P + (b + 1) * NQ],
                                             ctxT[:, BPT * t + b, :], start=True, stop=True, tile_position=(0, b * NQ))
                    i.then_inc(sem("b_scores"), 1)
            for t in range(TILES):
                pe.wait_ge(*nth("b_exp", t + 1))
                for c in range(KC):
                    nc.tensor.transpose(bank[t][:, c * P:(c + 1) * P], b_probs(t)[:, c * P:(c + 1) * P], ident[:, :])
                pe.wait_ge(sem("b_last"), t + 1)
                nc.tensor.transpose(bank[t][0:NB, KC * P:KC * P + P], b_last[:, t, :], ident[:, :]).then_inc(sem("b_pT"), 1)
            for t in range(TILES):
                pe.wait_ge(*nth("b_probsT", t + 1))
                nc.tensor.matmul(bank[t][:, 0:D], b_lastT[:, t, :], ctx_last[:, :], start=True, stop=False)
                for c in range(KC):
                    for b in range(BPT):
                        i = nc.tensor.matmul(bank[t][b * NQ:(b + 1) * NQ, 0:D], b_probsT(t)[:, c * P + b * NQ:c * P + (b + 1) * NQ],
                                             ctx_keys[:, BPT * t + b, c, :], start=False, stop=c == KC - 1,
                                             tile_position=(0, b * NQ))
                i.then_inc(sem("b_av"), 1)
            for g in range(GROUPS):
                pe_transpose_group(pe, g, h, 1, [("b_o", TPG * (g + 1))]).then_inc(sem("b_oT_p"), 1)
            for g in range(GROUPS):
                pe.wait_ge(*nth("b_oT", g + 1))
                nc.tensor.matmul(group_bank(g, 2)[:, :], w_aT[:, 1, :], gx(oT, g), start=True, stop=True).then_inc(sem("b_vo_p"), 1)
            for g in range(GROUPS):
                pe.wait_ge(sem("b_voT"), g + 1)
                for j in range(TPG):
                    t = g * TPG + j
                    i = nc.tensor.matmul(group_bank(g, 3)[:, j * P:(j + 1) * P], aT[:, t * P:(t + 1) * P], w_aT[:, 2, :], start=True, stop=True)
                i.then_inc(sem("b_out"), 1)

            pe.wait_ge(sem("c_w_loaded"), 16 * 6)
            for g in range(GROUPS):
                pe_transpose_group(pe, g, h, 0, [("c_h", g + 1)]).then_inc(sem("c_hT_p"), 1)
            for g in range(GROUPS):
                pe.wait_ge(*nth("c_hT", g + 1))
                nc.tensor.matmul(group_bank(g, 1)[:, :], w_qkv[:, D:2 * D], gx(hT, g), start=True, stop=True).then_inc(sem("c_k_p"), 1)
                nc.tensor.matmul(group_bank(g, 2)[:, :], w_qkv[:, 0:D], gx(hT, g), start=True, stop=True).then_inc(sem("c_q_p"), 1)
            for g in range(GROUPS):
                pe.wait_ge(*nth("c_qT", g + 1))
            pe_self_attention(pe, "c", w_qkv[:, 2 * D:3 * D])
            for g in range(GROUPS):
                pe.wait_ge(*nth("c_obT", g + 1))
                for j in range(TPG):
                    t = g * TPG + j
                    i = nc.tensor.matmul(group_bank(g, 2)[:, j * P:(j + 1) * P], oT[:, t * P:(t + 1) * P], w_proj[:, :], start=True, stop=True)
                i.then_inc(sem("c_projected"), 1)

            pe.wait_ge(sem("d_w_loaded"), 160)
            for g in range(GROUPS):
                pe_transpose_group(pe, g, h, 0, [("d_h", g + 1)]).then_inc(sem("d_hT_p"), 1)
            nc.tensor.transpose(group_bank(1, 1)[:, 0:4 * NE], b1_rows[:, :], ident[0:4 * NE, 0:4 * NE]).then_inc(sem("d_wT_p"), 1)
            for g in range(GROUPS):
                pe.wait_ge(*nth("d_hT", g + 1))
                for j in range(TPG):
                    t = g * TPG + j
                    i = nc.tensor.matmul(bank[7][:, t * NE:(t + 1) * NE], hT[:, t * P:(t + 1) * P], gate_w[:, :], start=True, stop=True)
            i.then_inc(sem("d_logits"), 1)
            def up(e, slot, first):
                pe.wait_ge(*nth("d_w1_split", e + 1))
                if first:
                    pe.wait_ge(*nth("d_x_split", GROUPS))
                for n in range(8):
                    if not (first and n < 4):
                        pe.wait_ge(sem("d_gelu"), 8 * e + (n - 3))
                    c, g = n // GROUPS, n % GROUPS
                    split_product(bank[n % 4][:, :], slot, slice(c * P, (c + 1) * P), g).then_inc(sem("d_up"), 1)

            def down(e, slot):
                pe.wait_ge(*nth(f"d_w2_loaded{slot}", 8 * (e - slot) + 16))
                pe.wait_ge(sem("d_gelu"), 8 * e + 8)
                for g in range(GROUPS):
                    pe.wait_ge(*nth("d_acc", 2 * e + g + 1))
                    for j in range(TPG):
                        t = g * TPG + j
                        for c in range(4):
                            i = nc.tensor.matmul(bank[4 + g][:, j * P:(j + 1) * P], hidden(slot)[:, c, t * P:(t + 1) * P], w2[:, slot, c, :],
                                                 start=c == 0, stop=c == 3)
                    i.then_inc(sem("d_down"), 1)

            def squaring(k):
                pe.wait_ge(sem("taylor"), k + (ORDER - 1))
                pe.wait_ge(sem("taylorT"), k + 0)
                for i_ in range(3):
                    i = nc.tensor.matmul(bank[6][:, i_ * P:(i_ + 1) * P], taylorT[:, i_, :], taylor[:, i_, :], start=True, stop=True)
                i.then_inc(sem("taylor_p"), 1)
                for i_ in range(3):
                    i = nc.tensor.matmul(bank[7][:, i_ * P:(i_ + 1) * P], taylor[:, i_, :], taylorT[:, i_, :], start=True, stop=True)
                i.then_inc(sem("taylorT_p"), 1)

            up(0, 0, True)
            for g in range(GROUPS):
                pe.wait_ge(*nth("d_wT", 1))
                for j in range(TPG):
                    t = g * TPG + j
                    i = nc.tensor.matmul(bank[5 + g][:, j * P:(j + 1) * P], hT[:, t * P:(t + 1) * P], abel_w[:, :], start=True, stop=True)
                i.then_inc(sem("d_abel_p"), 1)
            up(1, 1, False)
            pe.wait_ge(sem("d_w_token"), 1)
            for g in range(GROUPS):
                for j in range(TPG):
                    t = g * TPG + j
                    i = nc.tensor.transpose(bank[(4, 7)[g]][0:NE, j * P:(j + 1) * P], w_token[:, :, t], ident[:, :])
                i.then_inc(sem("d_w_tokenT_p"), 1)
            for g in range(GROUPS):
                pe.wait_ge(sem("d_abel_s"), g + 1)
                pe.wait_ge(sem("d_w_tokenT"), g + 1)
                for j in range(TPG):
                    t = g * TPG + j
                    i = nc.tensor.matmul(bank[5 + g][:, j * P:(j + 1) * P], w_tokenT[:, t * P:(t + 1) * P], b2_rows[:, :], start=True, stop=True)
                i.then_inc(sem("d_moe_b2"), 1)
            pe.wait_ge(*nth("d_acc", GROUPS))
            down(0, 0)
            with pe.Fori(1, NE // 2) as pair_of_experts:
                e = 2 * pair_of_experts
                up(e, 0, False)
                squaring(pair_of_experts)
                down(e - 1, 1)
                up(e + 1, 1, False)
                down(e, 0)
            pe.wait_ge(sem("taylor"), ORDER + SQUARINGS)
            pe.wait_ge(sem("taylorT"), SQUARINGS + 1)
            nc.tensor.matmul(bank[6][:, 0:P], taylorT[:, 1, :], taylor[:, 2, :], start=True, stop=True).then_inc(sem("taylor_p"), 1)
            down(NE - 1, 1)
            pe.wait_ge(sem("pair"), 1)
            nc.tensor.matmul(bank[6][:, 0:P], taylorT[:, 0, :], pair[:, :], start=True, stop=True).then_inc(sem("taylor_p"), 1)
            for g in range(GROUPS):
                pe_transpose_group(pe, g, moe, 3, [("d_acc", 2 * NE + g + 1)]).then_inc(sem("d_moeT_p"), 1)
            pe.wait_ge(sem("rot"), 1)
            for g in range(GROUPS):
                pe.wait_ge(sem("d_moeT"), g + 1)
                for j in range(TPG):
                    t = g * TPG + j
                    i = nc.tensor.matmul(group_bank(g, 2)[:, j * P:(j + 1) * P], moeT[:, t * P:(t + 1) * P], rot[:, :], start=True, stop=True)
                i.then_inc(sem("d_nonabel"), 1)

            pe.wait_ge(sem("e_w_loaded"), 16 * 8)

            def keys(t, slot, b):
                pe.wait_ge(sem("e_v"), BPT * t + (b + 1))
                nc.tensor.matmul(bank[4][:, 0:NK], w_e[:, 1, :], ctxT[:, bass.ds(BPT * t + b, 1), :].rearrange("p a k -> p (a k)"),
                                 start=True, stop=True).then_inc(sem("e_k_p"), 1)

            def values(t, slot, b):
                pe.wait_ge(sem("e_prep"), BPT * t + (b + 1))
                if not (first_batches(t) and b == 0):
                    pe.wait_ge(sem("e_k"), BPT * t + b)
                for c in range(KC):
                    i = nc.tensor.matmul(bank[4][:, c * D:(c + 1) * D], e_ctx[:, b, c * P:(c + 1) * P], w_e[:, 2, :], start=True, stop=True)
                i.then_inc(sem("e_v_p"), 1)

            def last_values(t, slot, b):
                if b == 0:
                    nc.tensor.matmul(bank[7][0:BPT * HG, 3 * P:4 * P], e_last_in[:, slot, :], w_e[:, 2, :], start=True, stop=True).then_inc(sem("e_v_last_p"), 1)

            def scores(t, slot, b):
                pe.wait_ge(sem("e_k"), BPT * t + (b + 1))
                pe.wait_ge(sem("e_q"), BPT * t + (b + 1))
                if not (first_batches(t) and b == 0):
                    pe.wait_ge(sem("e_masked"), BPT * t + b)
                for g in range(HG):
                    nc.tensor.matmul(bank[g][:, 0:NK], e_q[:, b, g * P:(g + 1) * P], e_k[:, b, :], start=True, stop=True).then_inc(sem("e_scores"), 1)

            def transpose_probs(t, slot, b):
                pe.wait_ge(sem("e_p_last"), BPT * t + (b + 1))
                if not (first_batches(t) and b == 0):
                    pe.wait_ge(sem("e_done"), BPT * t + b)
                nc.tensor.transpose(bank[7][0:BPT * HG, 2 * P:3 * P], e_p_last[:, b, :], ident[:, :]).then_inc(sem("e_p_last_p"), 1)
                pe.wait_ge(sem("e_exp"), BPT * t + (b + 1))
                for c in range(KC):
                    if not (first_batches(t) and b == 0):
                        pe.wait_ge(sem(("e_pT_a", "e_pT_v")[c]), BPT * t + b)
                    for g in range(HG):
                        i = nc.tensor.transpose(bank[5 + c][:, g * P:(g + 1) * P], e_probs[b][:, g, c * P:(c + 1) * P], ident[:, :])
                    i.then_inc(sem(f"e_pT{c}"), 1)

            def outputs(t, slot, b):
                if first_batches(t) and b == 0:
                    pe.wait_ge(sem("e_v_last"), 1)
                nc.tensor.matmul(bank[7][:, 0:P], e_v_last[:, slot, :], e_p_lastT[:, b % 2, :], start=True, stop=False)
                pe.wait_ge(sem("e_v"), BPT * t + (b + 1))
                for c in range(KC):
                    pe.wait_ge(sem(("e_pT_a", "e_pT_v")[c]), BPT * t + (b + 1))
                    for g in range(HG):
                        nc.tensor.matmul(bank[7][g * NQ:(g + 1) * NQ, 0:P], e_v[:, b, c, g * NQ:(g + 1) * NQ],
                                         e_probsT[b % 2][:, c, g, :], start=False, stop=c == KC - 1, tile_position=(0, g * NQ))
                pe.wait_ge(sem("e_inv_tok"), BPT * t + (b + 1))
                nc.tensor.transpose(bank[7][:, P:2 * P], e_inv_tok[:, b % 2, :], ident[:, :]).then_inc(sem("e_out"), 1)

            def pe_step(t, slot, b):
                later(scores, t, slot, b, 1)
                later(values, t, slot, b, 2)
                transpose_probs(t, slot, b)
                later(keys, t, slot, b, 2)
                pe.wait_ge(sem("e_p_lastT"), BPT * t + (b + 1))
                if b == 2:
                    later(last_values, t, slot, b, 2)
                outputs(t, slot, b)

            values(0, 0, 0)
            keys(0, 0, 0)
            for g in range(GROUPS):
                pe_transpose_group(pe, g, h, 2, [("e_h", g + 1)]).then_inc(sem("e_hT_p"), 1)
            for g in range(GROUPS):
                pe.wait_ge(*nth("e_hT", g + 1))
                nc.tensor.matmul(group_bank(g, 1)[:, :], w_e[:, 0, :], gx(hT, g), start=True, stop=True).then_inc(sem("e_q_p"), 1)
            values(0, 0, 1)
            last_values(0, 0, 0)
            keys(0, 0, 1)
            pe.wait_ge(*nth("e_qT", GROUPS))
            scores(0, 0, 0)
            over_batches(pe, pe_step)
            for g in range(GROUPS):
                pe.wait_ge(*nth("e_obT", g + 1))
                for j in range(TPG):
                    t = g * TPG + j
                    i = nc.tensor.matmul(group_bank(g, 0)[:, j * P:(j + 1) * P], oT[:, t * P:(t + 1) * P], w_e[:, 3, :], start=True, stop=True)
                i.then_inc(sem("e_projected"), 1)

            pe.wait_ge(sem("f_w_loaded"), 16 * 9)
            for i_ in range(3):
                i = nc.tensor.transpose(bank[2][:, i_ * P:(i_ + 1) * P], w_b[:, i_, :], ident[:, :])
            i.then_inc(sem("f_wT_p"), 1)
            for i_ in range(4):
                i = nc.tensor.transpose(bank[3][:, i_ * P:(i_ + 1) * P], f_k[:, i_, :], ident[:, :])
            i.then_inc(sem("f_wT_p"), 1)
            for g in range(GROUPS):
                pe_transpose_group(pe, g, h, 1, [("f_h", g + 1)]).then_inc(sem("f_hT_p"), 1)
            pe.wait_ge(*nth("f_wT", 2))
            for g in range(GROUPS):
                pe.wait_ge(*nth("f_hT", g + 1))
                for j in range(TPG):
                    t = g * TPG + j
                    nc.tensor.matmul(group_bank(g, j)[:, 0:3 * D], hT[:, t * P:(t + 1) * P], w_bT[:, 0:3, :].rearrange("p i n -> p (i n)"),
                                     start=True, stop=True).then_inc(sem("f_scores3"), 1)
            for g in range(GROUPS):
                pe.wait_ge(sem("f_patterns"), g + 1)
                for k in range(3):
                    for j in range(TPG):
                        i = nc.tensor.transpose(group_bank(g, k)[:, j * P:(j + 1) * P], patterns(g)[:, j, k, :], ident[:, :])
                    i.then_inc(sem("f_patterns_T"), 1)
            for g in range(GROUPS):
                pe.wait_ge(sem("f_aqT"), g + 1)
                nc.tensor.matmul(group_bank(g, 3)[:, :], w_v[:, 0, :], gx(hT, g), start=True, stop=True).then_inc(sem("f_q_p"), 1)
                pe.wait_ge(sem("f_akT"), g + 1)
                nc.tensor.matmul(group_bank(g, 0)[:, :], w_v[:, 1, :], gx(aT, g), start=True, stop=True).then_inc(sem("f_k_p"), 1)
            for g in range(GROUPS):
                pe.wait_ge(*nth("f_qT", g + 1))
                pe.wait_ge(*nth("f_kT", g + 1))
            pe_self_attention(pe, "f", w_v[:, 2, :])
            for g in range(GROUPS):
                pe.wait_ge(*nth("f_oT", g + 1))
                for j in range(TPG):
                    t = g * TPG + j
                    i = nc.tensor.matmul(group_bank(g, 2)[:, j * P:(j + 1) * P], oT[:, t * P:(t + 1) * P], w_aT[:, 3, :], start=True, stop=True)
                i.then_inc(sem("f_p_scores"), 1)
            for g in range(GROUPS):
                pe.wait_ge(sem("f_p_exp"), g + 1)
                for j in range(TPG):
                    i = nc.tensor.transpose(group_bank(g, 3)[:, j * P:(j + 1) * P], p_probs(g)[:, j, :], ident[:, :])
                i.then_inc(sem("f_pp_T_p"), 1)
            for g in range(GROUPS):
                pe.wait_ge(sem("f_ppT"), g + 1)
                for j in range(TPG):
                    t = g * TPG + j
                    i = nc.tensor.matmul(group_bank(g, 0)[:, j * P:(j + 1) * P], aT[:, t * P:(t + 1) * P], w_v[:, 3, :], start=True, stop=True)
                i.then_inc(sem("f_p_out"), 1)
            for g in range(GROUPS):
                pe_transpose_group(pe, g, h, 1, [("f2_h", g + 1)]).then_inc(sem("f2_hT_p"), 1)
            for g in range(GROUPS):
                pe.wait_ge(*nth("f2_hT", g + 1))
                for j in range(TPG):
                    t = g * TPG + j
                    nc.tensor.matmul(group_bank(g, j)[:, :], hT[:, t * P:(t + 1) * P], f_kT, start=True, stop=True).then_inc(sem("f_f_scores"), 1)
            for g in range(GROUPS):
                for j in range(TPG):
                    pe.wait_ge(sem("f_f_exp"), g * TPG + j + 1)
                    for c in range(4):
                        i = nc.tensor.transpose(group_bank(g, j)[:, c * P:(c + 1) * P], f_probs(g)[:, j, c, :], ident[:, :])
                    i.then_inc(sem("f_f_T"), 1)
            for g in range(GROUPS):
                pe.wait_ge(sem("f_fT"), TPG * (g + 1))
                for j in range(TPG):
                    for c in range(4):
                        i = nc.tensor.matmul(group_bank(g, 0)[:, j * P:(j + 1) * P], probsT(g)[:, j, c, :], f_v[:, c, :], start=c == 0, stop=c == 3)
                i.then_inc(sem("f_f_out"), 1)

            pe.wait_ge(sem("g_w_loaded"), 32)
            nc.tensor.transpose(bank[2][:, 0:NE], router_rows[:, :], ident[0:NE, 0:NE]).then_inc(sem("g_wT_p"), 1)
            for g in range(GROUPS):
                pe_transpose_group(pe, g, h, 1, [("g_h", g + 1)]).then_inc(sem("g_hT_p"), 1)
            pe.wait_ge(*nth("g_wT", 1))
            for g in range(GROUPS):
                pe.wait_ge(*nth("g_hT", g + 1))
                for j in range(TPG):
                    t = g * TPG + j
                    i = nc.tensor.matmul(bank[7][:, t * NE:(t + 1) * NE], hT[:, t * P:(t + 1) * P], routerT[:, :], start=True, stop=True)
            i.then_inc(sem("g_logits"), 1)
            def gated_up(e, slot, first):
                pe.wait_ge(*nth("g_w1_split", e + 1))
                if first:
                    pe.wait_ge(*nth("g_x_split", GROUPS))
                for n in range(4):
                    if not (first and n < 2):
                        pe.wait_ge(sem("g_hidden"), 4 * e + (n - 1))
                    c, g = n // GROUPS, n % GROUPS
                    for i_ in range(2):
                        i = split_product(bank[2 * (n % 2) + i_][:, :], slot, slice(i_ * DH + c * P, i_ * DH + (c + 1) * P), g)
                    i.then_inc(sem("g_up"), 1)

            def gated_down(e, slot):
                pe.wait_ge(*nth(f"g_w2_loaded{slot}", 8 * (e - slot) + 16))
                pe.wait_ge(sem("g_hidden"), 4 * e + 4)
                for g in range(GROUPS):
                    pe.wait_ge(*nth("g_acc", 2 * e + (g + 1)))
                    for j in range(TPG):
                        t = g * TPG + j
                        for c in range(2):
                            i = nc.tensor.matmul(bank[4 + g][:, j * P:(j + 1) * P], hidden(slot)[:, c, t * P:(t + 1) * P], w2[:, slot, c, :],
                                                 start=c == 0, stop=c == 1)
                    i.then_inc(sem("g_down"), 1)

            gated_up(0, 0, True)
            pe.wait_ge(sem("g_before"), 1)
            pe.wait_ge(sem("g_picked_before"), TILES)
            nc.tensor.matmul(bank[6][:, 0:TILES * NE], before[:, :], picked[:, :, :].rearrange("p t e -> p (t e)"), start=True, stop=False)
            nc.tensor.matmul(bank[6][:, 0:TILES * NE], ones[:, :], picked_before[:, :, :].rearrange("p t e -> p (t e)"),
                             start=False, stop=True).then_inc(sem("g_rank"), 1)
            gated_up(1, 1, False)
            gated_down(0, 0)
            with pe.Fori(1, NE // 2) as pair_of_experts:
                e = 2 * pair_of_experts
                gated_up(e, 0, False)
                gated_down(e - 1, 1)
                gated_up(e + 1, 1, False)
                gated_down(e, 0)
            gated_down(NE - 1, 1)

        @block.scalar
        def _(a_):
            def out_of_bank(dst, src, wait, done, bias=None, scale=None):
                a_.wait_ge(*nth(wait[0], wait[1]))
                if bias is None and scale is None:
                    i = nc.scalar.activation(dst, src, ACT.Copy)
                else:
                    i = nc.scalar.activation(dst, src, ACT.Identity, bias=bias if bias is not None else 0.0,
                                             scale=scale if scale is not None else 1.0)
                i.then_inc(sem(done), 1)

            out_of_bank(genT[:, :, :], bank[4][:, 0:3 * P].rearrange("p (i n) -> p i n", i=3), ("m_wT_p", 1), "m_wT")
            out_of_bank(w_aT[:, :, :], bank[0][:, :].rearrange("p (i n) -> p i n", i=4), ("b_wT_p", 1), "b_wT")
            for g in range(GROUPS):
                out_of_bank(gx(hT, g), group_bank(g, 1)[:, :], ("b_hT_p", g + 1), "b_hT")
            a_.wait_ge(sem("b_w_loaded"), 16 * 5)
            for g in range(GROUPS):
                out_of_bank(gx(qT, g), group_bank(g, 2)[:, :], ("b_q_p", g + 1), "b_qT", bias=cols[:, BQ0:BQ0 + 1])
            for g in range(GROUPS):
                out_of_bank(gx(kT, g), group_bank(g, 1)[:, :], ("b_q2_p", g + 1), "b_q2")
            for n in range(0, NB // 2, 2):
                if n == ORDER - 4:
                    out_of_bank(taylorT[:, :, :], bank[5][:, 0:3 * P].rearrange("p (i n) -> p i n", i=3), ("taylorT_p", 1), "taylorT")
                out_of_bank(ctxT[:, 2 * n:2 * n + 2, 0:LAST], bank[n % 4][:, :].rearrange("p (b k) -> p b k", b=2), ("ctxT_p", n + 1), "ctxT_a")
            for t in range(TILES):
                a_.wait_ge(sem("b_max"), t + 1)
                nc.scalar.activation(b_probs(t), b_probs(t), ACT.Exp, bias=row_max[:, TILES + t:TILES + t + 1], scale=D ** -0.5,
                                     accum_out=row_sum[:, t:t + 1]).then_inc(sem("b_exp"), 1)
            for t in range(TILES):
                a_.wait_ge(sem("b_lastT"), t + 1)
                out_of_bank(b_probsT(t), bank[t][:, 0:LAST], ("b_pT", t + 1), "b_probsT")
            for t in range(TILES):
                a_.wait_ge(*nth("b_inv", t + 1))
                out_of_bank(h[:, t, :], bank[t][:, 0:D], ("b_av", t + 1), "b_o", scale=row_inv[:, t:t + 1])
            for g in range(GROUPS):
                out_of_bank(gx(oT, g), group_bank(g, 1)[:, :], ("b_oT_p", g + 1), "b_oT")
            for g in range(GROUPS):
                out_of_bank(gx(aT, g), group_bank(g, 2)[:, :], ("b_vo_p", g + 1), "b_voT", bias=cols[:, BV0:BV0 + 1])

            a_.wait_ge(sem("c_w_loaded"), 16 * 6)
            for g in range(GROUPS):
                out_of_bank(gx(hT, g), group_bank(g, 0)[:, :], ("c_hT_p", g + 1), "c_hT")
            for g in range(GROUPS):
                out_of_bank(gx(kT, g), group_bank(g, 1)[:, :], ("c_k_p", g + 1), "c_kT", bias=cols[:, BK:BK + 1])
                out_of_bank(gx(qT, g), group_bank(g, 2)[:, :], ("c_q_p", g + 1), "c_qT", bias=cols[:, BQ:BQ + 1])
            act_self_attention(a_, "c", hT, "c_hT")
            for g in range(GROUPS):
                a_.wait_ge(*nth("c_oT", g + 1))
                nc.scalar.activation(gx(oT, g), gx(oT, g), ACT.Identity, bias=cols[:, BV:BV + 1]).then_inc(sem("c_obT"), 1)

            a_.wait_ge(sem("d_w_loaded"), 160)
            for g in range(GROUPS):
                out_of_bank(gx(hT, g), group_bank(g, 0)[:, :], ("d_hT_p", g + 1), "d_hT", bias=cols[:, LN_B:LN_B + 1], scale=cols[:, LN_G:LN_G + 1])
            out_of_bank(b1_cols[:, :], group_bank(1, 1)[:, 0:4 * NE], ("d_wT_p", 1), "d_wT")
            def gelu(e, slot):
                nc.scalar.activation(b1_now[:, slot, :], b1_cols[:, bass.ds(4 * e, 4)], ACT.Copy).then_inc(sem("b1_now"), 1)
                a_.wait_ge(sem("b1_now"), e + 1)
                for n in range(8):
                    c, g = n // GROUPS, n % GROUPS
                    a_.wait_ge(*nth("d_up", 8 * e + (n + 1)))
                    nc.scalar.activation(hidden(slot)[:, c, g * GW:(g + 1) * GW], bank[n % 4][:, :], ACT.Gelu,
                                         bias=b1_now[:, slot, c:c + 1]).then_inc(sem("d_gelu"), 1)

            a_.wait_ge(*nth("d_wT", 1))
            a_.wait_ge(*nth("d_top_diff", 1))
            nc.scalar.activation(top_p[:, 1, :], top_p[:, 0, :], ACT.Exp).then_inc(sem("d_top_exp"), 1)
            gelu(0, 0)
            gelu(1, 1)
            for g in range(GROUPS):
                out_of_bank(w_tokenT[:, g * GW:(g + 1) * GW], bank[(4, 7)[g]][0:NE, :], ("d_w_tokenT_p", g + 1), "d_w_tokenT")
            for g in range(GROUPS):
                a_.wait_ge(sem("d_abel_s"), g + 1)
                nc.scalar.activation(gx(abel, g), gx(abel, g), ACT.Gelu).then_inc(sem("d_abel"), 1)
            with a_.Fori(1, NE // 2) as pair_of_experts:
                e = 2 * pair_of_experts
                gelu(e, 0)
                a_.wait_ge(sem("taylorT_p"), pair_of_experts + 1)
                nc.scalar.activation(taylorT[:, :, :], bank[7][:, 0:3 * P].rearrange("p (i n) -> p i n", i=3), ACT.Copy).then_inc(sem("taylorT"), 1)
                gelu(e + 1, 1)
            for g in range(GROUPS):
                out_of_bank(gx(moeT, g), group_bank(g, 3)[:, :], ("d_moeT_p", g + 1), "d_moeT")
            a_.wait_ge(sem("d_mix_z"), 1)
            nc.scalar.activation(mix_g[:, :], mix_z[:, 2, :], ACT.Sigmoid, bias=mix_b[:, 0:1]).then_inc(sem("d_mix_g"), 1)

            def values_out(t, slot, b):
                a_.wait_ge(sem("e_v_p"), BPT * t + (b + 1))
                nc.scalar.activation(e_v[:, b, :, :], bank[4][:, 0:LAST].rearrange("p (c d) -> p c d", c=KC), ACT.Copy).then_inc(sem("e_v"), 1)

            def exps(t, slot, b):
                a_.wait_ge(sem("e_masked"), BPT * t + (b + 1))
                for g in range(HG):
                    n = b * HG + g
                    i = nc.scalar.activation(e_probs[b][:, g, :], e_probs[b][:, g, :], ACT.Exp, bias=e_nmax[:, n:n + 1], scale=HD ** -0.5,
                                             accum_out=e_sum[:, n:n + 1])
                i.then_inc(sem("e_exp"), 1)

            def act_step(t, slot, b):
                later(values_out, t, slot, b, 2)
                a_.wait_ge(sem("e_p_last_p"), BPT * t + (b + 1))
                nc.scalar.activation(e_p_lastT[:, b % 2, :], bank[7][0:BPT * HG, 2 * P:3 * P], ACT.Copy).then_inc(sem("e_p_lastT"), 1)
                a_.wait_ge(sem("e_pT0"), BPT * t + (b + 1))
                nc.scalar.activation(e_probsT[b % 2][:, 0, :, :], bank[5][:, :].rearrange("p (g n) -> p g n", g=HG), ACT.Copy).then_inc(sem("e_pT_a"), 1)
                later(exps, t, slot, b, 1)

            values_out(0, 0, 0)
            for g in range(GROUPS):
                out_of_bank(gx(hT, g), group_bank(g, 2)[:, :], ("e_hT_p", g + 1), "e_hT")
            for g in range(GROUPS):
                out_of_bank(gx(qT, g), group_bank(g, 1)[:, :], ("e_q_p", g + 1), "e_qT", bias=cols[:, BQ1:BQ1 + 1])
            values_out(0, 0, 1)
            exps(0, 0, 0)
            over_batches(a_, act_step)
            for g in range(GROUPS):
                a_.wait_ge(sem("e_done"), BPT * TPG * (g + 1))
                nc.scalar.activation(gx(oT, g), gx(oT, g), ACT.Identity, bias=cols[:, BV1:BV1 + 1]).then_inc(sem("e_obT"), 1)

            out_of_bank(w_bT[:, 0:3, :], bank[2][:, 0:3 * P].rearrange("p (i n) -> p i n", i=3), ("f_wT_p", 1), "f_wT")
            out_of_bank(f_kT, bank[3][:, :], ("f_wT_p", 2), "f_wT")
            for g in range(GROUPS):
                out_of_bank(gx(hT, g), group_bank(g, 1)[:, :], ("f_hT_p", g + 1), "f_hT")
            for g in range(GROUPS):
                a_.wait_ge(sem("f_max3"), g + 1)
                for j in range(TPG):
                    t = g * TPG + j
                    for k in range(3):
                        i = nc.scalar.activation(patterns(g)[:, j, k, :], group_bank(g, j)[:, k * D:(k + 1) * D], ACT.Exp,
                                                 bias=f_nmax[:, k, t:t + 1], scale=D ** -0.5, accum_out=f_sum[:, k, t:t + 1])
                i.then_inc(sem("f_exp3"), 1)
            for g in range(GROUPS):
                for k, (dst, name) in enumerate(((hT, "f_aqT"), (aT, "f_akT"), (oT, "f_vT"))):
                    out_of_bank(gx(dst, g), group_bank(g, k)[:, :], ("f_patterns_T", 3 * g + k + 1), name)
            for g in range(GROUPS):
                out_of_bank(gx(qT, g), group_bank(g, 3)[:, :], ("f_q_p", g + 1), "f_qT")
                out_of_bank(gx(kT, g), group_bank(g, 0)[:, :], ("f_k_p", g + 1), "f_kT")
            act_self_attention(a_, "f", oT, "f_vT")
            for g in range(GROUPS):
                a_.wait_ge(sem("f_p_max"), g + 1)
                for j in range(TPG):
                    t = g * TPG + j
                    i = nc.scalar.activation(p_probs(g)[:, j, :], group_bank(g, 2)[:, j * D:(j + 1) * D], ACT.Exp,
                                             bias=f_nmax[:, 3, t:t + 1], scale=D ** -0.5, accum_out=f_sum[:, 3, t:t + 1])
                i.then_inc(sem("f_p_exp"), 1)
            for g in range(GROUPS):
                out_of_bank(gx(aT, g), group_bank(g, 3)[:, :], ("f_pp_T_p", g + 1), "f_ppT")
            for g in range(GROUPS):
                out_of_bank(gx(hT, g), group_bank(g, 1)[:, :], ("f2_hT_p", g + 1), "f2_hT")
            for g in range(GROUPS):
                for j in range(TPG):
                    t = g * TPG + j
                    a_.wait_ge(sem("f_f_max"), t + 1)
                    nc.scalar.activation(f_probs(g)[:, j, :, :].rearrange("p c n -> p (c n)"), group_bank(g, j)[:, :], ACT.Exp,
                                         bias=f_nmax[:, 4, t:t + 1], scale=D ** -0.5, accum_out=f_sum[:, 4, t:t + 1]).then_inc(sem("f_f_exp"), 1)
            for g in range(GROUPS):
                for j in range(TPG):
                    out_of_bank(probsT(g)[:, j, :, :], group_bank(g, j)[:, :].rearrange("p (c n) -> p c n", c=4), ("f_f_T", g * TPG + j + 1), "f_fT")

            out_of_bank(routerT[:, :], bank[2][:, 0:NE], ("g_wT_p", 1), "g_wT")
            for g in range(GROUPS):
                out_of_bank(gx(hT, g), group_bank(g, 1)[:, :], ("g_hT_p", g + 1), "g_hT")
            a_.wait_ge(*nth("g_top_diff", 1))
            nc.scalar.activation(top_p[:, 1, :], top_p[:, 0, :], ACT.Exp).then_inc(sem("g_top_exp"), 1)
            with a_.Fori(0, NE // 2) as pair_of_experts:
                for k in range(8):
                    n = k % 4
                    a_.wait_ge(*nth("g_up", 8 * pair_of_experts + (k + 1)))
                    nc.scalar.activation(silu_b(n), bank[2 * (n % 2) + 1][:, :], ACT.Silu).then_inc(sem("g_silu"), 1)

        @block.vector
        def _(v):
            eye3 = ident[:, :].unsqueeze(1).broadcast_to([P, 3, D])
            bank3 = bank[4][:, 0:3 * P].rearrange("p (i n) -> p i n", i=3)

            def dve_expm_step(n):
                if n == 0:
                    v.wait_ge(sem("gen_loaded"), 16)
                    nc.vector.scalar_tensor_tensor(taylor[:, :, :], gen[:, :, :], 1.0 / (ORDER << SQUARINGS), eye3, ALU.mult, ALU.add).then_inc(sem("taylor"), 1)
                elif n < ORDER:
                    v.wait_ge(sem("taylor_p"), n)
                    nc.vector.scalar_tensor_tensor(taylor[:, :, :], bank3, 1.0 / ((ORDER - n) << SQUARINGS), eye3, ALU.mult, ALU.add).then_inc(sem("taylor"), 1)

            v.wait_ge(sem("x_loaded"), 16)
            for g in range(GROUPS):
                dve_layer_norm(v, "b", g, x)
            v.wait_ge(sem("constants"), 1)
            dve_expm_step(0)
            for g in range(GROUPS):
                dve_normalise(v, "b", g, x)
            dve_expm_step(1)
            link(v, "v", nc.vector.tensor_reduce(head_mask[:, :], blk[:, :, :].rearrange("p g h -> p h g"), AX, ALU.add))
            link(v, "v", nc.vector.tensor_reduce(causal[:, :], causal4[:, :, :].rearrange("p b k -> p k b"), AX, ALU.add))
            i = nc.vector.tensor_copy(iota8[:, :], iota_i[:, :])
            link(v, "v", nc.vector.tensor_reduce(e_group[:, :], e_group16[:, :, :].rearrange("p b g -> p g b"), AX, ALU.add))
            dve_expm_step(2)
            dve_expm_step(3)
            for g in range(GROUPS):
                v.wait_ge(sem("b_qbk_p"), g + 1)
                nc.vector.tensor_copy(q_bk[:, g * TPG:(g + 1) * TPG], group_bank(g, 3)[:, 0:TPG]).then_inc(sem("b_qbk"), 1)
                dve_expm_step(4 + g)
            v.wait_ge(sem("b_qbk"), GROUPS)
            v.wait_ge(sem("ctx_last_p"), 1)
            nc.vector.tensor_copy(ctxT[:, :, LAST:NK].rearrange("p b a -> p (b a)"), bank[7][:, 0:NB]).then_inc(sem("ctxT_v"), 1)
            for n in range(0, NB // 2):
                dve_expm_step(6 + n)
                if n % 2 == 0:
                    continue
                v.wait_ge(sem("ctxT_p"), n + 1)
                nc.vector.tensor_copy(ctxT[:, 2 * n:2 * n + 2, 0:LAST], bank[n % 4][:, :].rearrange("p (b k) -> p b k", b=2)).then_inc(sem("ctxT_v"), 1)
            v.wait_ge(sem("mask0_loaded"), 16)
            link(v, "v", nc.vector.tensor_scalar(b_mask, b_mask.bitcast(i32), 0, NEG, ALU.is_equal, ALU.mult))
            masked_at, max_at = {}, {}
            for t in range(TILES + 2):
                if t < TILES:
                    v.wait_ge(*nth("b_scores", t + 1))
                    masked_at[t] = mark("v", nc.vector.scalar_tensor_tensor(b_probs(t), bank[t][:, 0:NK], q_bk[:, t:t + 1], b_mask[:, t, :], ALU.add, ALU.add))
                if 1 <= t <= TILES:
                    v.wait_ge(sem("step_v"), masked_at[t - 1])
                    max_at[t - 1] = mark("v", nc.vector.tensor_reduce(row_max[:, t - 1:t], b_probs(t - 1), AX, ALU.max))
                if t >= 2:
                    v.wait_ge(sem("step_v"), max_at[t - 2])
                    nc.vector.tensor_scalar(row_max[:, TILES + t - 2:TILES + t - 1], row_max[:, t - 2:t - 1], -D ** -0.5, None, ALU.mult).then_inc(sem("b_max"), 1)
            for t in range(TILES):
                v.wait_ge(*nth("b_exp", t + 1))
                nc.vector.tensor_scalar(b_last[:, t, :], last_mask[:, t, :], b_probs(t)[:, LAST:NK], None, ALU.mult).then_inc(sem("b_last"), 1)
                nc.vector.reciprocal(row_inv[:, t:t + 1], row_sum[:, t:t + 1]).then_inc(sem("b_inv"), 1)
            for t in range(TILES):
                v.wait_ge(*nth("b_pT", t + 1))
                nc.vector.tensor_copy(b_lastT[:, t, :], bank[t][0:NB, KC * P:KC * P + P]).then_inc(sem("b_lastT"), 1)
            for g in range(GROUPS):
                v.wait_ge(*nth("b_x_bias", g + 1))
                v.wait_ge(*nth("b_out", g + 1))
                link(v, "v", nc.vector.tensor_tensor(gx(x, g), gx(x, g), group_bank(g, 3)[:, :].rearrange("p (j n) -> p j n", j=TPG), ALU.add))
            for g in range(GROUPS):
                dve_layer_norm(v, "c", g, x)
            for g in range(GROUPS):
                dve_normalise(v, "c", g, x)
            dve_self_attention(v, "c", False)
            for g in range(GROUPS):
                v.wait_ge(*nth("c_x_bias", g + 1))
                v.wait_ge(*nth("c_projected", g + 1))
                nc.vector.tensor_tensor(gx(x, g), gx(x, g), group_bank(g, 2)[:, :].rearrange("p (j n) -> p j n", j=TPG), ALU.add).then_inc(sem("c_x"), 1)
            v.wait_ge(*nth("c_x", GROUPS))
            for g in range(GROUPS):
                dve_layer_norm(v, "d", g, x, twice=True)
            for g in range(GROUPS):
                dve_normalise(v, "d", g, x, twice=True)
            dve_split_x(v, "d")
            v.wait_ge(sem("d_w_loaded"), 160)
            v.wait_ge(*nth("d_logits", 1))
            link(v, "v", nc.vector.tensor_tensor(logits[:, :, :], bank[7][:, 0:TILES * NE].rearrange("p (t e) -> p t e", t=TILES),
                                                 gate_row[:, :].unsqueeze(1).broadcast_to([P, TILES, NE]), ALU.add))
            dve_top2(v, "d")
            by_expert = w_token[:, :, :].rearrange("p e t -> p t e")
            nc.vector.tensor_tensor(by_expert, pick[:, 0, :, :], pick[:, 1, :, :], ALU.add).then_inc(sem("d_w_token"), 1)
            for g in range(GROUPS):
                v.wait_ge(sem("d_abel_p"), g + 1)
                nc.vector.tensor_tensor(gx(abel, g), bank[5 + g][:, :].rearrange("p (j n) -> p j n", j=TPG),
                                        abel_row[:, :].unsqueeze(1).broadcast_to([P, TPG, D]), ALU.add).then_inc(sem("d_abel_s"), 1)
            for g in range(GROUPS):
                v.wait_ge(sem("d_moe_b2"), g + 1)
                nc.vector.tensor_copy(gx(moe, g), bank[5 + g][:, :].rearrange("p (j n) -> p j n", j=TPG)).then_inc(sem("d_acc"), 1)
            v.wait_ge(sem("d_abel"), GROUPS)
            for t in range(TILES):
                i = nc.vector.tensor_tensor_reduce(out=mixed[:, t, :], in0=abel[:, t, :], in1=mix_row[:, 0:D], scale=1.0, scalar=0.0,
                                                   op0=ALU.mult, op1=ALU.add, accum_out=mix_z[:, 0, t:t + 1])
            link(v, "v", i)
            dve_accumulate(v, "d", 0)
            with v.Fori(1, NE // 2) as pair_of_experts:
                e = 2 * pair_of_experts
                v.wait_ge(sem("taylor_p"), pair_of_experts + (ORDER - 1))
                v.wait_ge(sem("taylorT_p"), pair_of_experts + 1)
                nc.vector.tensor_copy(taylor[:, :, :], bank[6][:, 0:3 * P].rearrange("p (i n) -> p i n", i=3)).then_inc(sem("taylor"), 1)
                dve_accumulate(v, "d", e - 1)
                dve_accumulate(v, "d", e)
            v.wait_ge(sem("taylor_p"), ORDER + SQUARINGS)
            nc.vector.tensor_copy(pair[:, :], bank[6][:, 0:P]).then_inc(sem("pair"), 1)
            dve_accumulate(v, "d", NE - 1)
            v.wait_ge(sem("taylor_p"), ORDER + SQUARINGS + 1)
            nc.vector.tensor_copy(rot[:, :], bank[6][:, 0:P]).then_inc(sem("rot"), 1)
            for g in range(GROUPS):
                v.wait_ge(sem("d_nonabel"), g + 1)
                for j in range(TPG):
                    t = g * TPG + j
                    nc_bank = group_bank(g, 2)[:, j * P:(j + 1) * P]
                    i = nc.vector.tensor_tensor_reduce(out=mixed[:, t, :], in0=nc_bank, in1=mix_row[:, D:2 * D], scale=1.0, scalar=0.0,
                                                       op0=ALU.mult, op1=ALU.add, accum_out=mix_z[:, 1, t:t + 1])
            link(v, "v", i)
            nc.vector.tensor_tensor(mix_z[:, 2, :], mix_z[:, 0, :], mix_z[:, 1, :], ALU.add).then_inc(sem("d_mix_z"), 1)
            for g in range(GROUPS):
                i = nc.vector.tensor_tensor(gx(mixed, g), group_bank(g, 2)[:, :].rearrange("p (j n) -> p j n", j=TPG), gx(abel, g), ALU.subtract)
            link(v, "v", i)
            v.wait_ge(sem("d_mix_g"), 1)
            for g in range(GROUPS):
                v.wait_ge(sem("d_x_abel"), g + 1)
                for t in range(g * TPG, (g + 1) * TPG):
                    i = nc.vector.scalar_tensor_tensor(x[:, t, :], mixed[:, t, :], mix_g[:, t:t + 1], x[:, t, :], ALU.mult, ALU.add)
                i.then_inc(sem("d_x"), 1)

            v.wait_ge(*nth("d_x", GROUPS))
            for g in range(GROUPS):
                v.wait_ge(*nth("d_x", g + 1))
                dve_layer_norm(v, "e", g, x)
            for g in range(GROUPS):
                dve_normalise(v, "e", g, x)

            def keys_out(t, slot, b):
                v.wait_ge(sem("e_prep"), BPT * t + (b + 1))
                v.wait_ge(sem("e_k_p"), BPT * t + (b + 1))
                nc.vector.scalar_tensor_tensor(e_k[:, b, :], bank[4][:, 0:NK], cols[:, BK1:BK1 + 1], e_keep[:, b, :], ALU.add, ALU.mult).then_inc(sem("e_k"), 1)
                nc.vector.tensor_scalar(e_add[:, b, :], e_keep[:, b, :], 1.0, 10000.0 * HD ** 0.5, ALU.subtract, ALU.mult).then_inc(sem("e_add"), 1)

            def last_values_out(t, slot, b):
                if b == 0:
                    v.wait_ge(sem("e_v_last_p"), t + 1)
                    nc.vector.tensor_tensor(e_v_last[:, slot, :].rearrange("p (g f) -> p g f", g=HG),
                                            bank[7][0:BPT * HG, 3 * P:4 * P].rearrange("p (g f) -> p g f", g=HG),
                                            e_group[:, :].unsqueeze(2).broadcast_to([BPT * HG, HG, NQ]), ALU.mult).then_inc(sem("e_v_last"), 1)

            def masked(t, slot, b):
                for g in range(HG):
                    n = b * HG + g
                    if g == 0:
                        wait_alone(v, "e_add", BPT * t + (b + 1))
                    wait_alone(v, "e_scores", HG * (BPT * t + b) + (g + 1))
                    i = nc.vector.tensor_tensor_reduce(out=e_probs[b][:, g, :], in0=bank[g][:, 0:NK], in1=e_add[:, b, :], scale=1.0,
                                                       scalar=-3e38, op0=ALU.add, op1=ALU.max, accum_out=e_max[:, n:n + 1])
                i.then_inc(sem("e_max"), 1)
                v.wait_ge(sem("e_max"), BPT * t + (b + 1))
                nc.vector.tensor_scalar(e_nmax[:, b * HG:(b + 1) * HG], e_max[:, b * HG:(b + 1) * HG], -HD ** -0.5, None, ALU.mult).then_inc(sem("e_masked"), 1)

            def dve_step(t, slot, b):
                later(masked, t, slot, b, 1)
                v.wait_ge(sem("e_exp"), BPT * t + (b + 1))
                nc.vector.reciprocal(e_inv[:, b * HG:(b + 1) * HG], e_sum[:, b * HG:(b + 1) * HG]).then_inc(sem("e_inv"), 1)
                v.wait_ge(sem("e_pT1"), BPT * t + (b + 1))
                nc.vector.tensor_copy(e_probsT[b % 2][:, 1, :, :], bank[6][:, :].rearrange("p (g n) -> p g n", g=HG)).then_inc(sem("e_pT_v"), 1)
                later(keys_out, t, slot, b, 2)
                v.wait_ge(sem("e_out"), BPT * t + (b + 1))
                if b == 2:
                    later(last_values_out, t, slot, b, 2)
                nc.vector.tensor_copy(e_scaled[:, 0, :, :], bank[7][:, P:2 * P].rearrange("p (h q) -> p h q", h=HPG)).then_inc(sem("e_scale"), 1)
                v.wait_ge(sem("e_scale"), BPT * t + (b + 1))
                nc.vector.tensor_tensor(e_scaled[:, 1, :, :], bank[7][:, 0:P].rearrange("p (h q) -> p h q", h=HPG), e_scaled[:, 0, :, :],
                                        ALU.mult).then_inc(sem("e_scaled"), 1)
                v.wait_ge(sem("e_scaled"), BPT * t + (b + 1))
                nc.vector.tensor_reduce(oT[:, bass.ds(t * P + b * NQ, NQ)], e_scaled[:, 1, :, :].rearrange("p h q -> p q h"),
                                        AX, ALU.add).then_inc(sem("e_done"), 1)

            keys_out(0, 0, 0)
            last_values_out(0, 0, 0)
            keys_out(0, 0, 1)
            masked(0, 0, 0)
            over_batches(v, dve_step)
            for g in range(GROUPS):
                v.wait_ge(*nth("e_x_bias", g + 1))
                v.wait_ge(*nth("e_projected", g + 1))
                nc.vector.tensor_tensor(gx(x, g), gx(x, g), group_bank(g, 0)[:, :].rearrange("p (j n) -> p j n", j=TPG), ALU.add).then_inc(sem("e_x"), 1)

            v.wait_ge(*nth("e_x", GROUPS))
            for g in range(GROUPS):
                dve_layer_norm(v, "f", g, x, twice=True)
            for g in range(GROUPS):
                dve_normalise(v, "f", g, x, twice=True)

            def negative_max(ph, kinds, tiles, scores_of, done):
                k0, k1 = kinds
                for t in tiles:
                    i = nc.vector.tensor_reduce(f_max[:, k0:k1, t:t + 1], scores_of(t), AX, ALU.max)
                link(v, "v", i)
                a, b = tiles[0], tiles[-1] + 1
                nc.vector.tensor_scalar(f_nmax[:, k0:k1, a:b], f_max[:, k0:k1, a:b], -D ** -0.5, None, ALU.mult).then_inc(sem(done), 1)

            for g in range(GROUPS):
                v.wait_ge(sem("f_scores3"), TPG * (g + 1))
                negative_max("f", (0, 3), range(g * TPG, (g + 1) * TPG),
                             lambda t: group_bank(t // TPG, t % TPG)[:, 0:3 * D].rearrange("p (k n) -> p k n", k=3), "f_max3")
            for g in range(GROUPS):
                v.wait_ge(sem("f_exp3"), g + 1)
                sl = slice(g * TPG, (g + 1) * TPG)
                link(v, "v", nc.vector.reciprocal(f_inv[:, 0:3, sl], f_sum[:, 0:3, sl]))
                for k in range(3):
                    i = nc.vector.tensor_tensor(patterns(g)[:, :, k, :], patterns(g)[:, :, k, :],
                                                f_inv[:, k, sl].unsqueeze(2).broadcast_to([P, TPG, D]), ALU.mult)
                i.then_inc(sem("f_patterns"), 1)
            dve_self_attention(v, "f", True)
            for g in range(GROUPS):
                v.wait_ge(sem("f_p_scores"), g + 1)
                sl = slice(g * TPG, (g + 1) * TPG)
                link(v, "v", nc.vector.tensor_reduce(f_max[:, 3, sl], group_bank(g, 2)[:, :].rearrange("p (j n) -> p j n", j=TPG), AX, ALU.max))
                nc.vector.tensor_scalar(f_nmax[:, 3, sl], f_max[:, 3, sl], -D ** -0.5, None, ALU.mult).then_inc(sem("f_p_max"), 1)
            for g in range(GROUPS):
                v.wait_ge(sem("f_p_exp"), g + 1)
                sl = slice(g * TPG, (g + 1) * TPG)
                link(v, "v", nc.vector.reciprocal(f_inv[:, 3, sl], f_sum[:, 3, sl]))
                v.wait_ge(sem("f_p_out"), g + 1)
                for j in range(TPG):
                    t = g * TPG + j
                    i = nc.vector.scalar_tensor_tensor(res[:, t, :], group_bank(g, 0)[:, j * P:(j + 1) * P], f_inv[:, 3, t:t + 1], res[:, t, :], ALU.mult, ALU.add)
                i.then_inc(sem("f_x2"), 1)
                v.wait_ge(sem("f_x2"), g + 1)
                dve_layer_norm(v, "f2", g, res)
            for g in range(GROUPS):
                dve_normalise(v, "f2", g, res)
            for t in range(TILES):
                v.wait_ge(sem("f_f_scores"), t + 1)
                link(v, "v", nc.vector.tensor_reduce(f_max[:, 4, t:t + 1], group_bank(t // TPG, t % TPG)[:, :], AX, ALU.max))
                nc.vector.tensor_scalar(f_nmax[:, 4, t:t + 1], f_max[:, 4, t:t + 1], -D ** -0.5, None, ALU.mult).then_inc(sem("f_f_max"), 1)
            for g in range(GROUPS):
                nc.vector.memset(gx(moe, g), 0.0).then_inc(sem("g_acc"), 1)
            nc.vector.memset(picked_before[:, 0, :], 0.0)
            for g in range(GROUPS):
                v.wait_ge(sem("f_f_exp"), TPG * (g + 1))
                sl = slice(g * TPG, (g + 1) * TPG)
                link(v, "v", nc.vector.reciprocal(f_inv[:, 4, sl], f_sum[:, 4, sl]))
                v.wait_ge(*nth("f_x_res", g + 1))
                v.wait_ge(sem("f_f_out"), g + 1)
                for j in range(TPG):
                    t = g * TPG + j
                    i = nc.vector.scalar_tensor_tensor(x[:, t, :], group_bank(g, 0)[:, j * P:(j + 1) * P], f_inv[:, 4, t:t + 1], x[:, t, :], ALU.mult, ALU.add)
                i.then_inc(sem("f_x"), 1)
                v.wait_ge(*nth("f_x", g + 1))
                dve_layer_norm(v, "g", g, x)

            for g in range(GROUPS):
                dve_normalise(v, "g", g, x)
            dve_split_x(v, "g")
            v.wait_ge(sem("g_w_loaded"), 32)
            v.wait_ge(*nth("g_logits", 1))
            link(v, "v", nc.vector.tensor_tensor(logits[:, :, :], bank[7][:, 0:TILES * NE].rearrange("p (t e) -> p t e", t=TILES),
                                                 router_row[:, :].unsqueeze(1).broadcast_to([P, TILES, NE]), ALU.add))
            dve_top2(v, "g")
            def gated_hidden(e, slot):
                for n in range(4):
                    c, g = n // GROUPS, n % GROUPS
                    v.wait_ge(sem("g_silu"), 4 * e + (n + 1))
                    nc.vector.tensor_tensor(hidden(slot)[:, c, g * GW:(g + 1) * GW], bank[2 * (n % 2)][:, :], silu_b(n), ALU.mult).then_inc(sem("g_hidden"), 1)

            gated_hidden(0, 0)
            v.wait_ge(sem("g_rank"), 1)
            nc.vector.tensor_scalar(kept[:, :, :], bank[6][:, 0:TILES * NE].rearrange("p (t e) -> p t e", t=TILES), float(CAPACITY), None, ALU.is_lt)
            link(v, "v", nc.vector.tensor_tensor(pick[:, 0, :, :], pick[:, 0, :, :], pick[:, 1, :, :], ALU.add))
            link(v, "v", nc.vector.tensor_tensor(by_expert, pick[:, 0, :, :], kept[:, :, :], ALU.mult))
            gated_hidden(1, 1)
            dve_accumulate(v, "g", 0)
            with v.Fori(1, NE // 2) as pair_of_experts:
                e = 2 * pair_of_experts
                gated_hidden(e, 0)
                dve_accumulate(v, "g", e - 1)
                gated_hidden(e + 1, 1)
                dve_accumulate(v, "g", e)
            dve_accumulate(v, "g", NE - 1)
            for g in range(GROUPS):
                v.wait_ge(*nth("g_acc", 2 * NE + (g + 1)))
                nc.vector.tensor_tensor(gx(x, g), gx(x, g), gx(moe, g), ALU.add).then_inc(sem("x_final"), 1)


_OUT = ((32, 32, 128), "float32")


def kernel(**inputs):
    import numpy as _np
    import concourse.bacc as _bacc
    from concourse import mybir as _mybir
    from concourse.bass_utils import run_bass_kernel_spmd as _run

    nc = _bacc.Bacc("TRN2", target_bir_lowering=False, num_devices=1)
    arrays, io = {}, {}
    for name, value in inputs.items():
        a = _np.ascontiguousarray(value)
        arrays[f"in_{name}"] = a
        io[name] = nc.dram_tensor(f"in_{name}", a.shape, _mybir.dt.from_np(a.dtype), kind="ExternalInput").ap()
    out = nc.dram_tensor("out_0", _OUT[0], _mybir.dt.from_np(_np.dtype(_OUT[1])), kind="ExternalOutput").ap()
    perceiver(nc, io, out)
    r = _run(nc, [arrays], core_ids=[0])
    return r.results[0]["out_0"]
```
